# Optimizing a Trainium2 kernel written in Bass

```python
import numpy as np
import jax
import jax.numpy as jnp

def _softmax(x, axis=-1):
    return jax.nn.softmax(x, axis=axis)

def _gelu(x):
    return jax.nn.gelu(x, approximate=True)

def _silu(x):
    return jax.nn.silu(x)

def _sigmoid(x):
    return jax.nn.sigmoid(x)

def _layernorm(x, axis=-1, eps=1e-05):
    m = jnp.mean(x, axis=axis, keepdims=True)
    v = jnp.var(x, axis=axis, keepdims=True)
    return (x - m) / jnp.sqrt(v + eps)

def _scatter_add(tgt, idx, src, axis=0):
    return tgt.at[idx].add(src)

def _segment_sum(src, seg, n):
    return jax.ops.segment_sum(src, seg, n)
kernel_name = 'mk_seq_postln_d1_jaxref_r4_0c6e3d'

def setup_inputs(seed: int=0):
    np.random.seed(seed)
    _w = jnp.asarray

    def _L0_attn_setup():
        import jax, jax.numpy as jnp
        import numpy as np
        import math
        DIM = 256
        HEADS = 16
        HEAD_DIM = DIM // HEADS
        B, N = (1, 1024)
        key = jax.random.key(seed)
        k1, k2, k3, k4 = jax.random.split(key, 4)
        content = jax.random.normal(k1, (B, N, DIM), dtype=jnp.float32)
        Wq = jnp.eye(DIM, dtype=jnp.float32) + 0.02 * jax.random.normal(k2, (DIM, DIM), dtype=jnp.float32)
        Wk = jnp.eye(DIM, dtype=jnp.float32) + 0.02 * jax.random.normal(k3, (DIM, DIM), dtype=jnp.float32)
        Wv = jnp.eye(DIM, dtype=jnp.float32) + 0.02 * jax.random.normal(k4, (DIM, DIM), dtype=jnp.float32)
        return {'content': content, 'Wq': Wq, 'Wk': Wk, 'Wv': Wv}
    _L0_attn_in = _L0_attn_setup()

    def _L0_ffn_setup():
        import jax, jax.numpy as jnp
        import numpy as np
        import math
        DMODEL = 256
        DFF = 1024
        NUM_EXPERTS = 8
        TOPK = 2
        CAP_FACTOR = 1.25
        EPS = 1.1920929e-07

        def _trunc_normal(key, shape, fan_in, scale=1.0):
            std = scale * (1.0 / fan_in) ** 0.5
            return jax.random.truncated_normal(key, -2.0, 2.0, shape, jnp.float32) * std
        key = jax.random.key(seed)
        ks = jax.random.split(key, 5)
        return {'x': jax.random.normal(ks[0], (2, 512, DMODEL), jnp.float32), 'router_weight': _trunc_normal(ks[1], (NUM_EXPERTS, DMODEL), DMODEL), 'ff_pre_act_weight': _trunc_normal(ks[2], (NUM_EXPERTS, DFF, DMODEL), DMODEL), 'gate_weight': _trunc_normal(ks[3], (NUM_EXPERTS, DFF, DMODEL), DMODEL), 'ff_post_act_weight': _trunc_normal(ks[4], (NUM_EXPERTS, DMODEL, DFF), DFF)}
    _L0_ffn_in = _L0_ffn_setup()
    _d = {'L0_attn_content': _L0_attn_in['content'], 'L0_attn_Wq': _L0_attn_in['Wq'], 'L0_attn_Wk': _L0_attn_in['Wk'], 'L0_attn_Wv': _L0_attn_in['Wv'], 'L0_ffn_router_weight': _L0_ffn_in['router_weight'], 'L0_ffn_ff_pre_act_weight': _L0_ffn_in['ff_pre_act_weight'], 'L0_ffn_gate_weight': _L0_ffn_in['gate_weight'], 'L0_ffn_ff_post_act_weight': _L0_ffn_in['ff_post_act_weight']}
    _x0 = _d['L0_attn_content']
    _d['L0_attn_content'] = jax.random.normal(jax.random.fold_in(jax.random.key(seed), 1), (2, 2048, 256), dtype=_x0.dtype)
    del _x0
    return _d

def reference(L0_attn_content, L0_attn_Wq, L0_attn_Wk, L0_attn_Wv, L0_ffn_router_weight, L0_ffn_ff_pre_act_weight, L0_ffn_gate_weight, L0_ffn_ff_post_act_weight):

    def _L0_attn_ref(content, Wq, Wk, Wv):
        import jax, jax.numpy as jnp
        import numpy as np
        import math
        DIM = 256
        HEADS = 16
        HEAD_DIM = DIM // HEADS
        B, N = (1, 1024)
        b, n, d = content.shape
        Q = (content @ Wq).reshape(b, n, HEADS, HEAD_DIM)
        K = (content @ Wk).reshape(b, n, HEADS, HEAD_DIM)
        V = (content @ Wv).reshape(b, n, HEADS, HEAD_DIM)
        scores = jnp.einsum('bqhd,bkhd->bhqk', Q, K) / math.sqrt(HEAD_DIM)
        alpha = jax.nn.softmax(scores, axis=-1)
        causal = jnp.tril(jnp.ones((n, n), dtype=bool))
        alpha = jnp.where(causal, alpha, jnp.zeros((), dtype=alpha.dtype))
        Y = jnp.einsum('bhqk,bkhd->bqhd', alpha, V).reshape(b, n, d)
        return Y

    def _L0_ffn_ref(x, router_weight, ff_pre_act_weight, gate_weight, ff_post_act_weight):
        import jax, jax.numpy as jnp
        import numpy as np
        import math
        DMODEL = 256
        DFF = 1024
        NUM_EXPERTS = 8
        TOPK = 2
        CAP_FACTOR = 1.25
        EPS = 1.1920929e-07

        def _trunc_normal(key, shape, fan_in, scale=1.0):
            std = scale * (1.0 / fan_in) ** 0.5
            return jax.random.truncated_normal(key, -2.0, 2.0, shape, jnp.float32) * std
        orig_shape = x.shape
        h = x.reshape(-1, DMODEL)
        T = h.shape[0]
        logits = jnp.einsum('th,eh->te', h, router_weight)
        probs = jax.nn.softmax(logits.astype(jnp.float32), axis=-1)
        topk_probs, selected = jax.lax.top_k(probs, TOPK)
        topk_probs = topk_probs / jnp.maximum(topk_probs.sum(-1, keepdims=True), EPS)
        flat_tokens = jnp.repeat(jnp.arange(T), TOPK)
        flat_experts = selected.reshape(-1)
        flat_weights = topk_probs.reshape(-1)
        A = T * TOPK
        capacity = max(1, math.ceil(CAP_FACTOR * A / NUM_EXPERTS))
        weight_order = jnp.argsort(-flat_weights, stable=True)
        grouped_order = jnp.argsort(flat_experts[weight_order], stable=True)
        sort_order = weight_order[grouped_order]
        se = flat_experts[sort_order]
        st = flat_tokens[sort_order]
        sw = flat_weights[sort_order]
        counts = jnp.bincount(se, length=NUM_EXPERTS)
        offsets = jnp.cumsum(counts) - counts
        slot = jnp.arange(A) - offsets[se]
        keep = slot < capacity
        sw = jnp.where(keep, sw, 0.0)
        token_wsum = jnp.zeros(T, jnp.float32).at[st].add(sw)
        kept_w = sw / jnp.maximum(token_wsum[st], EPS)
        FC = NUM_EXPERTS * capacity
        dispatch = jnp.where(keep, se * capacity + slot, FC)
        expert_inputs = jnp.zeros((FC + 1, DMODEL), x.dtype).at[dispatch].set(h[st])
        expert_inputs = expert_inputs[:FC].reshape(NUM_EXPERTS, capacity, DMODEL)
        pre = jnp.einsum('ech,edh->ecd', expert_inputs, ff_pre_act_weight)
        gate = jnp.einsum('ech,edh->ecd', expert_inputs, gate_weight)
        expert_out = jnp.einsum('ecd,ehd->ech', pre * jax.nn.silu(gate), ff_post_act_weight)
        eo_flat = jnp.concatenate([expert_out.reshape(FC, DMODEL), jnp.zeros((1, DMODEL), x.dtype)], axis=0)
        updates = eo_flat[dispatch] * kept_w.astype(x.dtype)[:, None]
        out = jnp.zeros((T, DMODEL), x.dtype).at[st].add(updates)
        return out.reshape(orig_shape)
    x = L0_attn_content
    x = _layernorm(x + _L0_attn_ref(x, L0_attn_Wq, L0_attn_Wk, L0_attn_Wv), axis=-1)
    x = _layernorm(x + _L0_ffn_ref(x, L0_ffn_router_weight, L0_ffn_ff_pre_act_weight, L0_ffn_gate_weight, L0_ffn_ff_post_act_weight), axis=-1)
    return x

_drawn_inputs = setup_inputs


def setup_inputs(seed=0):
    import zlib

    import numpy as np

    out = dict(_drawn_inputs(seed))
    spreads = {}
    factors = {}
    for name, (base, spread) in spreads.items():
        noise = np.random.default_rng([zlib.crc32(name.encode()), seed]).standard_normal(out[name].shape)
        drawn = base * np.exp(spread * noise) if base else spread * noise
        out[name] = jnp.asarray(drawn.astype(out[name].dtype))
    for name, factor in factors.items():
        out[name] = (out[name] * factor).astype(out[name].dtype)
    return out
```

```python
import concourse.bass as bass
from concourse import mybir
from contextlib import ExitStack

FP32 = mybir.dt.float32
BF16 = mybir.dt.bfloat16
I32 = mybir.dt.int32
U32 = mybir.dt.uint32
ALU = mybir.AluOpType
ACT = mybir.ActivationFunctionType
AX = mybir.AxisListType

P = 128
B, N, D = 2, 2048, 256
H, HD = 16, 16
T = B * N
NH = B * H
DC = D // P
TT = T // P
NT = N // P
BLK = 512
E, TOPK, F = 8, 2, 1024
FC = F // P
CAP = 1280
CT = CAP // P
ROW = 264
COL_W, COL_E, COL_ID = 256, 258, 260
LN_EPS = 1e-5
MOE_EPS = 1.1920929e-07
TAU_BITS = 30
BOUND_MAX = 30.0

KSPAN = 3 * BLK
NG = N // BLK
D_AT = (0, 512, 1024, 896)


def key_tiles():
    diag = [[(g, 4 * g + r, D_AT[r], BLK - P * r) for r in range(4)] for g in range(NG)]
    full = [(g, j) for g in range(NG) for j in range(4 * g)]
    off = [[(g, j, BLK * n, BLK) for n, (g, j) in enumerate(full[3 * f:3 * f + 3])] for f in range(8)]
    return [diag[0], off[0], off[1], diag[1], off[2], off[3], diag[2], off[4], off[5], diag[3], off[6], off[7]]


def query_tiles():
    pieces = []
    for i in range(NT - 1):
        lo, left = P * (i + 1), N - P * (i + 1)
        if left > KSPAN:
            pieces.append((i, lo, KSPAN, i))
            pieces.append((i, lo + KSPAN, left - KSPAN, NT + i))
        else:
            pieces.append((i, lo, left, i))
    tiles = []
    for i, lo, w, col in sorted(pieces, key=lambda x: -x[2]):
        for t in tiles:
            if sum(x[3] for x in t) + w <= KSPAN:
                t.append((i, sum(x[3] for x in t), lo, w, col))
                break
        else:
            tiles.append([(i, 0, lo, w, col)])
    return tiles


KT = key_tiles()
QT = query_tiles()
NK, NQ = len(KT), len(QT)
ORDER = "KQKQKQKQKKQKQKKQKQKKQQ"
assert ORDER.count("K") == NK and ORDER.count("Q") == NQ
SEQ = []
for c in ORDER:
    SEQ.append((c, sum(1 for k, _ in SEQ if k == c)))
NS = len(SEQ)
K_POS = [n for n, (k, _) in enumerate(SEQ) if k == "K"]
DIAG = [0, 3, 6, 9]
LAST = [max(m for m in range(NK) if any(u[0] == g for u in KT[m])) for g in range(NG)]
LAG = 3
S_RING, P_RING, O_RING = 2, 4, 2
TURN_AT = {5: 0, 11: 1, 16: 2}


def chain(eng, semaphore):
    count = [0]

    def link(instruction):
        count[0] += 1
        instruction.then_inc(semaphore, 1)
        eng.wait_ge(semaphore, count[0])

    def skip(n):
        count[0] += n

    link.count, link.skip = lambda: count[0], skip
    return link


def layer_stats(nc, link, stats, mean, var, tmp):
    link(nc.vector.tensor_tensor(mean, stats[:, :, 1], stats[:, :, 4], ALU.add))
    link(nc.vector.tensor_scalar(mean, mean, 0.5, None, ALU.mult))
    link(nc.vector.tensor_tensor(tmp, stats[:, :, 1], mean, ALU.subtract))
    link(nc.vector.tensor_tensor(tmp, tmp, tmp, ALU.mult))
    link(nc.vector.tensor_tensor(var, stats[:, :, 2], stats[:, :, 5], ALU.add))
    link(nc.vector.tensor_scalar(var, var, 1.0 / D, LN_EPS, ALU.mult, ALU.add))
    return nc.vector.tensor_tensor(var, var, tmp, ALU.add)


def inverse_root(nc, link, var, std, rstd, tmp):
    link(nc.vector.reciprocal(rstd, std))
    link(nc.vector.tensor_tensor(tmp, rstd, rstd, ALU.mult))
    link(nc.vector.tensor_tensor(tmp, tmp, var, ALU.mult))
    link(nc.vector.tensor_scalar(tmp, tmp, -0.5, 1.5, ALU.mult, ALU.add))
    link(nc.vector.tensor_tensor(rstd, rstd, tmp, ALU.mult))


def program(nc, x_tok, x_T, wq, wk, wv, wr_T, w1_T, wg_T, w2_T, out):
    ctx = ExitStack()
    with ctx:
        def sem(name):
            return ctx.enter_context(nc.semaphore(name))

        def sb(stack, name, shape, dt=FP32):
            return stack.enter_context(nc.sbuf_tensor(name, shape, dt))

        def ps(stack, name, shape, dt=FP32):
            return stack.enter_context(nc.psum_tensor(name, shape, dt))

        split_dram = nc.dram_tensor("split_dram", (2, 3, NH * HD, N), BF16).ap()
        shift_dram = nc.dram_tensor("shift_dram", (2, NH, N), BF16).ap()
        xe_dram = nc.dram_tensor("xe_dram", (E * CAP, ROW), FP32).ap()
        acc_dram = nc.dram_tensor("acc_dram", (T, D), FP32).ap()

        ident = sb(ctx, "ident", [P, P])
        ones = sb(ctx, "ones", [P, P])
        before = sb(ctx, "before", [P, P])
        upto = sb(ctx, "upto", [P, 4, P])
        after = sb(ctx, "after", [P, 4, P])
        one_head = sb(ctx, "one_head", [P, DC, H], BF16)
        flag = sb(ctx, "flag", [1, 4], I32)
        consts_ready = sem("consts_ready")

        att = ctx.enter_context(ExitStack())
        v_all = sb(att, "v_all", [P, NH, NT, HD])

        NB = T // BLK
        U = 2 * DC
        xT_loaded = [sem(f"xT_loaded{j}") for j in range(2)]
        w_loaded = sem("w_loaded")
        proj_ready, hi_ready, proj_split = sem("proj_ready"), sem("hi_ready"), sem("proj_split")
        sq_ready, norm_ready, norm_read = sem("sq_ready"), sem("norm_ready"), sem("norm_read")
        v_ready, v_read = sem("v_ready"), sem("v_read")
        dve1, parts_stored, shift_ready, shift_stored = sem("dve1"), sem("parts_stored"), sem("shift_ready"), sem("shift_stored")
        top_ready, top_row, flag_ready = sem("top_ready"), sem("top_row"), sem("flag_ready")
        blank_ready, xe_cleared = sem("blank_ready"), sem("xe_cleared")

        with ExitStack() as st, nc.Block() as block:
            xT = sb(st, "xT", [P, 2, DC, BLK])
            w_qk = sb(st, "w_qk", [P, 2, DC, D])
            w_v = sb(st, "w_v", [P, DC, D])
            parts = sb(st, "parts", [P, 3, U, T], BF16)
            rest = sb(st, "rest", [P, BLK])
            sq = sb(st, "sq", [P, U, BLK], BF16)
            qn = sb(st, "qn", [H, N])
            kn = sb(st, "kn", [H, NB // B])
            kmax = sb(st, "kmax", [H, 1])
            shift = sb(st, "shift", [H, 2, T], BF16)
            bound = sb(st, "bound", [H, N])
            topb = sb(st, "topb", [H, B])
            top = sb(st, "top", [H, 1])
            topr = sb(st, "topr", [1, 1])
            blank = sb(st, "blank", [P, ROW])
            proj = ps(st, "proj", [P, U, BLK])
            norm = ps(st, "norm", [P, 2, BLK])
            vps = ps(st, "vps", [P, 2, 2, D])

            @block.gpsimd
            def _(pool):
                pool.memset(ident[:], 0.0).then_inc(consts_ready, 1)
                pool.memset(ones[:], 1.0).then_inc(consts_ready, 1)
                pool.memset(one_head[:], 1.0).then_inc(consts_ready, 1)
                pool.memset(upto[:], 1.0).then_inc(consts_ready, 1)
                pool.memset(after[:], 1.0).then_inc(consts_ready, 1)
                pool.memset(blank[:], 0.0).then_inc(consts_ready, 1)
                pool.wait_ge(consts_ready, 6)
                pool.memset(blank[:, COL_ID:COL_ID + 1], float(T)).then_inc(blank_ready, 1)
                pool.affine_select(out=ident[:], in_=ident[:], compare_op=ALU.not_equal, fill=1.0, base=0,
                                   pattern=[[-1, P]], channel_multiplier=1).then_inc(consts_ready, 1)
                pool.affine_select(out=before[:], in_=ones[:], compare_op=ALU.is_gt, fill=0.0, base=0,
                                   pattern=[[1, P]], channel_multiplier=-1).then_inc(consts_ready, 1)
                pool.affine_select(out=upto[:], in_=upto[:], compare_op=ALU.is_ge, fill=0.0, base=0,
                                   pattern=[[0, 4], [1, P]], channel_multiplier=-1).then_inc(consts_ready, 1)
                pool.affine_select(out=after[:], in_=after[:], compare_op=ALU.is_gt, fill=0.0, base=0,
                                   pattern=[[0, 4], [-1, P]], channel_multiplier=1).then_inc(consts_ready, 1)
                pool.affine_select(out=one_head[:], in_=one_head[:], compare_op=ALU.is_ge, fill=0.0, base=0,
                                   pattern=[[P, DC], [-HD, H]], channel_multiplier=1).then_inc(consts_ready, 1)
                pool.wait_ge(consts_ready, 11)
                pool.affine_select(out=one_head[:], in_=one_head[:], compare_op=ALU.is_ge, fill=0.0, base=HD - 1,
                                   pattern=[[-P, DC], [HD, H]], channel_multiplier=-1).then_inc(consts_ready, 1)

            @block.sync
            def _(sp):
                for i, w in enumerate((wq, wk)):
                    sp.dma_start(w_qk[:, i], w.rearrange("(c p) n -> p c n", p=P)).then_inc(w_loaded, 16)
                sp.dma_start(w_v[:], wv.rearrange("(c p) n -> p c n", p=P)).then_inc(w_loaded, 16)
                xT_view = x_T.rearrange("(c p) t -> p c t", p=P)
                for j in range(2):
                    sp.dma_start(xT[:, j], xT_view[:, :, j * BLK:(j + 1) * BLK]).then_inc(xT_loaded[j], 16)
                with sp.Fori(1, NB // 2) as i:
                    for j in range(2):
                        sp.wait_ge(v_ready, i * 8 + (4 * j - 4))
                        sp.dma_start(xT[:, j], xT_view[:, :, bass.ds(i * (2 * BLK) + j * BLK, BLK)]).then_inc(xT_loaded[j], 16)
                for b in range(B):
                    sp.wait_ge(proj_split, U + U * (NB // B) * (b + 1))
                    for i in range(2):
                        for s in range(3):
                            sp.dma_start(split_dram[i, s, b * D:(b + 1) * D, :].rearrange("(c p) t -> p c t", p=P),
                                         parts[:, s, DC * i:DC * (i + 1), b * N:(b + 1) * N]).then_inc(parts_stored, 16)
                    sp.wait_ge(shift_ready, b + 1)
                    sp.dma_start(shift_dram[:, b * H:(b + 1) * H, :].rearrange("s h t -> h s t"),
                                 shift[:, :, b * N:(b + 1) * N]).then_inc(shift_stored, 16)
                sp.wait_ge(blank_ready, 1)
                sp.wait_ge(consts_ready, 12)
                sp.dma_start(xe_dram.rearrange("(p s) c -> p s c", p=P),
                             blank[:, None, :].to_broadcast([P, E * CAP // P, ROW])).then_inc(xe_cleared, 16)
                sp.wait_ge(parts_stored, 16 * 6 * B)
                sp.wait_ge(shift_stored, 16 * B)
                sp.wait_ge(xe_cleared, 16)

            @block.tensor
            def _(pe):
                pe.sem_inc(norm_ready, 1)
                pe.wait_ge(w_loaded, 48)
                pe.wait_ge(consts_ready, 12)
                with pe.Fori(0, NB // 2) as i:
                    for j in range(2):
                        pe.wait_ge(xT_loaded[j], i * 16 + 16)
                        for u in range(U):
                            pe.wait_ge(proj_split, i * (2 * U) + (j * U + u + 1))
                            for c in range(DC):
                                last = nc.tensor.matmul(proj[:, u, :], w_qk[:, u // DC, c, (u % DC) * P:(u % DC + 1) * P],
                                                        xT[:, j, c, :], start=(c == 0), stop=(c == DC - 1))
                            last.then_inc(proj_ready, 1)
                        for t in range(4):
                            pe.wait_ge(v_read, i * 8 + (4 * j + 2 * (t // 2) + 2))
                            for c in range(DC):
                                last = nc.tensor.matmul(vps[:, t // 2, t % 2, :], xT[:, j, c, t * P:(t + 1) * P],
                                                        w_v[:, c, :], start=(c == 0), stop=(c == DC - 1))
                            last.then_inc(v_ready, 1)
                        pe.wait_ge(sq_ready, i * (2 * U) + (j + 1) * U)
                        pe.wait_ge(norm_read, i * 4 + (2 * j + 2))
                        for u in range(U):
                            last = nc.tensor.matmul(norm[0:H, u // DC, :], one_head[:, u % DC, :], sq[:, u, :],
                                                    start=(u % DC == 0), stop=(u % DC == DC - 1))
                        last.then_inc(norm_ready, 1)
                pe.wait_ge(top_ready, 1)
                nc.tensor.matmul(proj[0:1, 0, 0:H], top[:], ident[0:H, 0:H], start=True, stop=True).then_inc(top_row, 1)

            @block.scalar
            def _(act):
                act.sem_inc(v_read, 4)
                v_by_tile = v_all[:].rearrange("p (b h) t d -> p b h t d", b=B)
                with act.Fori(0, B) as b:
                    with act.Fori(0, NB // 2 // B) as i:
                        for j in range(2):
                            act.wait_ge(norm_ready, b * (NB // B) + i * 2 + (j + 1))
                            for u in range(U):
                                act.wait_ge(proj_ready, b * (U * NB // B) + i * (2 * U) + (j * U + u + 1))
                                nc.scalar.activation(sq[:, u, :], proj[:, u, :], ACT.Square).then_inc(sq_ready, 1)
                                nc.scalar.activation(parts[:, 0, u, bass.ds(b * N + i * (2 * BLK) + j * BLK, BLK)],
                                                     proj[:, u, :], ACT.Copy).then_inc(hi_ready, 1)
                            for t in range(4):
                                act.wait_ge(v_ready, b * (4 * NB // B) + i * 8 + (4 * j + 2 * (t // 2) + 2))
                                nc.scalar.activation(v_by_tile[:, bass.ds(b, 1), :, bass.ds(i * 8 + (4 * j + t), 1), :],
                                                     vps[:, t // 2, t % 2, :].rearrange("p (x h y d) -> p x h y d", x=1, y=1, h=H),
                                                     ACT.Copy).then_inc(v_read, 1)

            @block.vector
            def _(dve):
                dve.sem_inc(proj_split, U)
                dve.sem_inc(norm_read, 2)
                links_b = 2 * U * (NB // B) + 4
                with dve.Fori(0, B) as b:
                    with dve.Fori(0, NB // 2 // B) as i:
                        for j in range(2):
                            for u in range(U):
                                hi, mid, lo = (parts[:, s, u, bass.ds(b * N + i * (2 * BLK) + j * BLK, BLK)] for s in range(3))
                                step = b * links_b + i * (4 * U) + (2 * (j * U + u))
                                dve.wait_ge(hi_ready, b * (U * NB // B) + i * (2 * U) + (j * U + u + 1))
                                dve.wait_ge(proj_split, b * (U * NB // B) + i * (2 * U) + (j * U + u + U))
                                nc.vector.tensor_tensor(rest[:], proj[:, u, :], hi, ALU.subtract).then_inc(dve1, 1)
                                dve.wait_ge(dve1, step + 1)
                                nc.vector.tensor_copy(mid, rest[:]).then_inc(dve1, 1)
                                dve.wait_ge(dve1, step + 2)
                                nc.vector.tensor_tensor(lo, rest[:], mid, ALU.subtract).then_inc(proj_split, 1)
                            dve.wait_ge(norm_ready, b * (NB // B) + i * 2 + (j + 2))
                            nc.vector.tensor_copy(qn[:, bass.ds(i * (2 * BLK) + j * BLK, BLK)], norm[0:H, 0, :]).then_inc(norm_read, 1)
                            nc.vector.tensor_reduce(kn[:, bass.ds(i * 2 + j, 1)], norm[0:H, 1, :], AX.X, ALU.max).then_inc(norm_read, 1)
                    dve.wait_ge(norm_read, b * (2 * NB // B) + (2 * NB // B + 2))
                    nc.vector.tensor_reduce(kmax[:], kn[:], AX.X, ALU.max).then_inc(dve1, 1)
                    dve.wait_ge(dve1, b * links_b + (links_b - 3))
                    nc.vector.tensor_scalar(bound[:], qn[:], kmax[:], 0.125, ALU.add, ALU.mult).then_inc(dve1, 1)
                    dve.wait_ge(dve1, b * links_b + (links_b - 2))
                    nc.vector.tensor_copy(shift[:, 0, bass.ds(b * N, N)], bound[:]).then_inc(dve1, 1)
                    dve.wait_ge(dve1, b * links_b + (links_b - 1))
                    nc.vector.tensor_tensor(shift[:, 1, bass.ds(b * N, N)], bound[:], shift[:, 0, bass.ds(b * N, N)],
                                            ALU.subtract).then_inc(shift_ready, 1)
                    nc.vector.tensor_reduce(topb[:, bass.ds(b, 1)], bound[:], AX.X, ALU.max).then_inc(dve1, 1)
                    dve.wait_ge(dve1, b * links_b + links_b)
                nc.vector.tensor_reduce(top[:], topb[:], AX.X, ALU.max).then_inc(top_ready, 1)
                dve.wait_ge(top_row, 1)
                nc.vector.tensor_reduce(topr[:], proj[0:1, 0, 0:H], AX.X, ALU.max).then_inc(dve1, 1)
                dve.wait_ge(dve1, B * links_b + 1)
                nc.vector.tensor_scalar(flag[0:1, 0:1], topr[:], BOUND_MAX, None, ALU.is_gt).then_inc(flag_ready, 1)

        attn = sb(att, "attn", [P, NH, NT, HD])
        aq = [sb(att, f"aq{j}", [P, N], BF16) for j in range(2)]
        ak = [sb(att, f"ak{j}", [P, N], BF16) for j in range(2)]
        KR = 6 * HD
        AQ = ((0, 3), (1, 2), (2, 1))
        AK = ((0, 3), (3, 2), (5, 1))
        KS = KR + 2
        A_DMAS = 6 + 3

        def load_operands(sp, j, n, done):
            for s, (part, times) in enumerate(AQ):
                for r in range(times):
                    at = (0, 3, 5)[s] + r
                    sp.dma_start(aq[j][at * HD:(at + 1) * HD, :], split_dram[0, part, bass.ds(n * HD, HD), :]).then_inc(done, 16)
            for at, k in AK:
                sp.dma_start(ak[j][at * HD:(at + k) * HD, :], split_dram[1, 0:k, bass.ds(n * HD, HD), :]).then_inc(done, 16)

        g_loaded, g_link, g_scores, g_read = sem("g_loaded"), sem("g_link"), sem("g_scores"), sem("g_read")
        g_max, g_row, g_row_sb, g_stored, g_over = sem("g_max"), sem("g_row"), sem("g_row_sb"), sem("g_stored"), sem("g_over")
        with ExitStack() as st, nc.Block() as block:
            s_all = ps(st, "s_all", [P, N])
            m_ps = ps(st, "m_ps", [P, BLK])
            m_sb = sb(st, "m_sb", [P, NT])
            m_32 = sb(st, "m_32", [NT, P])
            m_row = sb(st, "m_row", [NT, 2, P], BF16)

            @block.sync
            def _(sp):
                sp.wait_ge(flag_ready, 1)
                loose = sp.value_load(flag[0:1, 0:1], min_val=0, max_val=1)
                with sp.If(loose > 0):
                    with sp.Fori(0, NH) as n:
                        load_operands(sp, 0, n, g_loaded)
                        sp.wait_ge(g_row_sb, n * 1 + 1)
                        for s in range(2):
                            sp.dma_start(shift_dram[s, bass.ds(n, 1), :].rearrange("o (t q) -> (o t) q", q=P),
                                         m_row[:, s, :]).then_inc(g_stored, 16)
                        sp.wait_ge(g_stored, n * 32 + 32)
                        sp.sem_inc(g_over, 1)

            @block.tensor
            def _(pe):
                pe.wait_ge(flag_ready, 1)
                loose = pe.value_load(flag[0:1, 0:1], min_val=0, max_val=1)
                with pe.If(loose > 0):
                    with pe.Fori(0, NH) as n:
                        pe.wait_ge(g_loaded, n * (16 * A_DMAS) + 16 * A_DMAS)
                        for i in range(NT):
                            pe.wait_ge(g_read, n * NT + i + 1)
                            for k in range(NG):
                                last = nc.tensor.matmul(s_all[:, k * BLK:(k + 1) * BLK], aq[0][0:KR, i * P:(i + 1) * P],
                                                        ak[0][0:KR, k * BLK:(k + 1) * BLK], start=True, stop=True)
                            last.then_inc(g_scores, 1)
                        pe.wait_ge(g_read, n * NT + NT + 1)
                        nc.tensor.matmul(m_ps[0:NT, 0:P], m_sb[:], ident[:], start=True, stop=True).then_inc(g_row, 1)

            @block.vector
            def _(dve):
                dve.wait_ge(flag_ready, 1)
                loose = dve.value_load(flag[0:1, 0:1], min_val=0, max_val=1)
                with dve.If(loose > 0):
                    dve.sem_inc(g_read, 1)
                    with dve.Fori(0, NH) as n:
                        for i in range(NT):
                            dve.wait_ge(g_scores, n * NT + i + 1)
                            nc.vector.tensor_reduce(m_sb[:, i:i + 1], s_all[:], AX.X, ALU.max).then_inc(g_read, 1)
                        dve.wait_ge(g_row, n * 1 + 1)
                        nc.vector.tensor_scalar(m_32[:], m_ps[0:NT, 0:P], 0.25, None, ALU.mult).then_inc(g_link, 1)
                        dve.wait_ge(g_link, n * 2 + 1)
                        nc.vector.tensor_copy(m_row[:, 0, :], m_32[:]).then_inc(g_link, 1)
                        dve.wait_ge(g_link, n * 2 + 2)
                        nc.vector.tensor_tensor(m_row[:, 1, :], m_32[:], m_row[:, 0, :], ALU.subtract).then_inc(g_row_sb, 1)

        a_loaded = [sem(f"a_loaded{j}") for j in range(2)]
        vh_ready, minus_ready, fills_ready = sem("vh_ready"), sem("minus_ready"), sem("fills_ready")
        scores_ready, exp_done, pv_done = sem("scores_ready"), sem("exp_done"), sem("pv_done")
        mask_done, out_copied, out_turned, out_read = sem("mask_done"), sem("out_copied"), sem("out_turned"), sem("out_read")
        head_done, dve3 = sem("head_done"), sem("dve3")
        x_loaded = sem("x_loaded")
        x_sb = sb(att, "x_sb", [P, TT, D])
        with ExitStack() as st, nc.Block() as block:
            probs = sb(st, "probs", [P, P_RING, KSPAN])
            vh = [sb(st, f"vh{j}", [P, NT, 32]) for j in range(2)]
            only_sum = sb(st, "only_sum", [P, 32])
            zeros = sb(st, "zeros", [P, 32])
            hidden = sb(st, "hidden", [P, 4, P])
            o_sb = sb(st, "o_sb", [P, O_RING, BLK])
            num = sb(st, "num", [P, NT, HD + 1])
            sums = sb(st, "sums", [P, 2, NT + 3])
            den = sb(st, "den", [P, NT])
            inv = sb(st, "inv", [P, NT])
            scores = [ps(st, f"scores{j}", [P, KSPAN]) for j in range(S_RING)]
            o_ps = [ps(st, f"o_ps{j}", [P, BLK]) for j in range(O_RING)]
            pairs = NH // 2

            @block.sync
            def _(sp):
                def load_head(j, n):
                    load_operands(sp, j, n, a_loaded[j])
                    sp.dma_start(aq[j][KR:KS, :], shift_dram[:, bass.ds(n, 1), :].rearrange("s o t -> (s o) t")).then_inc(a_loaded[j], 16)

                for j in range(2):
                    load_head(j, j)
                sp.dma_start(x_sb[:], x_tok.rearrange("(t p) d -> p t d", p=P)).then_inc(x_loaded, 16)
                with sp.Fori(1, pairs) as i:
                    for j in range(2):
                        sp.wait_ge(scores_ready, i * (2 * NS) + (j - 1) * NS)
                        load_head(j, i * 2 + j)
                sp.wait_ge(x_loaded, 16)

            @block.gpsimd
            def _(pool):
                for j in range(2):
                    pool.memset(vh[j][:], 0.0).then_inc(fills_ready, 1)
                    pool.memset(sums[:, j, :], 0.0).then_inc(fills_ready, 1)
                pool.memset(only_sum[:], 0.0).then_inc(fills_ready, 1)
                pool.memset(zeros[:], 0.0).then_inc(fills_ready, 1)
                pool.wait_ge(fills_ready, 6)
                pool.memset(only_sum[:, HD:HD + 1], 1.0).then_inc(fills_ready, 1)
                for j in range(2):
                    pool.memset(vh[j][:, :, HD:HD + 1], 1.0).then_inc(fills_ready, 1)
                pool.wait_ge(fills_ready, 9)
                with pool.Fori(0, pairs) as i:
                    for j in range(2):
                        pool.wait_ge(pv_done, i * (2 * NK) + (j * NK + NK + P_RING))
                        nc.gpsimd.tensor_copy(vh[j][:, :, 0:HD], v_all[:, bass.ds(i * 2 + j, 1), :, :].rearrange("p o t d -> p (o t) d")).then_inc(vh_ready, 1)

            @block.tensor
            def _(pe):
                pe.wait_ge(fills_ready, 9)
                pe.wait_ge(minus_ready, 2)
                pe.sem_inc(pv_done, P_RING + 2 * NK)

                def fill(i, j, t):
                    kind, m = SEQ[t]
                    pe.wait_ge(exp_done, i * (2 * NS) + (j * NS + t + 1))
                    dst = scores[t % S_RING]
                    pieces = []
                    if kind == "K":
                        for g, k, at, w in KT[m]:
                            pieces.append((at, ak[j][0:KS, k * P:(k + 1) * P], aq[j], (g + 1) * BLK - w, w))
                    else:
                        for q, at, lo, w, _ in QT[m]:
                            while w:
                                step = min(w, BLK - at % BLK)
                                pieces.append((at, aq[j][0:KS, q * P:(q + 1) * P], ak[j], lo, step))
                                at, lo, w = at + step, lo + step, w - step
                    for at, still, moving, lo, w in pieces:
                        last = nc.tensor.matmul(dst[:, at:at + w], still, moving[0:KS, lo:lo + w], start=True, stop=True, skip_group_check=True)
                    last.then_inc(scores_ready, 1)

                def products(i, j, t):
                    m = SEQ[t][1]
                    if m in DIAG:
                        pe.wait_ge(mask_done, i * (2 * NG) + (j * NG + DIAG.index(m) + 1))
                    else:
                        pe.wait_ge(exp_done, i * (2 * NS) + (j * NS + t + 1 + S_RING))
                    for g, k, at, w in KT[m]:
                        dst, r = o_ps[g % O_RING], k % 4
                        first = k < 4
                        if first and k == 0:
                            pe.wait_ge(out_read, i * (2 * NG) + (j * NG + g + 1))
                        if first and w < BLK:
                            nc.tensor.matmul(dst[32 * r:32 * r + 32, :], zeros[:], probs[:, m % P_RING, 0:BLK],
                                             start=True, stop=False, skip_group_check=True)
                        last = nc.tensor.matmul(dst[32 * r:32 * r + 32, BLK - w:BLK], vh[j][:, k, :], probs[:, m % P_RING, at:at + w],
                                                start=first and w == BLK, stop=True, skip_group_check=True)
                    if m in DIAG:
                        last = nc.tensor.matmul(o_ps[DIAG.index(m) % O_RING][96:128, :], only_sum[:], hidden[:].rearrange("p r c -> p (r c)"),
                                                start=False, stop=True, skip_group_check=True)
                    last.then_inc(pv_done, 1)

                def turn(i, j, g):
                    pe.wait_ge(out_copied, i * (2 * NG) + (j * NG + g + 1))
                    for q in range(4):
                        last = nc.tensor.transpose(o_ps[g % O_RING][:, q * P:(q + 1) * P], o_sb[:, g % O_RING, q * P:(q + 1) * P], ident[:])
                    last.then_inc(out_turned, 1)

                with pe.Fori(0, pairs) as i:
                    for j in range(2):
                        pe.wait_ge(a_loaded[j], i * (16 * (A_DMAS + 1)) + 16 * (A_DMAS + 1))
                        pe.wait_ge(vh_ready, i * 2 + (j + 1))
                        for t in range(NS):
                            fill(i, j, t)
                            if t >= LAG and SEQ[t - LAG][0] == "K":
                                products(i, j, t - LAG)
                            if t in TURN_AT:
                                turn(i, j, TURN_AT[t])
                        for t in range(NS - LAG, NS):
                            if SEQ[t][0] == "K":
                                products(i, j, t)
                        turn(i, j, NG - 1)

            @block.scalar
            def _(act):
                act.sem_inc(exp_done, S_RING)
                act.wait_ge(fills_ready, 9)
                with act.Fori(0, pairs) as i:
                    for j in range(2):
                        act.wait_ge(head_done, i * 2 + (j + 1))
                        for t, (kind, m) in enumerate(SEQ):
                            src = scores[t % S_RING]
                            act.wait_ge(scores_ready, i * (2 * NS) + (j * NS + t + 1))
                            if kind == "K":
                                act.wait_ge(pv_done, i * (2 * NK) + (j * NK + m + 1 + 2 * NK))
                                w = sum(u[3] for u in KT[m])
                                last = nc.scalar.activation(probs[:, m % P_RING, 0:w], src[:, 0:w], ACT.Exp, scale=HD ** -0.5)
                            else:
                                for q, at, lo, w, col in QT[m]:
                                    last = nc.scalar.activation(src[:, at:at + w], src[:, at:at + w], ACT.Exp, scale=HD ** -0.5,
                                                                accum_out=sums[:, j, col:col + 1])
                            last.then_inc(exp_done, 1)

            @block.vector
            def _(dve):
                for j in range(2):
                    nc.vector.memset(ak[j][KR:KS, :], -1.0 / HD ** -0.5).then_inc(minus_ready, 1)
                dve.sem_inc(out_read, O_RING)
                dve.sem_inc(head_done, 2)
                LINKS = 2 * NG + 3

                def mask(i, j, g):
                    m = DIAG[g]
                    dve.wait_ge(exp_done, i * (2 * NS) + (j * NS + K_POS[m] + 1 + S_RING))
                    three = probs[:, m % P_RING, :].rearrange("p (r c) -> p r c", c=BLK)[:, :, 0:P]
                    fourth = probs[:, m % P_RING, D_AT[3]:D_AT[3] + P]
                    nc.vector.tensor_tensor(hidden[:, 0:3, :], three, after[:, 0:3, :], ALU.mult).then_inc(dve3, 1)
                    nc.vector.tensor_tensor(hidden[:, 3, :], fourth, after[:, 3, :], ALU.mult).then_inc(dve3, 1)
                    dve.wait_ge(dve3, i * (2 * LINKS) + (j * LINKS + 2 * g + 2))
                    nc.vector.tensor_tensor(three, three, upto[:, 0:3, :], ALU.mult)
                    nc.vector.tensor_tensor(fourth, fourth, upto[:, 3, :], ALU.mult).then_inc(mask_done, 1)

                def take(i, j, g):
                    dve.wait_ge(pv_done, i * (2 * NK) + (j * NK + LAST[g] + 1 + P_RING + 2 * NK))
                    nc.vector.tensor_copy(o_sb[:, g % O_RING, :], o_ps[g % O_RING][:]).then_inc(out_copied, 1)
                    dve.wait_ge(out_turned, i * (2 * NG) + (j * NG + g + 1))
                    turned = o_ps[g % O_RING][:].rearrange("p (q r d) -> p q d r", q=4, r=4)[:, :, 0:HD + 1, :]
                    nc.vector.tensor_reduce(num[:, 4 * g:4 * g + 4, :], turned, AX.X, ALU.add).then_inc(out_read, 1)

                with dve.Fori(0, pairs) as i:
                    for j in range(2):
                        dve.wait_ge(head_done, i * 2 + (j + 2))
                        for g in range(NG):
                            mask(i, j, g)
                            take(i, j, g)
                        step = i * (2 * LINKS) + (j * LINKS + 2 * NG)
                        dve.wait_ge(exp_done, i * (2 * NS) + (j * NS + NS + S_RING))
                        dve.wait_ge(out_read, i * (2 * NG) + (j * NG + NG + O_RING))
                        nc.vector.tensor_tensor(den[:], num[:, :, HD], sums[:, j, 0:NT], ALU.add).then_inc(dve3, 1)
                        dve.wait_ge(dve3, step + 1)
                        nc.vector.tensor_tensor(den[:, 0:3], den[:, 0:3], sums[:, j, NT:NT + 3], ALU.add).then_inc(dve3, 1)
                        dve.wait_ge(dve3, step + 2)
                        nc.vector.reciprocal(inv[:], den[:]).then_inc(dve3, 1)
                        dve.wait_ge(dve3, step + 3)
                        nc.vector.tensor_tensor(attn[:, bass.ds(i * 2 + j, 1), :, :].rearrange("p o t d -> p (o t) d"), num[:, :, 0:HD],
                                                inv[:, :, None].to_broadcast([P, NT, HD]), ALU.mult).then_inc(head_done, 1)


        h_added, st_ready, dve4 = sem("h_added"), sem("st_ready"), sem("dve4")
        var_ready, std_ready, h_ready = sem("var_ready"), sem("std_ready"), sem("h_ready")
        hT_ready, hT_copied, lg_ready, lg_copied, lgT_ready = sem("hT_ready"), sem("hT_copied"), sem("lg_ready"), sem("lg_copied"), sem("lgT_ready")
        wr_loaded, logit_off, p_exp = sem("wr_loaded"), sem("logit_off"), sem("p_exp")
        iota_ready, keep_ready, prefix_ready = sem("iota_ready"), sem("keep_ready"), sem("prefix_ready")
        over_ready, cand_ready, cand_count, dve5 = sem("over_ready"), sem("cand_ready"), sem("cand_count"), sem("dve5")
        rows_ready, rows_sent, acc_stored = sem("rows_ready"), sem("rows_sent"), sem("acc_stored")
        GT = 4
        GR = TT // GT
        with ExitStack() as st, nc.Block() as block:
            stats = sb(st, "stats", [P, TT, 6])
            mean = sb(st, "mean", [P, TT])
            var = sb(st, "var", [P, TT])
            std = sb(st, "std", [P, TT])
            rstd = sb(st, "rstd", [P, TT])
            tmp = sb(st, "tmp", [P, TT])
            h = sb(st, "h", [P, TT, ROW])
            hT = [sb(st, f"hT{j}", [P, DC, GT * P]) for j in range(2)]
            wr = sb(st, "wr", [P, DC, E])
            lg = [sb(st, f"lg{j}", [E, GT * P]) for j in range(2)]
            probs = sb(st, "rprobs", [P, TT, E])
            work = sb(st, "work", [P, TT, E])
            pick = [sb(st, f"pick{k}", [P, TT, E]) for k in range(TOPK)]
            keep = sb(st, "keep", [P, TT, E])
            wgt = sb(st, "wgt", [P, TOPK, TT])
            red = sb(st, "red", [P, TT])
            cs = [sb(st, f"cs{k}", [P, TT, E]) for k in range(2)]
            tot = sb(st, "tot", [P, TT, E])
            pos = sb(st, "pos", [P, TT, E])
            over = sb(st, "over", [P, 1])
            dest_f = sb(st, "dest_f", [P, TOPK, TT])
            dest = sb(st, "dest", [P, TOPK, TT], U32)
            ids = sb(st, "ids", [P, TT], I32)
            ebase_i = sb(st, "ebase_i", [P, E], I32)
            eid_i = sb(st, "eid_i", [P, E], I32)
            ebase = sb(st, "ebase", [P, E])
            eid = sb(st, "eid", [P, E])
            first = sb(st, "first", [P, E])
            wm = sb(st, "wm", [P, TT, E])
            tau = sb(st, "tau", [P, E], I32)
            cand = sb(st, "cand", [P, E], I32)
            bit = sb(st, "bit", [P, E], I32)
            bit_f = sb(st, "bit_f", [P, E])
            cnt = sb(st, "cnt", [P, E])
            step_i = sb(st, "step_i", [P, E], I32)
            hT_ps = [ps(st, f"hT_ps{j}", [P, DC, GT * P]) for j in range(2)]
            lg_ps = [ps(st, f"lg_ps{j}", [P, GT * P]) for j in range(2)]
            lgT_ps = ps(st, "lgT_ps", [P, TT, E])
            pf_ps = ps(st, "pf_ps", [P, 2, TT, E])

            def wide(x):
                return x[:, :, None].to_broadcast([P, TT, E])

            def each(x):
                return x[:, None, :].to_broadcast([P, TT, E])

            @block.sync
            def _(sp):
                sp.dma_start(wr[:], wr_T.rearrange("(c p) e -> p c e", p=P)).then_inc(wr_loaded, 16)
                sp.wait_ge(h_ready, TT)
                sp.dma_start(acc_dram.rearrange("(t p) d -> p t d", p=P), h[:, :, 0:D]).then_inc(acc_stored, 16)
                sp.wait_ge(wr_loaded, 16)
                sp.wait_ge(acc_stored, 16)

            @block.gpsimd
            def _(pool):
                pool.iota(ids[:], pattern=[[P, TT]], base=0, channel_multiplier=1).then_inc(iota_ready, 1)
                pool.iota(ebase_i[:], pattern=[[CAP, E]], base=0, channel_multiplier=0).then_inc(iota_ready, 1)
                pool.iota(eid_i[:], pattern=[[1, E]], base=0, channel_multiplier=0).then_inc(iota_ready, 1)
                pool.wait_ge(rows_ready, 1)
                for k in range(TOPK):
                    for t in range(TT):
                        pool.indirect_dma_start(out=xe_dram[:, :], out_offset=bass.IndirectOffsetOnAxis(ap=dest[:, k, t:t + 1], axis=0),
                                                in_=h[:, t, :], in_offset=None, bounds_check=E * CAP - 1,
                                                oob_is_err=False).then_inc(rows_sent, 16)
                pool.wait_ge(rows_sent, 16 * TOPK * TT)

            @block.scalar
            def _(act):
                act.wait_ge(var_ready, 1)
                nc.scalar.activation(std[:], var[:], ACT.Sqrt).then_inc(std_ready, 1)

                def copy_hT(g):
                    act.wait_ge(hT_ready, g + 1)
                    if g >= 2:
                        act.wait_ge(lg_ready, g - 1)
                    for c in range(DC):
                        nc.scalar.activation(hT[g % 2][:, c, :], hT_ps[g % 2][:, c, :], ACT.Copy).then_inc(hT_copied, 1)

                def copy_lg(g):
                    act.wait_ge(lg_ready, g + 1)
                    if g >= 2:
                        act.wait_ge(lgT_ready, g - 1)
                    nc.scalar.activation(lg[g % 2][:], lg_ps[g % 2][0:E, :], ACT.Copy).then_inc(lg_copied, 1)

                for g in range(GR + 1):
                    if g < GR:
                        copy_hT(g)
                    if g >= 1:
                        copy_lg(g - 1)
                act.wait_ge(logit_off, 1)
                nc.scalar.activation(probs[:], work[:], ACT.Exp).then_inc(p_exp, 1)

            def prefix_products():
                flat = keep[:].rearrange("p t e -> p (t e)")
                nc.tensor.matmul(pf_ps[:, 0].rearrange("p t e -> p (t e)"), before[:], flat, start=True, stop=True, skip_group_check=True)
                return nc.tensor.matmul(pf_ps[:, 1].rearrange("p t e -> p (t e)"), ones[:], flat, start=True, stop=True, skip_group_check=True)

            @block.tensor
            def _(pe):
                pe.wait_ge(wr_loaded, 16)

                def turn(g):
                    pe.wait_ge(h_ready, GT * (g + 1))
                    if g >= 2:
                        pe.wait_ge(hT_copied, DC * (g - 1))
                    for c in range(DC):
                        for t in range(GT):
                            last = nc.tensor.transpose(hT_ps[g % 2][:, c, t * P:(t + 1) * P], h[:, GT * g + t, c * P:(c + 1) * P], ident[:])
                    last.then_inc(hT_ready, 1)

                def logits(g):
                    pe.wait_ge(hT_copied, DC * (g + 1))
                    if g >= 2:
                        pe.wait_ge(lg_copied, g - 1)
                    for c in range(DC):
                        last = nc.tensor.matmul(lg_ps[g % 2][0:E, :], wr[:, c, :], hT[g % 2][:, c, :], start=(c == 0), stop=(c == DC - 1))
                    last.then_inc(lg_ready, 1)

                def turn_back(g):
                    pe.wait_ge(lg_copied, g + 1)
                    for t in range(GT):
                        last = nc.tensor.transpose(lgT_ps[:, GT * g + t, :], lg[g % 2][:, t * P:(t + 1) * P], ident[0:E, 0:E])
                    last.then_inc(lgT_ready, 1)

                for g in range(GR + 2):
                    if g < GR:
                        turn(g)
                    if 1 <= g <= GR:
                        logits(g - 1)
                    if g >= 2:
                        turn_back(g - 2)
                pe.wait_ge(keep_ready, 1)
                prefix_products().then_inc(prefix_ready, 1)
                pe.wait_ge(over_ready, 1)
                too_many = pe.value_load(flag[0:1, 1:2], min_val=0, max_val=1)
                with pe.If(too_many > 0):
                    with pe.Fori(0, TAU_BITS) as i:
                        pe.wait_ge(cand_ready, i * 1 + 1)
                        nc.tensor.matmul(lg_ps[0][:, 0:E], ones[:], cnt[:], start=True, stop=True).then_inc(cand_count, 1)
                    pe.wait_ge(cand_ready, TAU_BITS + 1)
                    nc.tensor.matmul(lg_ps[0][:, 0:E], ones[:], cnt[:], start=True, stop=True).then_inc(cand_count, 1)
                    for n in range(2):
                        pe.wait_ge(keep_ready, n + 2)
                        prefix_products().then_inc(prefix_ready, 1)

            @block.vector
            def _(dve):
                link = chain(dve, dve4)
                for b in range(B):
                    whole = x_sb[:, b * NT:(b + 1) * NT, :].rearrange("p t (h d) -> p t h d", h=H)
                    nc.vector.tensor_tensor(whole, whole, attn[:, b * H:(b + 1) * H, :, :].rearrange("p h t d -> p t h d"),
                                            ALU.add).then_inc(h_added, 1)
                dve.wait_ge(h_added, B)
                with dve.Fori(0, TT) as t:
                    nc.vector.bn_stats(stats[:, bass.ds(t, 1), :].rearrange("p o s -> p (o s)"),
                                       x_sb[:, bass.ds(t, 1), :].rearrange("p o d -> p (o d)")).then_inc(st_ready, 1)
                dve.wait_ge(st_ready, TT)
                layer_stats(nc, link, stats, mean[:], var[:], tmp[:]).then_inc(var_ready, 1)
                dve.wait_ge(std_ready, 1)
                inverse_root(nc, link, var[:], std[:], rstd[:], tmp[:])
                with dve.Fori(0, TT) as t:
                    nc.vector.tensor_scalar(h[:, bass.ds(t, 1), 0:D].rearrange("p o d -> p (o d)"),
                                            x_sb[:, bass.ds(t, 1), :].rearrange("p o d -> p (o d)"),
                                            mean[:, bass.ds(t, 1)], rstd[:, bass.ds(t, 1)], ALU.subtract, ALU.mult).then_inc(h_ready, 1)

                dve.wait_ge(lgT_ready, GR)
                link(nc.vector.tensor_reduce(red[:], lgT_ps[:], AX.X, ALU.max))
                nc.vector.tensor_tensor(work[:], lgT_ps[:], wide(red), ALU.subtract).then_inc(logit_off, 1)
                dve.wait_ge(iota_ready, 3)
                link(nc.vector.tensor_copy(ebase[:], ebase_i[:]))
                link(nc.vector.tensor_copy(eid[:], eid_i[:]))
                link(nc.vector.tensor_scalar(first[:], eid[:], -1.0, float(E), ALU.mult, ALU.add))
                link(nc.vector.tensor_copy(h[:, :, COL_ID], ids[:]))
                link(nc.vector.memset(h[:, :, COL_ID + 1:ROW], 0.0))
                dve.wait_ge(p_exp, 1)
                link(nc.vector.tensor_reduce(red[:], probs[:], AX.X, ALU.add))
                link(nc.vector.reciprocal(tmp[:], red[:]))
                link(nc.vector.tensor_tensor(probs[:], probs[:], wide(tmp), ALU.mult))
                for k in range(TOPK):
                    link(nc.vector.tensor_reduce(wgt[:, k, :], probs[:], AX.X, ALU.max))
                    link(nc.vector.tensor_tensor(work[:], probs[:], wide(wgt[:, k, :]), ALU.is_equal))
                    link(nc.vector.tensor_tensor(work[:], work[:], each(first), ALU.mult))
                    link(nc.vector.tensor_reduce(red[:], work[:], AX.X, ALU.max))
                    link(nc.vector.tensor_tensor(pick[k][:], work[:], wide(red), ALU.is_equal))
                    if k == 0:
                        link(nc.vector.scalar_tensor_tensor(probs[:], pick[0][:], -4.0, probs[:], ALU.mult, ALU.add))

                def normalise_weights():
                    link(nc.vector.tensor_tensor(red[:], wgt[:, 0, :], wgt[:, 1, :], ALU.add))
                    link(nc.vector.tensor_scalar(red[:], red[:], MOE_EPS, None, ALU.max))
                    link(nc.vector.reciprocal(tmp[:], red[:]))
                    link(nc.vector.tensor_tensor(wgt[:], wgt[:], tmp[:, None, :].to_broadcast([P, TOPK, TT]), ALU.mult))

                normalise_weights()
                nc.vector.tensor_tensor(keep[:], pick[0][:], pick[1][:], ALU.add).then_inc(keep_ready, 1)

                def prefixes(link, n):
                    dve.wait_ge(prefix_ready, n)
                    link(nc.vector.tensor_copy(tot[:], pf_ps[:, 1]))
                    a, s, src = 0, 1, tot
                    while s < TT:
                        nc.vector.tensor_copy(cs[a][:, 0:s, :], src[:, 0:s, :])
                        link(nc.vector.tensor_tensor(cs[a][:, s:, :], src[:, s:, :], src[:, :TT - s, :], ALU.add))
                        a, s, src = 1 - a, 2 * s, cs[a]
                    link(nc.vector.tensor_tensor(pos[:], src[:], tot[:], ALU.subtract))
                    link(nc.vector.tensor_tensor(pos[:], pos[:], pf_ps[:, 0], ALU.add))
                    return src

                upto_tile = prefixes(link, 1)
                link(nc.vector.tensor_reduce(over[:], upto_tile[:, TT - 1, :], AX.X, ALU.max))
                nc.vector.tensor_scalar(flag[0:1, 1:2], over[0:1, :], float(CAP), None, ALU.is_gt).then_inc(over_ready, 1)
                dve.wait_ge(over_ready, 1)
                too_many = dve.value_load(flag[0:1, 1:2], min_val=0, max_val=1)
                with dve.If(too_many > 0):
                    link5 = chain(dve, dve5)
                    link5(nc.vector.tensor_tensor(wm[:], pick[0][:], wide(wgt[:, 0, :]), ALU.mult))
                    link5(nc.vector.tensor_tensor(work[:], pick[1][:], wide(wgt[:, 1, :]), ALU.mult))
                    link5(nc.vector.tensor_tensor(wm[:], wm[:], work[:], ALU.add))
                    link5(nc.vector.scalar_tensor_tensor(wm[:], keep[:], -1.0, wm[:], ALU.add, ALU.add))
                    link5(nc.vector.memset(tau[:], 0))
                    link5(nc.vector.memset(bit[:], 1 << (TAU_BITS - 1)))
                    pre = link5.count()
                    with dve.Fori(0, TAU_BITS) as i:
                        at = i * 6 + pre
                        nc.vector.tensor_tensor(cand[:], tau[:], bit[:], ALU.bitwise_or).then_inc(dve5, 1)
                        dve.wait_ge(dve5, at + 1)
                        nc.vector.tensor_tensor(work[:], wm[:], each(cand.bitcast(FP32)), ALU.is_ge).then_inc(dve5, 1)
                        dve.wait_ge(dve5, at + 2)
                        nc.vector.tensor_reduce(cnt[:], work[:].rearrange("p t e -> p e t"), AX.X, ALU.add).then_inc(cand_ready, 1)
                        nc.vector.tensor_copy(bit_f[:], bit[:]).then_inc(dve5, 1)
                        dve.wait_ge(dve5, at + 3)
                        dve.wait_ge(cand_count, i * 1 + 1)
                        nc.vector.scalar_tensor_tensor(step_i[:], lg_ps[0][:, 0:E], float(CAP), bit_f[:], ALU.is_ge, ALU.mult).then_inc(dve5, 1)
                        dve.wait_ge(dve5, at + 4)
                        nc.vector.tensor_tensor(tau[:], tau[:], step_i[:], ALU.bitwise_or).then_inc(dve5, 1)
                        nc.vector.tensor_scalar(bit[:], bit[:], 1, None, ALU.logical_shift_right).then_inc(dve5, 1)
                        dve.wait_ge(dve5, at + 6)
                    link5.skip(6 * TAU_BITS)
                    link5(nc.vector.tensor_tensor(work[:], wm[:], each(tau.bitcast(FP32)), ALU.is_gt))
                    nc.vector.tensor_reduce(cnt[:], work[:].rearrange("p t e -> p e t"), AX.X, ALU.add).then_inc(cand_ready, 1)
                    nc.vector.tensor_tensor(keep[:], wm[:], each(tau.bitcast(FP32)), ALU.is_equal).then_inc(keep_ready, 1)
                    dve.wait_ge(cand_count, TAU_BITS + 1)
                    link5(nc.vector.tensor_copy(cnt[:], lg_ps[0][:, 0:E]))
                    prefixes(link5, 2)
                    link5(nc.vector.tensor_tensor(pos[:], pos[:], each(cnt), ALU.add))
                    link5(nc.vector.scalar_tensor_tensor(wm[:], pos[:], float(CAP), keep[:], ALU.is_lt, ALU.mult))
                    nc.vector.tensor_tensor(keep[:], work[:], wm[:], ALU.add).then_inc(keep_ready, 1)
                    prefixes(link5, 3)
                link(nc.vector.tensor_tensor(pos[:], pos[:], each(ebase), ALU.add))
                for k in range(TOPK):
                    link(nc.vector.tensor_tensor(work[:], pick[k][:], keep[:], ALU.mult))
                    link(nc.vector.tensor_reduce(red[:], work[:], AX.X, ALU.add))
                    link(nc.vector.tensor_tensor(wgt[:, k, :], wgt[:, k, :], red[:], ALU.mult))
                    link(nc.vector.tensor_tensor(work[:], work[:], pos[:], ALU.mult))
                    link(nc.vector.tensor_reduce(dest_f[:, k, :], work[:], AX.X, ALU.add))
                    link(nc.vector.tensor_scalar(red[:], red[:], -float(E * CAP), float(E * CAP), ALU.mult, ALU.add))
                    link(nc.vector.tensor_tensor(dest_f[:, k, :], dest_f[:, k, :], red[:], ALU.add))
                    link(nc.vector.tensor_tensor(work[:], pick[k][:], each(eid), ALU.mult))
                    link(nc.vector.tensor_reduce(h[:, :, COL_E + k], work[:], AX.X, ALU.add))
                link(nc.vector.tensor_copy(dest[:], dest_f[:]))
                normalise_weights()
                nc.vector.tensor_copy(h[:, :, COL_W:COL_W + TOPK], wgt[:].rearrange("p k t -> p t k")).then_inc(rows_ready, 1)
        att.close()

        e_loaded = [sem(f"e_loaded{j}") for j in range(2)]
        xt_ready, xt_copied, wt_ready = sem("xt_ready"), sem("xt_copied"), sem("wt_ready")
        up_ready, silu_done, mid_done = sem("up_ready"), sem("silu_done"), sem("mid_done")
        y_ready, y_done, added, expert_over, adding, dve6 = sem("y_ready"), sem("y_done"), sem("added"), sem("expert_over"), sem("adding"), sem("dve6")
        with ExitStack() as st, nc.Block() as block:
            XG = [(t, min(4, CT - t)) for t in range(0, CT, 4)]
            UNITS = [(f, t, n) for f in range(FC) for t, n in XG]
            w1 = [sb(st, f"w1_{j}", [P, DC, F]) for j in range(2)]
            wg = [sb(st, f"wg_{j}", [P, DC, F]) for j in range(2)]
            w2 = [sb(st, f"w2_{j}", [P, FC, D]) for j in range(2)]
            xin = [sb(st, f"xin{j}", [P, CT, ROW]) for j in range(2)]
            xT = sb(st, "xeT", [P, DC, CAP])
            gate = [sb(st, f"gate{j}", [P, BLK]) for j in range(2)]
            mid = sb(st, "mid", [P, FC, CAP])
            y = [sb(st, f"y{j}", [P, CT, D]) for j in range(2)]
            wt = sb(st, "wt", [P, 2, CT])
            wt2 = sb(st, "wt2", [P, CT])
            row = [sb(st, f"row{j}", [P, CT], U32) for j in range(2)]
            e_now = sb(st, "e_now", [P, 1])
            xt_ps = [ps(st, f"xt_ps{j}", [P, BLK]) for j in range(2)]
            pre_ps = [ps(st, f"pre_ps{j}", [P, BLK]) for j in range(2)]
            gate_ps = [ps(st, f"gate_ps{j}", [P, BLK]) for j in range(2)]
            y_ps = [ps(st, f"y_ps{j}", [P, D]) for j in range(2)]
            XN, UN = DC * len(XG), len(UNITS)

            @block.sync
            def _(sp):
                def load_expert(j, e):
                    one = bass.ds(e, 1)
                    sp.dma_start(xin[j][:], xe_dram[bass.ds(e * CAP, CAP), :].rearrange("(s p) c -> p s c", p=P)).then_inc(e_loaded[j], 16)
                    sp.dma_start(w1[j][:], w1_T[one].rearrange("o (c p) f -> p (o c) f", p=P)).then_inc(e_loaded[j], 16)
                    sp.dma_start(wg[j][:], wg_T[one].rearrange("o (c p) f -> p (o c) f", p=P)).then_inc(e_loaded[j], 16)
                    sp.dma_start(w2[j][:], w2_T[one].rearrange("o (c p) d -> p (o c) d", p=P)).then_inc(e_loaded[j], 16)

                for j in range(2):
                    load_expert(j, j)
                with sp.Fori(1, E // 2) as i:
                    for j in range(2):
                        sp.wait_ge(y_done, i * (2 * CT) + ((j - 1) * CT + 2))
                        load_expert(j, i * 2 + j)

            @block.gpsimd
            def _(pool):
                pool.sem_inc(expert_over, 2)
                with pool.Fori(0, E // 2) as i:
                    for j in range(2):
                        pool.wait_ge(y_done, i * (2 * CT) + ((j + 1) * CT + 2))
                        pool.sem_inc(adding, 1)
                        for t in range(CT):
                            pool.indirect_dma_start(out=acc_dram[:, :], out_offset=bass.IndirectOffsetOnAxis(ap=row[j][:, t:t + 1], axis=0),
                                                    in_=y[j][:, t, :], in_offset=None, bounds_check=T - 1, oob_is_err=False,
                                                    compute_op=ALU.add).then_inc(added, 16)
                        pool.wait_ge(added, i * (2 * 16 * CT) + (j + 1) * 16 * CT)
                        pool.sem_inc(expert_over, 1)

            @block.tensor
            def _(pe):
                with pe.Fori(0, E // 2) as i:
                    for j in range(2):
                        pe.wait_ge(e_loaded[j], i * 64 + 64)
                        for n, (c, (t0, nt)) in enumerate((c, x) for c in range(DC) for x in XG):
                            pe.wait_ge(xt_copied, i * (2 * XN) + (j * XN + n + 1))
                            for t in range(nt):
                                last = nc.tensor.transpose(xt_ps[n % 2][:, t * P:(t + 1) * P], xin[j][:, t0 + t, c * P:(c + 1) * P], ident[:])
                            last.then_inc(xt_ready, 1)
                        pe.wait_ge(xt_copied, i * (2 * XN) + ((j + 1) * XN + 2))
                        for n, (f, t0, nt) in enumerate(UNITS):
                            pe.wait_ge(mid_done, i * (2 * UN) + (j * UN + n + 1))
                            for dst, w in ((gate_ps, wg), (pre_ps, w1)):
                                for c in range(DC):
                                    last = nc.tensor.matmul(dst[n % 2][:, 0:nt * P], w[j][:, c, f * P:(f + 1) * P], xT[:, c, t0 * P:(t0 + nt) * P],
                                                            start=(c == 0), stop=(c == DC - 1))
                            last.then_inc(up_ready, 1)
                        pe.wait_ge(mid_done, i * (2 * UN) + ((j + 1) * UN + 2))
                        for t in range(CT):
                            pe.wait_ge(y_done, i * (2 * CT) + (j * CT + t + 1))
                            for f in range(FC):
                                last = nc.tensor.matmul(y_ps[t % 2][:], mid[:, f, t * P:(t + 1) * P], w2[j][:, f, :],
                                                        start=(f == 0), stop=(f == FC - 1))
                            last.then_inc(y_ready, 1)

            @block.scalar
            def _(act):
                act.sem_inc(xt_copied, 2)
                with act.Fori(0, E // 2) as i:
                    for j in range(2):
                        for n, (c, (t0, nt)) in enumerate((c, x) for c in range(DC) for x in XG):
                            act.wait_ge(xt_ready, i * (2 * XN) + (j * XN + n + 1))
                            nc.scalar.activation(xT[:, c, t0 * P:(t0 + nt) * P], xt_ps[n % 2][:, 0:nt * P], ACT.Copy).then_inc(xt_copied, 1)
                        for n, (f, t0, nt) in enumerate(UNITS):
                            act.wait_ge(up_ready, i * (2 * UN) + (j * UN + n + 1))
                            act.wait_ge(mid_done, i * (2 * UN) + (j * UN + n + 1))
                            nc.scalar.activation(gate[n % 2][:, 0:nt * P], gate_ps[n % 2][:, 0:nt * P], ACT.Silu).then_inc(silu_done, 1)

            @block.vector
            def _(dve):
                dve.sem_inc(mid_done, 2)
                dve.sem_inc(y_done, 2)
                nc.vector.memset(e_now[:], 0.0).then_inc(dve6, 1)
                LINKS = 4
                with dve.Fori(0, E // 2) as i:
                    for j in range(2):
                        step = i * (2 * LINKS) + (j * LINKS + 1)
                        dve.wait_ge(e_loaded[j], i * 64 + 64)
                        dve.wait_ge(dve6, step)
                        dve.wait_ge(y_done, i * (2 * CT) + (j * CT + 2))
                        dve.wait_ge(expert_over, i * 2 + (j + 1))
                        for k in range(TOPK):
                            nc.vector.scalar_tensor_tensor(wt[:, k, :], xin[j][:, :, COL_E + k], e_now[:], xin[j][:, :, COL_W + k],
                                                           ALU.is_equal, ALU.mult).then_inc(dve6, 1)
                        nc.vector.tensor_copy(row[j][:], xin[j][:, :, COL_ID])
                        dve.wait_ge(dve6, step + 2)
                        nc.vector.tensor_tensor(wt2[:], wt[:, 0, :], wt[:, 1, :], ALU.add).then_inc(dve6, 1)
                        nc.vector.tensor_scalar(e_now[:], e_now[:], 1.0, None, ALU.add).then_inc(dve6, 1)
                        for n, (f, t0, nt) in enumerate(UNITS):
                            dve.wait_ge(silu_done, i * (2 * UN) + (j * UN + n + 1))
                            nc.vector.tensor_tensor(mid[:, f, t0 * P:(t0 + nt) * P], pre_ps[n % 2][:, 0:nt * P], gate[n % 2][:, 0:nt * P],
                                                    ALU.mult).then_inc(mid_done, 1)
                        for t in range(CT):
                            dve.wait_ge(y_ready, i * (2 * CT) + (j * CT + t + 1))
                            nc.vector.tensor_scalar(y[j][:, t, :], y_ps[t % 2][:], wt2[:, t:t + 1], None, ALU.mult).then_inc(y_done, 1)

        CH = 8
        acc_loaded = [sem(f"acc_loaded{c}") for c in range(TT // CH)]
        st2_ready, var2_ready, std2_ready, dve7, normed, stored = sem("st2_ready"), sem("var2_ready"), sem("std2_ready"), sem("dve7"), sem("normed"), sem("stored")
        with ExitStack() as st, nc.Block() as block:
            a = sb(st, "a", [P, TT, D])
            stats = sb(st, "stats2", [P, TT, 6])
            mean = sb(st, "mean2", [P, TT])
            var = sb(st, "var2", [P, TT])
            std = sb(st, "std2", [P, TT])
            rstd = sb(st, "rstd2", [P, TT])
            tmp = sb(st, "tmp2", [P, TT])
            acc_view = acc_dram.rearrange("(t p) d -> p t d", p=P)
            out_view = out.rearrange("(t p) d -> p t d", p=P)

            @block.sync
            def _(sp):
                for c in range(TT // CH):
                    part = slice(c * CH, (c + 1) * CH)
                    sp.dma_start(a[:, part, :], acc_view[:, part, :]).then_inc(acc_loaded[c], 16)
                for c in range(TT // CH):
                    part = slice(c * CH, (c + 1) * CH)
                    sp.wait_ge(normed, (c + 1) * CH)
                    sp.dma_start(out_view[:, part, :], a[:, part, :]).then_inc(stored, 16)
                sp.wait_ge(stored, 16 * (TT // CH))

            @block.scalar
            def _(act):
                act.wait_ge(var2_ready, 1)
                nc.scalar.activation(std[:], var[:], ACT.Sqrt).then_inc(std2_ready, 1)

            @block.vector
            def _(dve):
                link = chain(dve, dve7)
                for c in range(TT // CH):
                    dve.wait_ge(acc_loaded[c], 16)
                    with dve.Fori(c * CH, (c + 1) * CH) as t:
                        nc.vector.bn_stats(stats[:, bass.ds(t, 1), :].rearrange("p o s -> p (o s)"),
                                           a[:, bass.ds(t, 1), :].rearrange("p o d -> p (o d)")).then_inc(st2_ready, 1)
                dve.wait_ge(st2_ready, TT)
                layer_stats(nc, link, stats, mean[:], var[:], tmp[:]).then_inc(var2_ready, 1)
                dve.wait_ge(std2_ready, 1)
                inverse_root(nc, link, var[:], std[:], rstd[:], tmp[:])
                with dve.Fori(0, TT) as t:
                    tile = a[:, bass.ds(t, 1), :].rearrange("p o d -> p (o d)")
                    nc.vector.tensor_scalar(tile, tile, mean[:, bass.ds(t, 1)], rstd[:, bass.ds(t, 1)],
                                            ALU.subtract, ALU.mult).then_inc(normed, 1)


def kernel(L0_attn_content, L0_attn_Wq, L0_attn_Wk, L0_attn_Wv, L0_ffn_router_weight, L0_ffn_ff_pre_act_weight,
           L0_ffn_gate_weight, L0_ffn_ff_post_act_weight):
    import numpy as np
    import concourse.bacc as bacc
    from concourse.bass_utils import run_bass_kernel_spmd

    x = np.asarray(L0_attn_content).reshape(T, D)
    arrays = {
        "x_tok": x,
        "x_T": x.T,
        "wq": np.asarray(L0_attn_Wq),
        "wk": np.asarray(L0_attn_Wk),
        "wv": np.asarray(L0_attn_Wv),
        "wr_T": np.asarray(L0_ffn_router_weight).T,
        "w1_T": np.asarray(L0_ffn_ff_pre_act_weight).transpose(0, 2, 1),
        "wg_T": np.asarray(L0_ffn_gate_weight).transpose(0, 2, 1),
        "w2_T": np.asarray(L0_ffn_ff_post_act_weight).transpose(0, 2, 1),
    }
    arrays = {name: np.ascontiguousarray(a) for name, a in arrays.items()}
    nc = bacc.Bacc("TRN2", target_bir_lowering=False, num_devices=1)
    args = [nc.dram_tensor(name, a.shape, mybir.dt.from_np(a.dtype), kind="ExternalInput").ap() for name, a in arrays.items()]
    out = nc.dram_tensor("out", (T, D), FP32, kind="ExternalOutput").ap()
    program(nc, *args, out)
    result = run_bass_kernel_spmd(nc, [arrays], core_ids=[0])
    return result.results[0]["out"].reshape(B, N, D)
```

```python
import concourse.bass as bass
from concourse import mybir
from contextlib import ExitStack

FP32 = mybir.dt.float32
BF16 = mybir.dt.bfloat16
FP32R = mybir.dt.float32r
I32 = mybir.dt.int32
U32 = mybir.dt.uint32
ALU = mybir.AluOpType
ACT = mybir.ActivationFunctionType
AX = mybir.AxisListType

P = 128
B, N, D = 2, 2048, 256
H, HD = 16, 16
T = B * N
NH = B * H
DC = D // P
TT = T // P
NT = N // P
BLK = 512
E, TOPK, F = 8, 2, 1024
FC = F // P
CAP = 1280
CT = CAP // P
GA = 512
GC = CAP - 2 * GA
NA, NC = GA // P, GC // P
ROW = 264
COL_W, COL_E, COL_ID = 256, 258, 260
LN_EPS = 1e-5
MOE_EPS = 1.1920929e-07
TAU_BITS = 30
BOUND_MAX = 30.0

KSPAN = 3 * BLK
NG = N // BLK
D_AT = (0, 512, 1024, 896)


def key_tiles():
    diag = [[(g, 4 * g + r, D_AT[r], BLK - P * r) for r in range(4)] for g in range(NG)]
    full = [(g, j) for g in range(NG) for j in range(4 * g)]
    off = [[(g, j, BLK * n, BLK) for n, (g, j) in enumerate(full[3 * f:3 * f + 3])] for f in range(8)]
    return [diag[0], off[0], off[1], diag[1], off[2], off[3], diag[2], off[4], off[5], diag[3], off[6], off[7]]


def query_tiles():
    pieces = []
    for i in range(NT - 1):
        lo, left = P * (i + 1), N - P * (i + 1)
        if left > KSPAN:
            pieces.append((i, lo, KSPAN, i))
            pieces.append((i, lo + KSPAN, left - KSPAN, NT + i))
        else:
            pieces.append((i, lo, left, i))
    tiles = []
    for i, lo, w, col in sorted(pieces, key=lambda x: -x[2]):
        for t in tiles:
            if sum(x[3] for x in t) + w <= KSPAN:
                t.append((i, sum(x[3] for x in t), lo, w, col))
                break
        else:
            tiles.append([(i, 0, lo, w, col)])
    return tiles


KT = key_tiles()
QT = query_tiles()
NK, NQ = len(KT), len(QT)
ORDER = "KQKKKQKQKQQKQKQKKKQQKQ"
assert ORDER.count("K") == NK and ORDER.count("Q") == NQ
MANY = [n for n in range(NQ) if len(QT[n]) > 1]
Q_ORDER = MANY + [n for n in range(NQ) if n not in MANY]
SEQ = []
for c in ORDER:
    n = sum(1 for k, _ in SEQ if k == c)
    SEQ.append((c, n if c == "K" else Q_ORDER[n]))
NS = len(SEQ)
NM = len(MANY)
K_POS = [n for n, (k, _) in enumerate(SEQ) if k == "K"]
Q_POS = {m: n for n, (k, m) in enumerate(SEQ) if k == "Q"}
DIAG = [0, 3, 6, 9]
LAST = [max(m for m in range(NK) if any(u[0] == g for u in KT[m])) for g in range(NG)]
S_RING, P_RING, O_RING, X_RING = 2, 4, 2, 2


UNIT_AT = {3: ("D", 0), 6: ("G", 0), 8: ("G", 1), 10: ("D", 1), 13: ("G", 2), 15: ("D", 2),
           18: ("G", 3), 20: ("G", 4), 21: ("D", 3), 23: ("G", 5)}
TURN_AT = {5: 0, 14: 1, 17: 2, 26: 3}


def product_units():
    diag = {("D", g): [(DIAG[g],) + u for u in KT[DIAG[g]]] for g in range(NG)}
    off = [(m,) + u for m in range(NK) if m not in DIAG for u in KT[m]]
    groups = {("G", n): off[4 * n:4 * n + 4] for n in range(len(off) // 4)}
    units, over, left = {}, 0, {m: len(KT[m]) for m in range(NK)}
    for t in sorted(UNIT_AT):
        name = UNIT_AT[t]
        unit = (diag | groups)[name]
        for u in unit:
            left[u[0]] -= 1
        done = 0
        while over < NK and left[over] == 0:
            over, done = over + 1, done + 1
        assert done
        units[name] = (unit, done)
    assert over == NK and len(units) == NG + len(groups)
    return units


UNITS = product_units()
AFTER = [[(back, work, what[t + back * NS]) for back in (1, 0) for work, what in (("unit", UNIT_AT), ("turn", TURN_AT)) if t + back * NS in what]
         for t in range(NS)]
DVE_ORDER = ((0, "mask", 0), (1, "take", 3), (0, "sum", 0), (0, "take", 0), (1, "gather", 3), (1, "final", 0),
             (0, "mask", 1), (0, "gather", 0), (0, "sum", 1), (0, "sum", 2), (0, "sum", 3), (0, "take", 1),
             (0, "sum", 4), (0, "mask", 2), (0, "sum", 5), (0, "gather", 1), (0, "take", 2), (0, "mask", 3),
             (0, "gather", 2))


def chain(eng, semaphore):
    count = [0]

    def link(instruction):
        count[0] += 1
        instruction.then_inc(semaphore, 1)
        eng.wait_ge(semaphore, count[0])

    def skip(n):
        count[0] += n

    link.count, link.skip = lambda: count[0], skip
    return link


def layer_stats(nc, link, stats, mean, var, tmp):
    link(nc.vector.tensor_tensor(mean, stats[:, :, 1], stats[:, :, 4], ALU.add))
    link(nc.vector.tensor_scalar(mean, mean, 0.5, None, ALU.mult))
    link(nc.vector.tensor_tensor(tmp, stats[:, :, 1], mean, ALU.subtract))
    link(nc.vector.tensor_tensor(tmp, tmp, tmp, ALU.mult))
    link(nc.vector.tensor_tensor(var, stats[:, :, 2], stats[:, :, 5], ALU.add))
    link(nc.vector.tensor_scalar(var, var, 1.0 / D, LN_EPS, ALU.mult, ALU.add))
    return nc.vector.tensor_tensor(var, var, tmp, ALU.add)


def inverse_root(nc, link, var, std, rstd, tmp):
    link(nc.vector.reciprocal(rstd, std))
    link(nc.vector.tensor_tensor(tmp, rstd, rstd, ALU.mult))
    link(nc.vector.tensor_tensor(tmp, tmp, var, ALU.mult))
    link(nc.vector.tensor_scalar(tmp, tmp, -0.5, 1.5, ALU.mult, ALU.add))
    return nc.vector.tensor_tensor(rstd, rstd, tmp, ALU.mult)


def program(nc, x_tok, x_T, wq, wk, wv, wr_T, w1_T, wg_T, w2_T, out):
    ctx = ExitStack()
    with ctx:
        def sem(name):
            return ctx.enter_context(nc.semaphore(name))

        def sb(stack, name, shape, dt=FP32):
            return stack.enter_context(nc.sbuf_tensor(name, shape, dt))

        def ps(stack, name, shape, dt=FP32):
            return stack.enter_context(nc.psum_tensor(name, shape, dt))

        split_dram = nc.dram_tensor("split_dram", (2, 3, NH * HD, N), BF16).ap()
        shift_dram = nc.dram_tensor("shift_dram", (2, NH, N), BF16).ap()
        xe_dram = nc.dram_tensor("xe_dram", (E * CAP, ROW), FP32).ap()
        acc_dram = nc.dram_tensor("acc_dram", (T, D), FP32).ap()

        ident = sb(ctx, "ident", [P, P])
        ones = sb(ctx, "ones", [P, P])
        before = sb(ctx, "before", [P, P])
        upto = sb(ctx, "upto", [P, 4, P])
        after = sb(ctx, "after", [P, 4, P])
        one_head = sb(ctx, "one_head", [P, DC, H], BF16)
        flag = sb(ctx, "flag", [1, 4], I32)
        more = sb(ctx, "more", [1, E], I32)
        more_before = sb(ctx, "more_before", [1, E], I32)
        consts_ready = sem("consts_ready")

        att = ctx.enter_context(ExitStack())
        v_all = sb(att, "v_all", [P, NH, NT, HD])
        blank = sb(att, "blank", [P, ROW])

        NB = T // BLK
        U = 2 * DC
        xT_loaded = [sem(f"xT_loaded{j}") for j in range(2)]
        w_loaded = sem("w_loaded")
        proj_ready, hi_ready, proj_split = sem("proj_ready"), sem("hi_ready"), sem("proj_split")
        sq_ready, norm_ready, norm_read = sem("sq_ready"), sem("norm_ready"), sem("norm_read")
        v_ready, v_read = sem("v_ready"), sem("v_read")
        dve1, parts_stored, shift_ready, shift_stored = sem("dve1"), sem("parts_stored"), sem("shift_ready"), sem("shift_stored")
        top_ready, top_row, flag_ready = sem("top_ready"), sem("top_row"), sem("flag_ready")
        blank_ready, xe_cleared = sem("blank_ready"), sem("xe_cleared")

        with ExitStack() as st, nc.Block() as block:
            xT = sb(st, "xT", [P, 2, DC, BLK])
            w_qk = sb(st, "w_qk", [P, 2, DC, D])
            w_v = sb(st, "w_v", [P, DC, D])
            parts = sb(st, "parts", [P, 3, U, T], BF16)
            rest = sb(st, "rest", [P, BLK])
            sq = sb(st, "sq", [P, U, BLK], BF16)
            qn = sb(st, "qn", [H, N])
            kn = sb(st, "kn", [H, NB // B])
            kmax = sb(st, "kmax", [H, 1])
            shift = sb(st, "shift", [H, 2, T], BF16)
            bound = sb(st, "bound", [H, N])
            topb = sb(st, "topb", [H, B])
            top = sb(st, "top", [H, 1])
            topr = sb(st, "topr", [1, 1])
            proj = ps(st, "proj", [P, U, BLK])
            norm = ps(st, "norm", [P, 2, BLK])
            vps = ps(st, "vps", [P, 2, 2, D])

            @block.gpsimd
            def _(pool):
                pool.memset(ident[:], 0.0).then_inc(consts_ready, 1)
                pool.memset(ones[:], 1.0).then_inc(consts_ready, 1)
                pool.memset(one_head[:], 1.0).then_inc(consts_ready, 1)
                pool.memset(upto[:], 1.0).then_inc(consts_ready, 1)
                pool.memset(after[:], 1.0).then_inc(consts_ready, 1)
                pool.memset(blank[:], 0.0).then_inc(consts_ready, 1)
                pool.wait_ge(consts_ready, 6)
                pool.memset(blank[:, COL_ID:COL_ID + 1], float(T)).then_inc(blank_ready, 1)
                pool.affine_select(out=ident[:], in_=ident[:], compare_op=ALU.not_equal, fill=1.0, base=0,
                                   pattern=[[-1, P]], channel_multiplier=1).then_inc(consts_ready, 1)
                pool.affine_select(out=before[:], in_=ones[:], compare_op=ALU.is_gt, fill=0.0, base=0,
                                   pattern=[[1, P]], channel_multiplier=-1).then_inc(consts_ready, 1)
                pool.affine_select(out=upto[:], in_=upto[:], compare_op=ALU.is_ge, fill=0.0, base=0,
                                   pattern=[[0, 4], [1, P]], channel_multiplier=-1).then_inc(consts_ready, 1)
                pool.affine_select(out=after[:], in_=after[:], compare_op=ALU.is_gt, fill=0.0, base=0,
                                   pattern=[[0, 4], [-1, P]], channel_multiplier=1).then_inc(consts_ready, 1)
                pool.affine_select(out=one_head[:], in_=one_head[:], compare_op=ALU.is_ge, fill=0.0, base=0,
                                   pattern=[[P, DC], [-HD, H]], channel_multiplier=1).then_inc(consts_ready, 1)
                pool.wait_ge(consts_ready, 11)
                pool.affine_select(out=one_head[:], in_=one_head[:], compare_op=ALU.is_ge, fill=0.0, base=HD - 1,
                                   pattern=[[-P, DC], [HD, H]], channel_multiplier=-1).then_inc(consts_ready, 1)

            @block.sync
            def _(sp):
                for i, w in enumerate((wq, wk)):
                    sp.dma_start(w_qk[:, i], w.rearrange("(c p) n -> p c n", p=P)).then_inc(w_loaded, 16)
                sp.dma_start(w_v[:], wv.rearrange("(c p) n -> p c n", p=P)).then_inc(w_loaded, 16)
                xT_view = x_T.rearrange("(c p) t -> p c t", p=P)
                for j in range(2):
                    sp.dma_start(xT[:, j], xT_view[:, :, j * BLK:(j + 1) * BLK]).then_inc(xT_loaded[j], 16)
                for n in range(NB):
                    if n + 2 < NB:
                        sp.wait_ge(v_ready, 4 * (n + 1))
                        sp.dma_start(xT[:, n % 2], xT_view[:, :, (n + 2) * BLK:(n + 3) * BLK]).then_inc(xT_loaded[n % 2], 16)
                    sp.wait_ge(proj_split, U + U * (n + 1))
                    b, cols = n // NG, slice(n % NG * BLK, (n % NG + 1) * BLK)
                    for i in range(2):
                        for s in range(3):
                            sp.dma_start(split_dram[i, s, b * D:(b + 1) * D, cols].rearrange("(c p) t -> p c t", p=P),
                                         parts[:, s, DC * i:DC * (i + 1), n * BLK:(n + 1) * BLK]).then_inc(parts_stored, 16)
                    if n % NG == NG - 1:
                        sp.wait_ge(shift_ready, b + 1)
                        sp.dma_start(shift_dram[:, b * H:(b + 1) * H, :].rearrange("s h t -> h s t"),
                                     shift[:, :, b * N:(b + 1) * N]).then_inc(shift_stored, 16)
                sp.wait_ge(parts_stored, 16 * 6 * NB)
                sp.wait_ge(shift_stored, 16 * B)

            @block.tensor
            def _(pe):
                pe.sem_inc(norm_ready, 1)
                pe.wait_ge(w_loaded, 48)
                pe.wait_ge(consts_ready, 12)
                with pe.Fori(0, NB // 2) as i:
                    for j in range(2):
                        pe.wait_ge(xT_loaded[j], i * 16 + 16)
                        for u in range(U):
                            pe.wait_ge(proj_split, i * (2 * U) + (j * U + u + 1))
                            for c in range(DC):
                                last = nc.tensor.matmul(proj[:, u, :], w_qk[:, u // DC, c, (u % DC) * P:(u % DC + 1) * P],
                                                        xT[:, j, c, :], start=(c == 0), stop=(c == DC - 1))
                            last.then_inc(proj_ready, 1)
                        for t in range(4):
                            pe.wait_ge(v_read, i * 8 + (4 * j + 2 * (t // 2) + 2))
                            for c in range(DC):
                                last = nc.tensor.matmul(vps[:, t // 2, t % 2, :], xT[:, j, c, t * P:(t + 1) * P],
                                                        w_v[:, c, :], start=(c == 0), stop=(c == DC - 1))
                            last.then_inc(v_ready, 1)
                        pe.wait_ge(sq_ready, i * (2 * U) + (j + 1) * U)
                        pe.wait_ge(norm_read, i * 4 + (2 * j + 2))
                        for u in range(U):
                            last = nc.tensor.matmul(norm[0:H, u // DC, :], one_head[:, u % DC, :], sq[:, u, :],
                                                    start=(u % DC == 0), stop=(u % DC == DC - 1))
                        last.then_inc(norm_ready, 1)
                pe.wait_ge(top_ready, 1)
                nc.tensor.matmul(proj[0:1, 0, 0:H], top[:], ident[0:H, 0:H], start=True, stop=True).then_inc(top_row, 1)

            @block.scalar
            def _(act):
                act.sem_inc(v_read, 4)
                v_by_tile = v_all[:].rearrange("p (b h) t d -> p b h t d", b=B)
                with act.Fori(0, B) as b:
                    with act.Fori(0, NB // 2 // B) as i:
                        for j in range(2):
                            act.wait_ge(norm_ready, b * (NB // B) + i * 2 + (j + 1))
                            for u in range(U):
                                act.wait_ge(proj_ready, b * (U * NB // B) + i * (2 * U) + (j * U + u + 1))
                                nc.scalar.activation(sq[:, u, :], proj[:, u, :], ACT.Square).then_inc(sq_ready, 1)
                                nc.scalar.activation(parts[:, 0, u, bass.ds(b * N + i * (2 * BLK) + j * BLK, BLK)],
                                                     proj[:, u, :], ACT.Copy).then_inc(hi_ready, 1)
                            for t in range(4):
                                act.wait_ge(v_ready, b * (4 * NB // B) + i * 8 + (4 * j + 2 * (t // 2) + 2))
                                nc.scalar.activation(v_by_tile[:, bass.ds(b, 1), :, bass.ds(i * 8 + (4 * j + t), 1), :],
                                                     vps[:, t // 2, t % 2, :].rearrange("p (x h y d) -> p x h y d", x=1, y=1, h=H),
                                                     ACT.Copy).then_inc(v_read, 1)

            @block.vector
            def _(dve):
                dve.sem_inc(proj_split, U)
                dve.sem_inc(norm_read, 2)
                links_b = 2 * U * (NB // B) + 4
                with dve.Fori(0, B) as b:
                    with dve.Fori(0, NB // 2 // B) as i:
                        for j in range(2):
                            for u in range(U):
                                hi, mid, lo = (parts[:, s, u, bass.ds(b * N + i * (2 * BLK) + j * BLK, BLK)] for s in range(3))
                                step = b * links_b + i * (4 * U) + (2 * (j * U + u))
                                dve.wait_ge(hi_ready, b * (U * NB // B) + i * (2 * U) + (j * U + u + 1))
                                dve.wait_ge(proj_split, b * (U * NB // B) + i * (2 * U) + (j * U + u + U))
                                nc.vector.tensor_tensor(rest[:], proj[:, u, :], hi, ALU.subtract).then_inc(dve1, 1)
                                dve.wait_ge(dve1, step + 1)
                                nc.vector.tensor_copy(mid, rest[:]).then_inc(dve1, 1)
                                dve.wait_ge(dve1, step + 2)
                                nc.vector.tensor_tensor(lo, rest[:], mid, ALU.subtract).then_inc(proj_split, 1)
                            dve.wait_ge(norm_ready, b * (NB // B) + i * 2 + (j + 2))
                            nc.vector.tensor_copy(qn[:, bass.ds(i * (2 * BLK) + j * BLK, BLK)], norm[0:H, 0, :]).then_inc(norm_read, 1)
                            nc.vector.tensor_reduce(kn[:, bass.ds(i * 2 + j, 1)], norm[0:H, 1, :], AX.X, ALU.max).then_inc(norm_read, 1)
                    dve.wait_ge(norm_read, b * (2 * NB // B) + (2 * NB // B + 2))
                    nc.vector.tensor_reduce(kmax[:], kn[:], AX.X, ALU.max).then_inc(dve1, 1)
                    dve.wait_ge(dve1, b * links_b + (links_b - 3))
                    nc.vector.tensor_scalar(bound[:], qn[:], kmax[:], 0.125, ALU.add, ALU.mult).then_inc(dve1, 1)
                    dve.wait_ge(dve1, b * links_b + (links_b - 2))
                    nc.vector.tensor_copy(shift[:, 0, bass.ds(b * N, N)], bound[:]).then_inc(dve1, 1)
                    dve.wait_ge(dve1, b * links_b + (links_b - 1))
                    nc.vector.tensor_tensor(shift[:, 1, bass.ds(b * N, N)], bound[:], shift[:, 0, bass.ds(b * N, N)],
                                            ALU.subtract).then_inc(shift_ready, 1)
                    nc.vector.tensor_reduce(topb[:, bass.ds(b, 1)], bound[:], AX.X, ALU.max).then_inc(dve1, 1)
                    dve.wait_ge(dve1, b * links_b + links_b)
                nc.vector.tensor_reduce(top[:], topb[:], AX.X, ALU.max).then_inc(top_ready, 1)
                dve.wait_ge(top_row, 1)
                nc.vector.tensor_reduce(topr[:], proj[0:1, 0, 0:H], AX.X, ALU.max).then_inc(dve1, 1)
                dve.wait_ge(dve1, B * links_b + 1)
                nc.vector.tensor_scalar(flag[0:1, 0:1], topr[:], BOUND_MAX, None, ALU.is_gt).then_inc(flag_ready, 1)

        attn = sb(att, "attn", [P, 2, NT, HD])
        aq = [sb(att, f"aq{j}", [P, N], BF16) for j in range(2)]
        ak = [sb(att, f"ak{j}", [P, N], BF16) for j in range(2)]
        KR = 6 * HD
        AQ = ((0, 3), (1, 2), (2, 1))
        AK = ((0, 3), (3, 2), (5, 1))
        KS = KR + 2
        A_DMAS = 6 + 3

        def load_operands(sp, j, n, done):
            for s, (part, times) in enumerate(AQ):
                for r in range(times):
                    at = (0, 3, 5)[s] + r
                    sp.dma_start(aq[j][at * HD:(at + 1) * HD, :], split_dram[0, part, bass.ds(n * HD, HD), :]).then_inc(done, 16)
            for at, k in AK:
                sp.dma_start(ak[j][at * HD:(at + k) * HD, :], split_dram[1, 0:k, bass.ds(n * HD, HD), :]).then_inc(done, 16)

        g_loaded, g_link, g_scores, g_read = sem("g_loaded"), sem("g_link"), sem("g_scores"), sem("g_read")
        g_max, g_row, g_row_sb, g_stored, g_over = sem("g_max"), sem("g_row"), sem("g_row_sb"), sem("g_stored"), sem("g_over")
        with ExitStack() as st, nc.Block() as block:
            s_all = ps(st, "s_all", [P, N])
            m_ps = ps(st, "m_ps", [P, BLK])
            m_sb = sb(st, "m_sb", [P, NT])
            m_32 = sb(st, "m_32", [NT, P])
            m_row = sb(st, "m_row", [NT, 2, P], BF16)

            @block.sync
            def _(sp):
                sp.wait_ge(flag_ready, 1)
                loose = sp.value_load(flag[0:1, 0:1], min_val=0, max_val=1)
                with sp.If(loose > 0):
                    with sp.Fori(0, NH) as n:
                        load_operands(sp, 0, n, g_loaded)
                        sp.wait_ge(g_row_sb, n * 1 + 1)
                        for s in range(2):
                            sp.dma_start(shift_dram[s, bass.ds(n, 1), :].rearrange("o (t q) -> (o t) q", q=P),
                                         m_row[:, s, :]).then_inc(g_stored, 16)
                        sp.wait_ge(g_stored, n * 32 + 32)
                        sp.sem_inc(g_over, 1)

            @block.tensor
            def _(pe):
                pe.wait_ge(flag_ready, 1)
                loose = pe.value_load(flag[0:1, 0:1], min_val=0, max_val=1)
                with pe.If(loose > 0):
                    with pe.Fori(0, NH) as n:
                        pe.wait_ge(g_loaded, n * (16 * A_DMAS) + 16 * A_DMAS)
                        for i in range(NT):
                            pe.wait_ge(g_read, n * NT + i + 1)
                            for k in range(NG):
                                last = nc.tensor.matmul(s_all[:, k * BLK:(k + 1) * BLK], aq[0][0:KR, i * P:(i + 1) * P],
                                                        ak[0][0:KR, k * BLK:(k + 1) * BLK], start=True, stop=True)
                            last.then_inc(g_scores, 1)
                        pe.wait_ge(g_read, n * NT + NT + 1)
                        nc.tensor.matmul(m_ps[0:NT, 0:P], m_sb[:], ident[:], start=True, stop=True).then_inc(g_row, 1)

            @block.vector
            def _(dve):
                dve.wait_ge(flag_ready, 1)
                loose = dve.value_load(flag[0:1, 0:1], min_val=0, max_val=1)
                with dve.If(loose > 0):
                    dve.sem_inc(g_read, 1)
                    with dve.Fori(0, NH) as n:
                        for i in range(NT):
                            dve.wait_ge(g_scores, n * NT + i + 1)
                            nc.vector.tensor_reduce(m_sb[:, i:i + 1], s_all[:], AX.X, ALU.max).then_inc(g_read, 1)
                        dve.wait_ge(g_row, n * 1 + 1)
                        nc.vector.tensor_scalar(m_32[:], m_ps[0:NT, 0:P], 0.25, None, ALU.mult).then_inc(g_link, 1)
                        dve.wait_ge(g_link, n * 2 + 1)
                        nc.vector.tensor_copy(m_row[:, 0, :], m_32[:]).then_inc(g_link, 1)
                        dve.wait_ge(g_link, n * 2 + 2)
                        nc.vector.tensor_tensor(m_row[:, 1, :], m_32[:], m_row[:, 0, :], ALU.subtract).then_inc(g_row_sb, 1)

        a_loaded = [sem(f"a_loaded{j}") for j in range(2)]
        vh_ready, minus_ready, fills_ready = sem("vh_ready"), sem("minus_ready"), sem("fills_ready")
        scores_ready, exp_done, pv_done = sem("scores_ready"), sem("exp_done"), sem("pv_done")
        mask_done, out_copied, out_turned, out_read = sem("mask_done"), sem("out_copied"), sem("out_turned"), sem("out_read")
        x_summed, head_done, hidden_ready, dve3 = sem("x_summed"), sem("head_done"), sem("hidden_ready"), sem("dve3")
        x_loaded = sem("x_loaded")
        adding_head = sem("adding_head")
        attn_added, st_ready = sem("attn_added"), sem("st_ready")
        x_sb = sb(att, "x_sb", [P, TT, D])
        stats = sb(att, "stats", [P, TT, 6])
        with ExitStack() as st, nc.Block() as block:
            probs = sb(st, "probs", [P, P_RING, KSPAN])
            expq = sb(st, "expq", [P, X_RING, KSPAN])
            vh = [sb(st, f"vh{j}", [P, NT, 32]) for j in range(2)]
            only_sum = sb(st, "only_sum", [P, 32])
            zeros = sb(st, "zeros", [P, 32])
            hidden = sb(st, "hidden", [P, 4, P])
            o_sb = sb(st, "o_sb", [P, O_RING, BLK])
            num = sb(st, "num", [P, NT, HD + 1])
            sums = sb(st, "sums", [P, 2, NT + 3])
            den = sb(st, "den", [P, NT])
            inv = sb(st, "inv", [P, NT])
            scores = [ps(st, f"scores{j}", [P, KSPAN]) for j in range(S_RING)]
            o_ps = [ps(st, f"o_ps{j}", [P, BLK]) for j in range(O_RING)]
            pairs = NH // 2

            @block.sync
            def _(sp):
                def load_head(j, n):
                    load_operands(sp, j, n, a_loaded[j])
                    sp.dma_start(aq[j][KR:KS, :], shift_dram[:, bass.ds(n, 1), :].rearrange("s o t -> (s o) t")).then_inc(a_loaded[j], 16)

                for j in range(2):
                    load_head(j, j)
                sp.dma_start(x_sb[:], x_tok.rearrange("(t p) d -> p t d", p=P)).then_inc(x_loaded, 16)
                sp.wait_ge(blank_ready, 1)
                sp.wait_ge(consts_ready, 12)
                sp.dma_start(xe_dram.rearrange("(p s) c -> p s c", p=P),
                             blank[:, None, :].to_broadcast([P, E * CAP // P, ROW])).then_inc(xe_cleared, 16)
                with sp.Fori(1, pairs) as i:
                    for j in range(2):
                        sp.wait_ge(scores_ready, i * (2 * NS) + (j - 1) * NS)
                        load_head(j, i * 2 + j)
                sp.wait_ge(x_loaded, 16)

            @block.gpsimd
            def _(pool):
                for j in range(2):
                    pool.memset(vh[j][:], 0.0).then_inc(fills_ready, 1)
                    pool.memset(sums[:, j, :], 0.0).then_inc(fills_ready, 1)
                pool.memset(only_sum[:], 0.0).then_inc(fills_ready, 1)
                pool.memset(zeros[:], 0.0).then_inc(fills_ready, 1)
                pool.wait_ge(fills_ready, 6)
                pool.memset(only_sum[:, HD:HD + 1], 1.0).then_inc(fills_ready, 1)
                for j in range(2):
                    pool.memset(vh[j][:, :, HD:HD + 1], 1.0).then_inc(fills_ready, 1)
                pool.wait_ge(fills_ready, 9)
                pool.sem_inc(attn_added, 2)

                def fill_v(i, j):
                    pool.wait_ge(pv_done, i * (2 * NK) + (j * NK + NK + P_RING))
                    nc.gpsimd.tensor_copy(vh[j][:, :, 0:HD], v_all[:, bass.ds(i * 2 + j, 1), :, :].rearrange("p o t d -> p (o t) d")).then_inc(vh_ready, 1)

                def add_before(i, j, b):
                    pool.wait_ge(head_done, i * 2 + (j - 2 + 1 + 2))
                    pool.sem_inc(adding_head, 1)
                    cols = x_sb[:, b * NT:(b + 1) * NT, bass.ds(i * (2 * HD) + ((j - 2) * HD - b * D), HD)]
                    nc.gpsimd.tensor_tensor(cols, cols, attn[:, j], ALU.add).then_inc(attn_added, 1)

                for j in range(2):
                    fill_v(0, j)
                pool.wait_ge(x_loaded, 16)
                for b in range(B):
                    with pool.Fori(b * H // 2 + 1, min((b + 1) * H // 2 + 1, pairs)) as i:
                        for j in range(2):
                            fill_v(i, j)
                            add_before(i, j, b)
                for j in range(2):
                    add_before(pairs, j, B - 1)

            @block.tensor
            def _(pe):
                pe.wait_ge(fills_ready, 9)
                pe.wait_ge(minus_ready, 2)
                pe.sem_inc(pv_done, P_RING + 2 * NK)

                def fill(i, j, t):
                    kind, m = SEQ[t]
                    pe.wait_ge(exp_done, i * (2 * NS) + (j * NS + t + 1))
                    dst = scores[t % S_RING]
                    pieces = []
                    if kind == "K":
                        for g, k, at, w in KT[m]:
                            pieces.append((at, ak[j][0:KS, k * P:(k + 1) * P], aq[j], (g + 1) * BLK - w, w))
                    else:
                        for q, at, lo, w, _ in QT[m]:
                            while w:
                                step = min(w, BLK - at % BLK)
                                pieces.append((at, aq[j][0:KS, q * P:(q + 1) * P], ak[j], lo, step))
                                at, lo, w = at + step, lo + step, w - step
                    for at, still, moving, lo, w in pieces:
                        last = nc.tensor.matmul(dst[:, at:at + w], still, moving[0:KS, lo:lo + w], start=True, stop=True, skip_group_check=True)
                    last.then_inc(scores_ready, 1)

                def products(i, j, name):
                    unit, done = UNITS[name]
                    if name[0] == "D":
                        pe.wait_ge(mask_done, i * (2 * NG) + (j * NG + name[1] + 1))
                    else:
                        pe.wait_ge(exp_done, i * (2 * NS) + (j * NS + K_POS[unit[-1][0]] + 1 + S_RING))
                    for m, g, k, at, w in unit:
                        dst, r = o_ps[g % O_RING], k % 4
                        first = k < 4
                        if first and k == 0:
                            pe.wait_ge(out_read, i * (2 * NG) + (j * NG + g + 1))
                        last = nc.tensor.matmul(dst[32 * r:32 * r + 32, BLK - w:BLK], vh[j % 2][:, k, :], probs[:, m % P_RING, at:at + w],
                                                start=first, stop=True, skip_group_check=True)
                    if name == ("D", 0):
                        for m, g, k, at, w in unit[1:]:
                            nc.tensor.matmul(o_ps[0][32 * k:32 * k + 32, 0:BLK - w], zeros[:], probs[:, m % P_RING, at:at + BLK - w],
                                             start=False, stop=True, skip_group_check=True)
                    if name[0] == "D":
                        for r, lo, n in ((3, 3, 1), (2, 1, 2), (1, 0, 1)):
                            last = nc.tensor.matmul(o_ps[name[1] % O_RING][32 * r:32 * r + 32, lo * P:(lo + n) * P], only_sum[:],
                                                    hidden[:, lo:lo + n, :].rearrange("p r c -> p (r c)"),
                                                    start=False, stop=True, skip_group_check=True)
                    last.then_inc(pv_done, done)

                def turn(i, j, g):
                    pe.wait_ge(out_copied, i * (2 * NG) + (j * NG + g + 1))
                    for q in range(4):
                        last = nc.tensor.transpose(o_ps[g % O_RING][:, q * P:(q + 1) * P], o_sb[:, g % O_RING, q * P:(q + 1) * P], ident[:])
                    last.then_inc(out_turned, 1)

                def head(i, j, older):
                    pe.wait_ge(a_loaded[j], i * (16 * (A_DMAS + 1)) + 16 * (A_DMAS + 1))
                    pe.wait_ge(vh_ready, i * 2 + (j + 1))
                    for t in range(NS):
                        fill(i, j, t)
                        for back, work, which in AFTER[t]:
                            if older or not back:
                                (products if work == "unit" else turn)(i, j - back, which)

                head(0, 0, False)
                head(0, 1, True)
                with pe.Fori(1, pairs) as i:
                    for j in range(2):
                        head(i, j, True)
                for t in range(NS):
                    for back, work, which in AFTER[t]:
                        if back:
                            (products if work == "unit" else turn)(pairs, -back, which)

            @block.scalar
            def _(act):
                act.sem_inc(exp_done, S_RING)
                act.wait_ge(fills_ready, 9)
                with act.Fori(0, pairs) as i:
                    for j in range(2):
                        act.wait_ge(head_done, i * 2 + (j + 1))
                        for t, (kind, m) in enumerate(SEQ):
                            src = scores[t % S_RING]
                            act.wait_ge(scores_ready, i * (2 * NS) + (j * NS + t + 1))
                            if kind == "K":
                                act.wait_ge(pv_done, i * (2 * NK) + (j * NK + m + 1 + 2 * NK))
                                w = sum(u[3] for u in KT[m])
                                last = nc.scalar.activation(probs[:, m % P_RING, 0:w], src[:, 0:w], ACT.Exp, scale=HD ** -0.5)
                            elif m in MANY:
                                n = MANY.index(m)
                                act.wait_ge(x_summed, i * (2 * NM) + (j * NM + n + 1))
                                w = sum(u[3] for u in QT[m])
                                last = nc.scalar.activation(expq[:, n % X_RING, 0:w], src[:, 0:w], ACT.Exp, scale=HD ** -0.5)
                            else:
                                (q, at, lo, w, col), = QT[m]
                                last = nc.scalar.activation(src[:, at:at + w], src[:, at:at + w], ACT.Exp, scale=HD ** -0.5,
                                                            accum_out=sums[:, j, col:col + 1])
                            last.then_inc(exp_done, 1)

            @block.vector
            def _(dve):
                for j in range(2):
                    nc.vector.memset(ak[j][KR:KS, :], -1.0 / HD ** -0.5).then_inc(minus_ready, 1)
                dve.sem_inc(out_read, O_RING)
                dve.sem_inc(x_summed, X_RING)
                dve.sem_inc(head_done, 2)
                LINKS = 3

                def mask(i, j, g):
                    m = DIAG[g]
                    dve.wait_ge(pv_done, i * (2 * NK) + (j * NK + (DIAG[g - 1] + 1 if g else DIAG[-1] + 1 - NK) + P_RING + 2 * NK))
                    dve.wait_ge(exp_done, i * (2 * NS) + (j * NS + K_POS[m] + 1 + S_RING))
                    three = probs[:, m % P_RING, :].rearrange("p (r c) -> p r c", c=BLK)[:, :, 0:P]
                    fourth = probs[:, m % P_RING, D_AT[3]:D_AT[3] + P]
                    nc.vector.tensor_tensor(hidden[:, 0:3, :], three, after[:, 0:3, :], ALU.mult).then_inc(hidden_ready, 1)
                    nc.vector.tensor_tensor(hidden[:, 3, :], fourth, after[:, 3, :], ALU.mult).then_inc(hidden_ready, 1)
                    dve.wait_ge(hidden_ready, i * (4 * NG) + (j * (2 * NG) + 2 * g + 2))
                    nc.vector.tensor_tensor(three, three, upto[:, 0:3, :], ALU.mult)
                    nc.vector.tensor_tensor(fourth, fourth, upto[:, 3, :], ALU.mult).then_inc(mask_done, 1)

                def sum_up(i, j, n):
                    m = MANY[n]
                    if n == 0:
                        dve.wait_ge(head_done, i * 2 + (j + 1))
                    dve.wait_ge(exp_done, i * (2 * NS) + (j * NS + Q_POS[m] + 1 + S_RING))
                    for q, at, lo, w, col in QT[m]:
                        last = nc.vector.tensor_reduce(sums[:, j % 2, col:col + 1], expq[:, n % X_RING, at:at + w], AX.X, ALU.add)
                    last.then_inc(x_summed, 1)

                def take(i, j, g):
                    dve.wait_ge(pv_done, i * (2 * NK) + (j * NK + LAST[g] + 1 + P_RING + 2 * NK))
                    nc.vector.tensor_copy(o_sb[:, g % O_RING, :], o_ps[g % O_RING][:]).then_inc(out_copied, 1)

                def gather(i, j, g):
                    if g == 0:
                        dve.wait_ge(head_done, i * 2 + (j + 2))
                    dve.wait_ge(out_turned, i * (2 * NG) + (j * NG + g + 1))
                    turned = o_ps[g % O_RING][:].rearrange("p (q r d) -> p q d r", q=4, r=4)[:, :, 0:HD + 1, :]
                    nc.vector.tensor_reduce(num[:, 4 * g:4 * g + 4, :], turned, AX.X, ALU.add).then_inc(out_read, 1)

                def finish(i, j, _):
                    step = i * (2 * LINKS) + j * LINKS
                    dve.wait_ge(attn_added, i * 2 + (j + 1))
                    dve.wait_ge(exp_done, i * (2 * NS) + (j * NS + NS + S_RING))
                    dve.wait_ge(x_summed, i * (2 * NM) + (j * NM + NM + X_RING))
                    dve.wait_ge(out_read, i * (2 * NG) + (j * NG + NG + O_RING))
                    nc.vector.tensor_tensor(den[:], num[:, :, HD], sums[:, j % 2, 0:NT], ALU.add).then_inc(dve3, 1)
                    dve.wait_ge(dve3, step + 1)
                    nc.vector.tensor_tensor(den[:, 0:3], den[:, 0:3], sums[:, j % 2, NT:NT + 3], ALU.add).then_inc(dve3, 1)
                    dve.wait_ge(dve3, step + 2)
                    nc.vector.reciprocal(inv[:], den[:]).then_inc(dve3, 1)
                    dve.wait_ge(dve3, step + 3)
                    nc.vector.tensor_tensor(attn[:, j % 2], num[:, :, 0:HD],
                                            inv[:, :, None].to_broadcast([P, NT, HD]), ALU.mult).then_inc(head_done, 1)

                WORK = {"mask": mask, "sum": sum_up, "take": take, "gather": gather, "final": finish}

                def head(i, j, older):
                    for back, work, which in DVE_ORDER:
                        if older or not back:
                            WORK[work](i, j - back, which)

                head(0, 0, False)
                head(0, 1, True)
                first = pairs - NT // 4
                with dve.Fori(1, first) as i:
                    for j in range(2):
                        head(i, j, True)
                dve.wait_ge(attn_added, H + 2)
                with dve.Fori(first, pairs) as i:
                    for j in range(2):
                        head(i, j, True)
                        for k in range(2):
                            tile = bass.ds(i * 4 + (2 * j + k - 4 * first), 1)
                            nc.vector.bn_stats(stats[:, tile, :].rearrange("p o s -> p (o s)"),
                                               x_sb[:, tile, :].rearrange("p o d -> p (o d)")).then_inc(st_ready, 1)
                for back, work, which in DVE_ORDER:
                    if back:
                        WORK[work](pairs, -back, which)

        dve4 = sem("dve4")
        var_ready, std_ready, scale_found, h_by_dve, h_by_pool = sem("var_ready"), sem("std_ready"), sem("scale_found"), sem("h_by_dve"), sem("h_by_pool")
        hT_ready, hT_by_act, hT_by_dve, lg_ready, lg_copied, lgT_ready = sem("hT_ready"), sem("hT_by_act"), sem("hT_by_dve"), sem("lg_ready"), sem("lg_copied"), sem("lgT_ready")
        wr_loaded, logit_off, p_exp = sem("wr_loaded"), sem("logit_off"), sem("p_exp")
        iota_ready, keep_ready, prefix_ready = sem("iota_ready"), sem("keep_ready"), sem("prefix_ready")
        over_ready, cand_ready, cand_count, dve5 = sem("over_ready"), sem("cand_ready"), sem("cand_count"), sem("dve5")
        rows_ready, more_ready, rows_sent, acc_stored = sem("rows_ready"), sem("more_ready"), sem("rows_sent"), sem("acc_stored")
        GT = 4
        GR = TT // GT
        with ExitStack() as st, nc.Block() as block:
            mean = sb(st, "mean", [P, TT])
            var = sb(st, "var", [P, TT])
            std = sb(st, "std", [P, TT])
            rstd = sb(st, "rstd", [P, TT])
            tmp = sb(st, "tmp", [P, TT])
            h = sb(st, "h", [P, TT, ROW])
            hT = [sb(st, f"hT{j}", [P, DC, GT * P]) for j in range(2)]
            wr = sb(st, "wr", [P, DC, E])
            lg = [sb(st, f"lg{j}", [E, GT * P]) for j in range(2)]
            probs = sb(st, "rprobs", [P, TT, E])
            work = sb(st, "work", [P, TT, E])
            pick = [sb(st, f"pick{k}", [P, TT, E]) for k in range(TOPK)]
            keep = sb(st, "keep", [P, TT, E])
            wgt = sb(st, "wgt", [P, TOPK, TT])
            kept_w = sb(st, "kept_w", [P, TOPK, TT])
            red = sb(st, "red", [P, TT])
            cs = [sb(st, f"cs{k}", [P, TT, E]) for k in range(2)]
            tot = sb(st, "tot", [P, TT, E])
            pos = sb(st, "pos", [P, TT, E])
            over = sb(st, "over", [P, 1])
            big = [sb(st, f"big{j}", [1, E]) for j in range(3)]
            dest_f = sb(st, "dest_f", [P, TOPK, TT])
            dest = sb(st, "dest", [P, TOPK, TT], U32)
            ids = sb(st, "ids", [P, TT], I32)
            ebase_i = sb(st, "ebase_i", [P, E], I32)
            first_i = sb(st, "first_i", [P, E], I32)
            ebase = sb(st, "ebase", [P, E])
            first = sb(st, "first", [P, E])
            wm = sb(st, "wm", [P, TT, E])
            tau = sb(st, "tau", [P, E], I32)
            cand = sb(st, "cand", [P, E], I32)
            bit = sb(st, "bit", [P, E], I32)
            bit_f = sb(st, "bit_f", [P, E])
            cnt = sb(st, "cnt", [P, E])
            step_i = sb(st, "step_i", [P, E], I32)
            hT_ps = [ps(st, f"hT_ps{j}", [P, DC, GT * P]) for j in range(2)]
            lg_ps = [ps(st, f"lg_ps{j}", [P, GT * P]) for j in range(2)]
            lgT_ps = ps(st, "lgT_ps", [P, TT, E])
            pf_ps = ps(st, "pf_ps", [P, 2, TT, E])

            def wide(x):
                return x[:, :, None].to_broadcast([P, TT, E])

            def each(x):
                return x[:, None, :].to_broadcast([P, TT, E])

            @block.sync
            def _(sp):
                sp.dma_start(wr[:], wr_T.rearrange("(c p) e -> p c e", p=P)).then_inc(wr_loaded, 16)
                sp.wait_ge(h_by_dve, TT // 2)
                sp.wait_ge(h_by_pool, TT // 2)
                sp.dma_start(acc_dram.rearrange("(t p) d -> p t d", p=P), h[:, :, 0:D]).then_inc(acc_stored, 16)
                sp.wait_ge(wr_loaded, 16)
                sp.wait_ge(acc_stored, 16)

            @block.gpsimd
            def _(pool):
                pool.iota(ids[:], pattern=[[P, TT]], base=0, channel_multiplier=1).then_inc(iota_ready, 1)
                pool.iota(ebase_i[:], pattern=[[CAP, E]], base=0, channel_multiplier=0).then_inc(iota_ready, 1)
                pool.iota(first_i[:], pattern=[[-1, E]], base=E, channel_multiplier=0).then_inc(iota_ready, 1)
                pool.wait_ge(iota_ready, 3)
                nc.gpsimd.tensor_copy(ebase[:], ebase_i[:]).then_inc(iota_ready, 1)
                nc.gpsimd.tensor_copy(first[:], first_i[:]).then_inc(iota_ready, 1)
                nc.gpsimd.tensor_copy(h[:, :, COL_ID], ids[:]).then_inc(iota_ready, 1)
                pool.memset(h[:, :, COL_ID + 1:ROW], 0.0).then_inc(iota_ready, 1)
                pool.wait_ge(scale_found, 1)
                for g in range(GR):
                    for t in range(GT * g + GT // 2, GT * (g + 1)):
                        nc.gpsimd.tensor_scalar(h[:, t, 0:D], x_sb[:, t, :], mean[:, t:t + 1], rstd[:, t:t + 1], ALU.subtract, ALU.mult).then_inc(h_by_pool, 1)
                pool.wait_ge(xe_cleared, 16)
                pool.wait_ge(rows_ready, 1)
                for k in range(TOPK):
                    for t in range(TT):
                        pool.indirect_dma_start(out=xe_dram[:, :], out_offset=bass.IndirectOffsetOnAxis(ap=dest[:, k, t:t + 1], axis=0),
                                                in_=h[:, t, :], in_offset=None, bounds_check=E * CAP - 1,
                                                oob_is_err=False).then_inc(rows_sent, 16)
                pool.wait_ge(rows_sent, 16 * TOPK * TT)

            @block.scalar
            def _(act):
                act.wait_ge(var_ready, 1)
                nc.scalar.activation(std[:], var[:], ACT.Sqrt).then_inc(std_ready, 1)

                def copy_hT(g):
                    act.wait_ge(hT_ready, g + 1)
                    if g >= 2:
                        act.wait_ge(lg_ready, g - 1)
                    nc.scalar.activation(hT[g % 2][:, 0, :], hT_ps[g % 2][:, 0, :], ACT.Copy).then_inc(hT_by_act, 1)

                def copy_lg(g):
                    act.wait_ge(lg_ready, g + 1)
                    if g >= 2:
                        act.wait_ge(lgT_ready, g - 1)
                    nc.scalar.activation(lg[g % 2][:], lg_ps[g % 2][0:E, :], ACT.Copy).then_inc(lg_copied, 1)

                for g in range(GR + 1):
                    if g < GR:
                        copy_hT(g)
                    if g >= 1:
                        copy_lg(g - 1)
                act.wait_ge(logit_off, 1)
                nc.scalar.activation(probs[:], work[:], ACT.Exp).then_inc(p_exp, 1)

            def prefix_products():
                flat = keep[:].rearrange("p t e -> p (t e)")
                nc.tensor.matmul(pf_ps[:, 0].rearrange("p t e -> p (t e)"), before[:], flat, start=True, stop=True, skip_group_check=True)
                return nc.tensor.matmul(pf_ps[:, 1].rearrange("p t e -> p (t e)"), ones[:], flat, start=True, stop=True, skip_group_check=True)

            @block.tensor
            def _(pe):
                pe.wait_ge(wr_loaded, 16)

                def turn(g):
                    pe.wait_ge(h_by_dve, GT // 2 * (g + 1))
                    pe.wait_ge(h_by_pool, GT // 2 * (g + 1))
                    if g >= 2:
                        pe.wait_ge(hT_by_act, g - 1)
                        pe.wait_ge(hT_by_dve, g - 1)
                    for c in range(DC):
                        for t in range(GT):
                            last = nc.tensor.transpose(hT_ps[g % 2][:, c, t * P:(t + 1) * P], h[:, GT * g + t, c * P:(c + 1) * P], ident[:])
                    last.then_inc(hT_ready, 1)

                def logits(g):
                    pe.wait_ge(hT_by_act, g + 1)
                    pe.wait_ge(hT_by_dve, g + 1)
                    if g >= 2:
                        pe.wait_ge(lg_copied, g - 1)
                    for c in range(DC):
                        last = nc.tensor.matmul(lg_ps[g % 2][0:E, :], wr[:, c, :], hT[g % 2][:, c, :], start=(c == 0), stop=(c == DC - 1))
                    last.then_inc(lg_ready, 1)

                def turn_back(g):
                    pe.wait_ge(lg_copied, g + 1)
                    for t in range(GT):
                        last = nc.tensor.transpose(lgT_ps[:, GT * g + t, :], lg[g % 2][:, t * P:(t + 1) * P], ident[0:E, 0:E])
                    last.then_inc(lgT_ready, 1)

                for g in range(GR + 2):
                    if g < GR:
                        turn(g)
                    if 1 <= g <= GR:
                        logits(g - 1)
                    if g >= 2:
                        turn_back(g - 2)
                pe.wait_ge(keep_ready, 1)
                prefix_products().then_inc(prefix_ready, 1)
                pe.wait_ge(over_ready, 1)
                too_many = pe.value_load(flag[0:1, 1:2], min_val=0, max_val=1)
                with pe.If(too_many > 0):
                    with pe.Fori(0, TAU_BITS) as i:
                        pe.wait_ge(cand_ready, i * 1 + 1)
                        nc.tensor.matmul(lg_ps[0][:, 0:E], ones[:], cnt[:], start=True, stop=True).then_inc(cand_count, 1)
                    pe.wait_ge(cand_ready, TAU_BITS + 1)
                    nc.tensor.matmul(lg_ps[0][:, 0:E], ones[:], cnt[:], start=True, stop=True).then_inc(cand_count, 1)
                    for n in range(2):
                        pe.wait_ge(keep_ready, n + 2)
                        prefix_products().then_inc(prefix_ready, 1)

            @block.vector
            def _(dve):
                link = chain(dve, dve4)
                dve.wait_ge(attn_added, NH + 2)
                for t in range(NT, TT):
                    nc.vector.bn_stats(stats[:, t, :], x_sb[:, t, :]).then_inc(st_ready, 1)
                dve.wait_ge(st_ready, TT)
                layer_stats(nc, link, stats, mean[:], var[:], tmp[:]).then_inc(var_ready, 1)
                dve.wait_ge(std_ready, 1)
                inverse_root(nc, link, var[:], std[:], rstd[:], tmp[:]).then_inc(scale_found, 1)
                dve.wait_ge(scale_found, 1)

                def normalise(g):
                    for t in range(GT * g, GT * g + GT // 2):
                        nc.vector.tensor_scalar(h[:, t, 0:D], x_sb[:, t, :], mean[:, t:t + 1], rstd[:, t:t + 1], ALU.subtract, ALU.mult).then_inc(h_by_dve, 1)

                def copy_hT(g):
                    dve.wait_ge(hT_ready, g + 1)
                    if g >= 2:
                        dve.wait_ge(lg_ready, g - 1)
                    nc.vector.tensor_copy(hT[g % 2][:, 1, :], hT_ps[g % 2][:, 1, :]).then_inc(hT_by_dve, 1)

                for g in range(GR + 2):
                    if g < GR:
                        normalise(g)
                    if g >= 2:
                        copy_hT(g - 2)

                dve.wait_ge(lgT_ready, GR)
                link(nc.vector.tensor_reduce(red[:], lgT_ps[:], AX.X, ALU.max))
                nc.vector.tensor_tensor(work[:], lgT_ps[:], wide(red), ALU.subtract).then_inc(logit_off, 1)
                dve.wait_ge(iota_ready, 7)
                dve.wait_ge(p_exp, 1)
                link(nc.vector.tensor_reduce(red[:], probs[:], AX.X, ALU.add))
                link(nc.vector.reciprocal(tmp[:], red[:]))
                link(nc.vector.tensor_tensor(probs[:], probs[:], wide(tmp), ALU.mult))
                for k in range(TOPK):
                    link(nc.vector.tensor_reduce(wgt[:, k, :], probs[:], AX.X, ALU.max))
                    link(nc.vector.tensor_tensor(work[:], probs[:], wide(wgt[:, k, :]), ALU.is_equal))
                    link(nc.vector.tensor_tensor(work[:], work[:], each(first), ALU.mult))
                    link(nc.vector.tensor_reduce(red[:], work[:], AX.X, ALU.max))
                    nc.vector.tensor_scalar(h[:, :, COL_E + k], red[:], -1.0, float(E), ALU.mult, ALU.add)
                    link(nc.vector.tensor_tensor(pick[k][:], work[:], wide(red), ALU.is_equal))
                    if k == 0:
                        link(nc.vector.scalar_tensor_tensor(probs[:], pick[0][:], -4.0, probs[:], ALU.mult, ALU.add))

                nc.vector.tensor_tensor(keep[:], pick[0][:], pick[1][:], ALU.add).then_inc(keep_ready, 1)

                def weigh(link, w, of):
                    link(nc.vector.tensor_tensor(red[:], of[:, 0, :], of[:, 1, :], ALU.add))
                    link(nc.vector.tensor_scalar(red[:], red[:], MOE_EPS, None, ALU.max))
                    link(nc.vector.reciprocal(tmp[:], red[:]))
                    link(nc.vector.tensor_tensor(w[:], of[:], tmp[:, None, :].to_broadcast([P, TOPK, TT]), ALU.mult))

                weigh(link, wgt, wgt)
                weigh(link, kept_w, wgt)

                def prefixes(link, n):
                    dve.wait_ge(prefix_ready, n)
                    link(nc.vector.tensor_copy(tot[:], pf_ps[:, 1]))
                    a, s, src = 0, 1, tot
                    while s < TT:
                        nc.vector.tensor_copy(cs[a][:, 0:s, :], src[:, 0:s, :])
                        link(nc.vector.tensor_tensor(cs[a][:, s:, :], src[:, s:, :], src[:, :TT - s, :], ALU.add))
                        a, s, src = 1 - a, 2 * s, cs[a]
                    link(nc.vector.tensor_tensor(pos[:], src[:], tot[:], ALU.subtract))
                    link(nc.vector.tensor_tensor(pos[:], pos[:], pf_ps[:, 0], ALU.add))
                    return src

                upto_tile = prefixes(link, 1)
                link(nc.vector.tensor_reduce(over[:], upto_tile[:, TT - 1, :], AX.X, ALU.max))
                nc.vector.tensor_scalar(flag[0:1, 1:2], over[0:1, :], float(CAP), None, ALU.is_gt).then_inc(over_ready, 1)
                dve.wait_ge(over_ready, 1)
                too_many = dve.value_load(flag[0:1, 1:2], min_val=0, max_val=1)
                with dve.If(too_many > 0):
                    link5 = chain(dve, dve5)
                    link5(nc.vector.tensor_tensor(wm[:], pick[0][:], wide(wgt[:, 0, :]), ALU.mult))
                    link5(nc.vector.tensor_tensor(work[:], pick[1][:], wide(wgt[:, 1, :]), ALU.mult))
                    link5(nc.vector.tensor_tensor(wm[:], wm[:], work[:], ALU.add))
                    link5(nc.vector.scalar_tensor_tensor(wm[:], keep[:], -1.0, wm[:], ALU.add, ALU.add))
                    link5(nc.vector.memset(tau[:], 0))
                    link5(nc.vector.memset(bit[:], 1 << (TAU_BITS - 1)))
                    pre = link5.count()
                    with dve.Fori(0, TAU_BITS) as i:
                        at = i * 6 + pre
                        nc.vector.tensor_tensor(cand[:], tau[:], bit[:], ALU.bitwise_or).then_inc(dve5, 1)
                        dve.wait_ge(dve5, at + 1)
                        nc.vector.tensor_tensor(work[:], wm[:], each(cand.bitcast(FP32)), ALU.is_ge).then_inc(dve5, 1)
                        dve.wait_ge(dve5, at + 2)
                        nc.vector.tensor_reduce(cnt[:], work[:].rearrange("p t e -> p e t"), AX.X, ALU.add).then_inc(cand_ready, 1)
                        nc.vector.tensor_copy(bit_f[:], bit[:]).then_inc(dve5, 1)
                        dve.wait_ge(dve5, at + 3)
                        dve.wait_ge(cand_count, i * 1 + 1)
                        nc.vector.scalar_tensor_tensor(step_i[:], lg_ps[0][:, 0:E], float(CAP), bit_f[:], ALU.is_ge, ALU.mult).then_inc(dve5, 1)
                        dve.wait_ge(dve5, at + 4)
                        nc.vector.tensor_tensor(tau[:], tau[:], step_i[:], ALU.bitwise_or).then_inc(dve5, 1)
                        nc.vector.tensor_scalar(bit[:], bit[:], 1, None, ALU.logical_shift_right).then_inc(dve5, 1)
                        dve.wait_ge(dve5, at + 6)
                    link5.skip(6 * TAU_BITS)
                    link5(nc.vector.tensor_tensor(work[:], wm[:], each(tau.bitcast(FP32)), ALU.is_gt))
                    nc.vector.tensor_reduce(cnt[:], work[:].rearrange("p t e -> p e t"), AX.X, ALU.add).then_inc(cand_ready, 1)
                    nc.vector.tensor_tensor(keep[:], wm[:], each(tau.bitcast(FP32)), ALU.is_equal).then_inc(keep_ready, 1)
                    dve.wait_ge(cand_count, TAU_BITS + 1)
                    link5(nc.vector.tensor_copy(cnt[:], lg_ps[0][:, 0:E]))
                    prefixes(link5, 2)
                    link5(nc.vector.tensor_tensor(pos[:], pos[:], each(cnt), ALU.add))
                    link5(nc.vector.scalar_tensor_tensor(wm[:], pos[:], float(CAP), keep[:], ALU.is_lt, ALU.mult))
                    nc.vector.tensor_tensor(keep[:], work[:], wm[:], ALU.add).then_inc(keep_ready, 1)
                    prefixes(link5, 3)
                    link5(nc.vector.scalar_tensor_tensor(pos[:], pos[:], -float(E * CAP), keep[:], ALU.add, ALU.mult))
                    link5(nc.vector.tensor_scalar(pos[:], pos[:], float(E * CAP), None, ALU.add))
                    for k in range(TOPK):
                        link5(nc.vector.tensor_tensor(work[:], pick[k][:], keep[:], ALU.mult))
                        link5(nc.vector.tensor_reduce(red[:], work[:], AX.X, ALU.add))
                        link5(nc.vector.tensor_tensor(kept_w[:, k, :], wgt[:, k, :], red[:], ALU.mult))
                    weigh(link5, kept_w, kept_w)
                nc.vector.tensor_copy(h[:, :, COL_W:COL_W + TOPK], kept_w[:].rearrange("p k t -> p t k"))
                link(nc.vector.tensor_tensor(pos[:], pos[:], each(ebase), ALU.add))
                link(nc.vector.tensor_tensor(work[:], pick[0][:], pos[:], ALU.mult))
                nc.vector.tensor_reduce(dest_f[:, 0, :], work[:], AX.X, ALU.add)
                link(nc.vector.tensor_tensor(pos[:], pick[1][:], pos[:], ALU.mult))
                link(nc.vector.tensor_reduce(dest_f[:, 1, :], pos[:], AX.X, ALU.add))
                nc.vector.tensor_copy(dest[:], dest_f[:]).then_inc(rows_ready, 1)
                link(nc.vector.tensor_scalar(big[0][:], upto_tile[0:1, TT - 1, :], float(2 * GA), None, ALU.is_gt))
                link(nc.vector.tensor_copy(more[:], big[0][:]))
                a, s, src = 1, 1, big[0]
                while s < E:
                    nc.vector.tensor_copy(big[a][:, 0:s], src[:, 0:s])
                    link(nc.vector.tensor_tensor(big[a][:, s:], src[:, s:], src[:, :E - s], ALU.add))
                    a, s, src = 3 - a, 2 * s, big[a]
                nc.vector.tensor_tensor(more_before[:], src[:], big[0][:], ALU.subtract).then_inc(more_ready, 1)
                dve.wait_ge(more_ready, 1)
        att.close()

        r1_loaded, r2_loaded, xin_loaded = sem("r1_loaded"), sem("r2_loaded"), [sem(f"xin_loaded{j}") for j in range(2)]
        w1_hi, w1_split, w2_hi, w2_split = sem("w1_hi"), sem("w1_split"), sem("w2_hi"), sem("w2_split")
        xt_ready, xt_hi, xt_split = sem("xt_ready"), sem("xt_hi"), sem("xt_split")
        y_cleared, splitting = sem("y_cleared"), sem("splitting")
        up_ready, silu_done, mul_done, mid_hi, mid_split = sem("up_ready"), sem("silu_done"), sem("mul_done"), sem("mid_hi"), sem("mid_split")
        c_up_ready, c_silu_done, c_mul_done, c_mid_hi, c_mid_split = (sem("c_up_ready"), sem("c_silu_done"), sem("c_mul_done"),
                                                                      sem("c_mid_hi"), sem("c_mid_split"))
        c_xt_ready, c_xt_hi, c_xt_split, c_y_ready, c_y_done = (sem("c_xt_ready"), sem("c_xt_hi"), sem("c_xt_split"), sem("c_y_ready"),
                                                                sem("c_y_done"))
        y_ready, y_done, added, expert_over, adding, c_over, dve6 = sem("y_ready"), sem("y_done"), sem("added"), sem("expert_over"), sem("adding"), sem("c_over"), sem("dve6")
        with ExitStack() as st, nc.Block() as block:
            raw1 = sb(st, "raw1", [P, 2, DC, F])
            raw2 = sb(st, "raw2", [P, FC, D])
            wup = [sb(st, f"wup_{s}", [P, 2, DC, F], FP32R) for s in ("hi", "lo")]
            w2 = [sb(st, f"w2_{s}", [P, FC, D], FP32R) for s in ("hi", "lo")]
            xin = [sb(st, f"xin{j}", [P, CT, ROW]) for j in range(2)]
            xT = [sb(st, f"xeT_{s}", [P, DC, 2 * GA], FP32R) for s in ("hi", "lo")]
            xTC = [sb(st, f"xeTC_{s}", [P, DC, GC], FP32R) for s in ("hi", "lo")]
            gate = [sb(st, f"gate{j}", [P, GA]) for j in range(2)]
            mid = [sb(st, f"mid{j}", [P, GA]) for j in range(2)]
            mid2 = [sb(st, f"mid_{s}", [P, FC, GA], FP32R) for s in ("hi", "lo")]
            y = [sb(st, f"y{j}", [P, CT, D]) for j in range(2)]
            wt = sb(st, "wt", [P, 2, CT])
            wt2 = [sb(st, f"wt2_{j}", [P, CT]) for j in range(2)]
            row = [sb(st, f"row{j}", [P, CT], U32) for j in range(2)]
            e_now = sb(st, "e_now", [P, 1])
            xt_ps = [ps(st, f"xt_ps{j}", [P, GA]) for j in range(2)]
            up_ps = [ps(st, f"up_ps{j}", [P, 2, GA]) for j in range(2)]
            y_ps = ps(st, "y_ps", [P, 4, D])
            PAIRS = ((0, 0), (1, 0), (0, 1))

            def count(per, i, j, k):
                return i * (2 * per) + (j * per + k)

            def experts(eng, body):
                with eng.Fori(0, E // 2 - 1) as i:
                    for j in range(2):
                        body(i, j, True)
                body(E // 2 - 1, 0, True)
                body(E // 2 - 1, 1, False)

            def extra(eng, i, j):
                e = i * 2 + j
                return (eng.value_load(more[0:1, bass.ds(e, 1)], min_val=0, max_val=1),
                        eng.value_load(more_before[0:1, bass.ds(e, 1)], min_val=0, max_val=E))

            @block.sync
            def _(sp):
                def load_up(e):
                    one = bass.ds(e, 1)
                    for k, w in enumerate((wg_T, w1_T)):
                        sp.dma_start(raw1[:, k], w[one].rearrange("o (c p) f -> p (o c) f", p=P)).then_inc(r1_loaded, 16)

                def load_down(e):
                    sp.dma_start(raw2[:], w2_T[bass.ds(e, 1)].rearrange("o (c p) d -> p (o c) d", p=P)).then_inc(r2_loaded, 16)

                def load_rows(e, j):
                    sp.dma_start(xin[j][:], xe_dram[bass.ds(e * CAP, CAP), :].rearrange("(s p) c -> p s c", p=P)).then_inc(xin_loaded[j], 16)

                load_up(0)
                load_rows(0, 0)
                load_down(0)
                load_rows(1, 1)

                def body(i, j, prep):
                    if not prep:
                        return
                    e = i * 2 + (j + 1)
                    sp.wait_ge(w1_split, count(4, i, j, 4))
                    load_up(e)
                    sp.wait_ge(w2_split, count(1, i, j, 1))
                    load_down(e)
                    if not (isinstance(i, int) and j == 0):
                        sp.wait_ge(y_done, count(2 * NA, i, j, 3 * NA))
                        load_rows(i * 2 + (j + 2), j)

                experts(sp, body)

            @block.gpsimd
            def _(pool):
                pool.sem_inc(expert_over, 2)
                for j in range(2):
                    pool.memset(y[j][:], 0.0).then_inc(y_cleared, 1)

                def split_up(i, j):
                    pool.wait_ge(r1_loaded, count(32, i, j, 32))
                    pool.sem_inc(splitting, 1)
                    for k in range(2):
                        for c in range(DC):
                            nc.gpsimd.tensor_copy(wup[0][:, k, c, :], raw1[:, k, c, :]).then_inc(w1_hi, 1)

                def split_down(i, j):
                    pool.wait_ge(r2_loaded, count(16, i, j, 16))
                    pool.sem_inc(splitting, 1)
                    nc.gpsimd.tensor_copy(w2[0][:], raw2[:]).then_inc(w2_hi, 1)

                split_down(0, 0)

                def body(i, j, prep):
                    def add(tiles):
                        for t in tiles:
                            pool.indirect_dma_start(out=acc_dram[:, :], out_offset=bass.IndirectOffsetOnAxis(ap=row[j][:, t:t + 1], axis=0),
                                                    in_=y[j][:, t, :], in_offset=None, bounds_check=T - 1, oob_is_err=False,
                                                    compute_op=ALU.add).then_inc(added, 16)

                    pool.wait_ge(y_done, count(2 * NA, i, j, 2 * NA))
                    pool.sem_inc(adding, 1)
                    add(range(NA))
                    if prep:
                        pool.wait_ge(up_ready, count(2 * FC, i, j, 2 * FC))
                        split_up(i, j + 1)
                        pool.wait_ge(y_ready, count(2, i, j, 2))
                        split_down(i, j + 1)
                    pool.wait_ge(y_done, count(2 * NA, i, j, 3 * NA))
                    pool.sem_inc(adding, 1)
                    add(range(NA, CT))
                    pool.wait_ge(added, count(16 * CT, i, j, 16 * CT))
                    pool.sem_inc(expert_over, 1)

                experts(pool, body)

            @block.tensor
            def _(pe):
                def turn(j, g):
                    for c in range(DC):
                        for t in range(NA):
                            last = nc.tensor.transpose(xt_ps[c][:, t * P:(t + 1) * P], xin[j][:, g * NA + t, c * P:(c + 1) * P], ident[:])
                        last.then_inc(xt_ready, 1)

                def up(n, f, x, cols):
                    for k in range(2):
                        for c in range(DC):
                            for a, b in PAIRS:
                                last = nc.tensor.matmul(up_ps[n % 2][:, k, 0:cols.stop - cols.start], wup[a][:, k, c, f * P:(f + 1) * P], x[b][:, c, cols],
                                                        start=(c == 0 and (a, b) == PAIRS[0]), stop=(c == DC - 1 and (a, b) == PAIRS[-1]))
                    return last

                def down(f, nt):
                    for t in range(nt):
                        for a, b in PAIRS:
                            last = nc.tensor.matmul(y_ps[:, t, :], mid2[a][:, f, t * P:(t + 1) * P], w2[b][:, f, :],
                                                    start=(f == 0 and t % 2 == 0 and (a, b) == PAIRS[0]),
                                                    stop=(f == FC - 1 and (a, b) == PAIRS[-1]), skip_group_check=True)
                    return last

                pe.wait_ge(xin_loaded[0], 16)
                for g in range(2):
                    if g == 1:
                        pe.wait_ge(xt_split, DC)
                    turn(0, g)

                def body(i, j, prep):
                    pe.wait_ge(xt_split, count(4, i, j, 4))
                    pe.wait_ge(w1_split, count(4, i, j, 4))
                    for g in range(2):
                        if g == 1:
                            has, before_it = extra(pe, i, j)
                            with pe.If(has > 0):
                                pe.wait_ge(mul_done, count(2 * FC, i, j, FC + 2))
                                for c in range(DC):
                                    for t in range(NC):
                                        last = nc.tensor.transpose(xt_ps[c][:, t * P:(t + 1) * P], xin[j][:, 2 * NA + t, c * P:(c + 1) * P], ident[:])
                                    last.then_inc(c_xt_ready, 1)
                                pe.wait_ge(c_xt_split, before_it * DC + DC)
                                for f in range(FC):
                                    if f >= 2:
                                        pe.wait_ge(c_mul_done, before_it * FC + (f - 1))
                                    up(f, f, xTC, slice(0, GC)).then_inc(c_up_ready, 1)
                                pe.wait_ge(y_done, count(2 * NA, i, j, 2 * NA))
                                for f in range(FC):
                                    pe.wait_ge(c_mid_split, before_it * FC + (f + 1))
                                    last = down(f, NC)
                                last.then_inc(c_y_ready, 1)
                                pe.wait_ge(c_y_done, before_it * NC + NC)
                                pe.sem_inc(c_over, 1)
                        for f in range(FC):
                            pe.wait_ge(mul_done, count(2 * FC, i, j, g * FC + f + 1))
                            up(f, f, xT, slice(g * GA, (g + 1) * GA)).then_inc(up_ready, 1)
                        if g == 0:
                            pe.wait_ge(w2_split, count(1, i, j, 1))
                        pe.wait_ge(y_done, count(2 * NA, i, j, (g + 1) * NA))
                        for f in range(FC):
                            if g == 1 and prep and f == 0:
                                pe.wait_ge(xin_loaded[1 - j], i * 16 + 16 * (j + 1))
                                turn(1 - j, 0)
                            if g == 1 and prep and f == FC // 2:
                                pe.wait_ge(xt_split, count(2 * DC, i, j, 3 * DC))
                                turn(1 - j, 1)
                            pe.wait_ge(mid_split, count(2 * FC, i, j, g * FC + f + 3))
                            last = down(f, NA)
                        last.then_inc(y_ready, 1)

                experts(pe, body)

            @block.scalar
            def _(act):
                def turn_hi(i, j):
                    for g in range(2):
                        for c in range(DC):
                            act.wait_ge(xt_ready, count(4, i, j, g * DC + c + 1))
                            nc.scalar.activation(xT[0][:, c, g * GA:(g + 1) * GA], xt_ps[c][:], ACT.Copy).then_inc(xt_hi, 1)

                act.wait_ge(r1_loaded, 32)
                for k in range(2):
                    for c in range(DC):
                        nc.scalar.activation(wup[0][:, k, c, :], raw1[:, k, c, :], ACT.Copy).then_inc(w1_hi, 1)
                turn_hi(0, 0)

                def body(i, j, prep):
                    for g in range(2):
                        if g == 1:
                            has, before_it = extra(act, i, j)
                            with act.If(has > 0):
                                for c in range(DC):
                                    act.wait_ge(c_xt_ready, before_it * DC + (c + 1))
                                    nc.scalar.activation(xTC[0][:, c, :], xt_ps[c][:, 0:GC], ACT.Copy).then_inc(c_xt_hi, 1)
                                for f in range(FC + 1):
                                    if f < FC:
                                        act.wait_ge(c_up_ready, before_it * FC + (f + 1))
                                        if f >= 2:
                                            act.wait_ge(c_mul_done, before_it * FC + (f - 1))
                                        nc.scalar.activation(gate[f % 2][:, 0:GC], up_ps[f % 2][:, 0, 0:GC], ACT.Silu).then_inc(c_silu_done, 1)
                                    if f >= 1:
                                        act.wait_ge(c_mul_done, before_it * FC + f)
                                        nc.scalar.activation(mid2[0][:, f - 1, 0:GC], mid[(f - 1) % 2][:, 0:GC], ACT.Copy).then_inc(c_mid_hi, 1)
                        for f in range(FC + 1):
                            if f < FC:
                                act.wait_ge(up_ready, count(2 * FC, i, j, g * FC + f + 1))
                                act.wait_ge(mul_done, count(2 * FC, i, j, g * FC + f + 1))
                                nc.scalar.activation(gate[f % 2][:], up_ps[f % 2][:, 0, :], ACT.Silu).then_inc(silu_done, 1)
                            if f >= 1:
                                act.wait_ge(mul_done, count(2 * FC, i, j, g * FC + f + 2))
                                nc.scalar.activation(mid2[0][:, f - 1, :], mid[(f - 1) % 2][:], ACT.Copy).then_inc(mid_hi, 1)
                    if prep:
                        turn_hi(i, j + 1)

                experts(act, body)

            @block.vector
            def _(dve):
                dve.sem_inc(mul_done, 2)
                dve.sem_inc(mid_split, 2)
                dve.sem_inc(y_done, NA)
                nc.vector.memset(e_now[:], 0.0).then_inc(dve6, 1)
                LINKS = 4

                def split_up(i, j):
                    for n in range(2 * DC):
                        k, c = n // DC, n % DC
                        dve.wait_ge(w1_hi, count(4, i, j, n + 1))
                        nc.vector.tensor_tensor(wup[1][:, k, c, :], raw1[:, k, c, :], wup[0][:, k, c, :].bitcast(FP32), ALU.subtract).then_inc(w1_split, 1)

                def split_down(i, j):
                    dve.wait_ge(w2_hi, count(1, i, j, 1))
                    nc.vector.tensor_tensor(w2[1][:], raw2[:], w2[0][:].bitcast(FP32), ALU.subtract).then_inc(w2_split, 1)

                def turn_lo(i, j):
                    for g in range(2):
                        for c in range(DC):
                            dve.wait_ge(xt_hi, count(4, i, j, g * DC + c + 1))
                            cols = slice(g * GA, (g + 1) * GA)
                            nc.vector.tensor_tensor(xT[1][:, c, cols], xt_ps[c][:], xT[0][:, c, cols].bitcast(FP32), ALU.subtract).then_inc(xt_split, 1)

                def lo_of_mid(f, n):
                    return nc.vector.tensor_tensor(mid2[1][:, f, 0:n], mid[f % 2][:, 0:n], mid2[0][:, f, 0:n].bitcast(FP32), ALU.subtract)

                split_up(0, 0)
                turn_lo(0, 0)
                split_down(0, 0)
                dve.wait_ge(y_cleared, 2)

                def body(i, j, prep):
                    step = count(LINKS, i, j, 1)
                    dve.wait_ge(xin_loaded[j], i * 16 + 16)
                    dve.wait_ge(dve6, step)
                    dve.wait_ge(expert_over, i * 2 + (j + 1))
                    for k in range(TOPK):
                        nc.vector.scalar_tensor_tensor(wt[:, k, :], xin[j][:, :, COL_E + k], e_now[:], xin[j][:, :, COL_W + k],
                                                       ALU.is_equal, ALU.mult).then_inc(dve6, 1)
                    nc.vector.tensor_copy(row[j][:], xin[j][:, :, COL_ID])
                    dve.wait_ge(dve6, step + 2)
                    nc.vector.tensor_tensor(wt2[j][:], wt[:, 0, :], wt[:, 1, :], ALU.add).then_inc(dve6, 1)
                    nc.vector.tensor_scalar(e_now[:], e_now[:], 1.0, None, ALU.add).then_inc(dve6, 1)
                    for g in range(2):
                        if g == 1:
                            has, before_it = extra(dve, i, j)
                            with dve.If(has > 0):
                                for c in range(DC):
                                    dve.wait_ge(c_xt_hi, before_it * DC + (c + 1))
                                    nc.vector.tensor_tensor(xTC[1][:, c, :], xt_ps[c][:, 0:GC], xTC[0][:, c, :].bitcast(FP32),
                                                            ALU.subtract).then_inc(c_xt_split, 1)
                                for f in range(FC + 1):
                                    if f < FC:
                                        dve.wait_ge(c_silu_done, before_it * FC + (f + 1))
                                        if f >= 2:
                                            dve.wait_ge(c_mid_split, before_it * FC + (f - 1))
                                        nc.vector.tensor_tensor(mid[f % 2][:, 0:GC], up_ps[f % 2][:, 1, 0:GC], gate[f % 2][:, 0:GC],
                                                                ALU.mult).then_inc(c_mul_done, 1)
                                    if f >= 1:
                                        dve.wait_ge(c_mid_hi, before_it * FC + f)
                                        lo_of_mid(f - 1, GC).then_inc(c_mid_split, 1)
                                dve.wait_ge(c_y_ready, before_it * 1 + 1)
                                for t in range(NC):
                                    nc.vector.tensor_scalar(y[j][:, 2 * NA + t, :], y_ps[:, t, :], wt2[j][:, 2 * NA + t:2 * NA + t + 1], None,
                                                            ALU.mult).then_inc(c_y_done, 1)
                        for f in range(FC + 1):
                            if f < FC:
                                dve.wait_ge(silu_done, count(2 * FC, i, j, g * FC + f + 1))
                                dve.wait_ge(mid_split, count(2 * FC, i, j, g * FC + f + 1))
                                nc.vector.tensor_tensor(mid[f % 2][:], up_ps[f % 2][:, 1, :], gate[f % 2][:], ALU.mult).then_inc(mul_done, 1)
                            if f >= 1:
                                dve.wait_ge(mid_hi, count(2 * FC, i, j, g * FC + f))
                                lo_of_mid(f - 1, GA).then_inc(mid_split, 1)
                        if g == 1 and prep:
                            turn_lo(i, j + 1)
                            split_up(i, j + 1)
                        dve.wait_ge(y_ready, count(2, i, j, g + 1))
                        for t in range(NA):
                            last = nc.vector.tensor_scalar(y[j][:, g * NA + t, :], y_ps[:, t, :], wt2[j][:, g * NA + t:g * NA + t + 1], None, ALU.mult)
                            last.then_inc(y_done, 1)
                        if g == 1 and prep:
                            split_down(i, j + 1)

                experts(dve, body)

        CH = 8
        NCH = TT // CH
        acc_loaded = [sem(f"acc_loaded{c}") for c in range(NCH)]
        st2_ready, var2_ready, std2_ready, scale_ready = sem("st2_ready"), sem("var2_ready"), sem("std2_ready"), sem("scale_ready")
        dve7, act_normed, dve_normed, stored = sem("dve7"), sem("act_normed"), sem("dve_normed"), sem("stored")
        with ExitStack() as st, nc.Block() as block:
            a = sb(st, "a", [P, TT, D])
            stats = sb(st, "stats2", [P, TT, 6])
            mean = sb(st, "mean2", [P, TT])
            var = sb(st, "var2", [P, TT])
            std = sb(st, "std2", [P, TT])
            rstd = sb(st, "rstd2", [P, TT])
            nbias = sb(st, "nbias2", [P, TT])
            tmp = sb(st, "tmp2", [P, TT])
            acc_view = acc_dram.rearrange("(t p) d -> p t d", p=P)
            out_view = out.rearrange("(t p) d -> p t d", p=P)
            BY_ACT = 5

            def part(c):
                return slice(c * CH, (c + 1) * CH)

            @block.sync
            def _(sp):
                for c in range(NCH):
                    sp.dma_start(a[:, part(c), :], acc_view[:, part(c), :]).then_inc(acc_loaded[c], 16)
                for c in range(NCH):
                    sp.wait_ge(act_normed, (c + 1) * BY_ACT)
                    sp.wait_ge(dve_normed, (c + 1) * (CH - BY_ACT))
                    sp.dma_start(out_view[:, part(c), :], a[:, part(c), :]).then_inc(stored, 16)
                sp.wait_ge(stored, 16 * NCH)

            @block.scalar
            def _(act):
                def root(c):
                    act.wait_ge(var2_ready, c + 1)
                    nc.scalar.activation(std[:, part(c)], var[:, part(c)], ACT.Sqrt).then_inc(std2_ready, 1)

                def normalise(c):
                    act.wait_ge(scale_ready, c + 1)
                    for t in range(c * CH, c * CH + BY_ACT):
                        nc.scalar.activation(a[:, t, :], a[:, t, :], ACT.Identity, bias=nbias[:, t:t + 1], scale=rstd[:, t:t + 1]).then_inc(act_normed, 1)

                for c in range(NCH + 1):
                    if c < NCH:
                        root(c)
                    if c >= 1:
                        normalise(c - 1)

            @block.vector
            def _(dve):
                link = chain(dve, dve7)

                def measure(c):
                    dve.wait_ge(acc_loaded[c], 16)
                    for t in range(c * CH, (c + 1) * CH):
                        nc.vector.bn_stats(stats[:, t, :], a[:, t, :]).then_inc(st2_ready, 1)
                    dve.wait_ge(st2_ready, (c + 1) * CH)
                    layer_stats(nc, link, stats[:, part(c), :], mean[:, part(c)], var[:, part(c)], tmp[:, part(c)]).then_inc(var2_ready, 1)

                def normalise(c):
                    dve.wait_ge(std2_ready, c + 1)
                    link(inverse_root(nc, link, var[:, part(c)], std[:, part(c)], rstd[:, part(c)], tmp[:, part(c)]))
                    nc.vector.scalar_tensor_tensor(nbias[:, part(c)], mean[:, part(c)], -1.0, rstd[:, part(c)], ALU.mult, ALU.mult).then_inc(scale_ready, 1)
                    for t in range(c * CH + BY_ACT, (c + 1) * CH):
                        nc.vector.tensor_scalar(a[:, t, :], a[:, t, :], mean[:, t:t + 1], rstd[:, t:t + 1], ALU.subtract, ALU.mult).then_inc(dve_normed, 1)

                for c in range(NCH + 1):
                    if c < NCH:
                        measure(c)
                    if c >= 1:
                        normalise(c - 1)


def kernel(L0_attn_content, L0_attn_Wq, L0_attn_Wk, L0_attn_Wv, L0_ffn_router_weight, L0_ffn_ff_pre_act_weight,
           L0_ffn_gate_weight, L0_ffn_ff_post_act_weight):
    import numpy as np
    import concourse.bacc as bacc
    from concourse.bass_utils import run_bass_kernel_spmd

    x = np.asarray(L0_attn_content).reshape(T, D)
    arrays = {
        "x_tok": x,
        "x_T": x.T,
        "wq": np.asarray(L0_attn_Wq),
        "wk": np.asarray(L0_attn_Wk),
        "wv": np.asarray(L0_attn_Wv),
        "wr_T": np.asarray(L0_ffn_router_weight).T,
        "w1_T": np.asarray(L0_ffn_ff_pre_act_weight).transpose(0, 2, 1),
        "wg_T": np.asarray(L0_ffn_gate_weight).transpose(0, 2, 1),
        "w2_T": np.asarray(L0_ffn_ff_post_act_weight).transpose(0, 2, 1),
    }
    arrays = {name: np.ascontiguousarray(a) for name, a in arrays.items()}
    nc = bacc.Bacc("TRN2", target_bir_lowering=False, num_devices=1)
    args = [nc.dram_tensor(name, a.shape, mybir.dt.from_np(a.dtype), kind="ExternalInput").ap() for name, a in arrays.items()]
    out = nc.dram_tensor("out", (T, D), FP32, kind="ExternalOutput").ap()
    program(nc, *args, out)
    result = run_bass_kernel_spmd(nc, [arrays], core_ids=[0])
    return result.results[0]["out"].reshape(B, N, D)
```

```python
import concourse.bass as bass
from concourse import mybir
from contextlib import ExitStack

FP32 = mybir.dt.float32
BF16 = mybir.dt.bfloat16
FP32R = mybir.dt.float32r
I32 = mybir.dt.int32
U32 = mybir.dt.uint32
ALU = mybir.AluOpType
ACT = mybir.ActivationFunctionType
AX = mybir.AxisListType

P = 128
B, N, D = 2, 2048, 256
H, HD = 16, 16
T = B * N
NH = B * H
DC = D // P
TT = T // P
NT = N // P
BLK = 512
E, TOPK, F = 8, 2, 1024
FC = F // P
CAP = 1280
CT = CAP // P
GA = 512
GC = CAP - 2 * GA
NA, NC = GA // P, GC // P
ROW = 264
COL_W, COL_E, COL_ID = 256, 258, 260
LN_EPS = 1e-5
MOE_EPS = 1.1920929e-07
TAU_BITS = 30
BOUND_MAX = 30.0

KSPAN = 3 * BLK
NG = N // BLK
D_AT = (0, 512, 1024, 896)


def key_tiles():
    diag = [[(g, 4 * g + r, D_AT[r], BLK - P * r) for r in range(4)] for g in range(NG)]
    full = [(g, j) for g in range(NG) for j in range(4 * g)]
    off = [[(g, j, BLK * n, BLK) for n, (g, j) in enumerate(full[3 * f:3 * f + 3])] for f in range(8)]
    return [diag[0], off[0], off[1], diag[1], off[2], off[3], diag[2], off[4], off[5], diag[3], off[6], off[7]]


def query_tiles():
    pieces = []
    for i in range(NT - 1):
        lo, left = P * (i + 1), N - P * (i + 1)
        if left > KSPAN:
            pieces.append((i, lo, KSPAN, i))
            pieces.append((i, lo + KSPAN, left - KSPAN, NT + i))
        else:
            pieces.append((i, lo, left, i))
    tiles = []
    for i, lo, w, col in sorted(pieces, key=lambda x: -x[2]):
        for t in tiles:
            if sum(x[3] for x in t) + w <= KSPAN:
                t.append((i, sum(x[3] for x in t), lo, w, col))
                break
        else:
            tiles.append([(i, 0, lo, w, col)])
    return tiles


KT = key_tiles()
QT = query_tiles()
NK, NQ = len(KT), len(QT)
ORDER = "KQKKKQKQKQQKQKQKKKQQKQ"
assert ORDER.count("K") == NK and ORDER.count("Q") == NQ
MANY = [n for n in range(NQ) if len(QT[n]) > 1]
Q_ORDER = MANY + [n for n in range(NQ) if n not in MANY]
SEQ = []
for c in ORDER:
    n = sum(1 for k, _ in SEQ if k == c)
    SEQ.append((c, n if c == "K" else Q_ORDER[n]))
NS = len(SEQ)
NM = len(MANY)
K_POS = [n for n, (k, _) in enumerate(SEQ) if k == "K"]
Q_POS = {m: n for n, (k, m) in enumerate(SEQ) if k == "Q"}
DIAG = [0, 3, 6, 9]
LAST = [max(m for m in range(NK) if any(u[0] == g for u in KT[m])) for g in range(NG)]
S_RING, P_RING, O_RING, X_RING = 2, 4, 2, 2


UNIT_AT = {3: ("D", 0), 6: ("G", 0), 8: ("G", 1), 10: ("D", 1), 13: ("G", 2), 15: ("D", 2),
           18: ("G", 3), 20: ("G", 4), 21: ("D", 3), 23: ("G", 5)}
TURN_AT = {5: 0, 14: 1, 17: 2, 26: 3}


def product_units():
    diag = {("D", g): [(DIAG[g],) + u for u in KT[DIAG[g]]] for g in range(NG)}
    off = [(m,) + u for m in range(NK) if m not in DIAG for u in KT[m]]
    groups = {("G", n): off[4 * n:4 * n + 4] for n in range(len(off) // 4)}
    units, over, left = {}, 0, {m: len(KT[m]) for m in range(NK)}
    for t in sorted(UNIT_AT):
        name = UNIT_AT[t]
        unit = (diag | groups)[name]
        for u in unit:
            left[u[0]] -= 1
        done = 0
        while over < NK and left[over] == 0:
            over, done = over + 1, done + 1
        assert done
        units[name] = (unit, done)
    assert over == NK and len(units) == NG + len(groups)
    return units


UNITS = product_units()
AFTER = [[(back, work, what[t + back * NS]) for back in (1, 0) for work, what in (("unit", UNIT_AT), ("turn", TURN_AT)) if t + back * NS in what]
         for t in range(NS)]
DVE_ORDER = ((0, "mask", 0), (1, "take", 3), (0, "sum", 0), (0, "take", 0), (1, "gather", 3), (1, "final", 0),
             (0, "mask", 1), (0, "gather", 0), (0, "sum", 1), (0, "sum", 2), (0, "sum", 3), (0, "take", 1),
             (0, "sum", 4), (0, "mask", 2), (0, "sum", 5), (0, "gather", 1), (0, "take", 2), (0, "mask", 3),
             (0, "gather", 2))


def chain(eng, semaphore):
    count = [0]

    def link(instruction):
        count[0] += 1
        instruction.then_inc(semaphore, 1)
        eng.wait_ge(semaphore, count[0])

    def skip(n):
        count[0] += n

    link.count, link.skip = lambda: count[0], skip
    return link


def layer_stats(nc, link, stats, mean, var, tmp):
    link(nc.vector.tensor_tensor(mean, stats[:, :, 1], stats[:, :, 4], ALU.add))
    link(nc.vector.tensor_scalar(mean, mean, 0.5, None, ALU.mult))
    link(nc.vector.tensor_tensor(tmp, stats[:, :, 1], mean, ALU.subtract))
    link(nc.vector.tensor_tensor(tmp, tmp, tmp, ALU.mult))
    link(nc.vector.tensor_tensor(var, stats[:, :, 2], stats[:, :, 5], ALU.add))
    link(nc.vector.tensor_scalar(var, var, 1.0 / D, LN_EPS, ALU.mult, ALU.add))
    return nc.vector.tensor_tensor(var, var, tmp, ALU.add)


def inverse_root(nc, link, var, std, rstd, tmp):
    link(nc.vector.reciprocal(rstd, std))
    link(nc.vector.tensor_tensor(tmp, rstd, rstd, ALU.mult))
    link(nc.vector.tensor_tensor(tmp, tmp, var, ALU.mult))
    link(nc.vector.tensor_scalar(tmp, tmp, -0.5, 1.5, ALU.mult, ALU.add))
    return nc.vector.tensor_tensor(rstd, rstd, tmp, ALU.mult)


def program(nc, x_tok, x_T, wq, wk, wv, wr_T, w1_T, wg_T, w2_T, out):
    ctx = ExitStack()
    with ctx:
        def sem(name):
            return ctx.enter_context(nc.semaphore(name))

        def sb(stack, name, shape, dt=FP32):
            return stack.enter_context(nc.sbuf_tensor(name, shape, dt))

        def ps(stack, name, shape, dt=FP32):
            return stack.enter_context(nc.psum_tensor(name, shape, dt))

        split_dram = nc.dram_tensor("split_dram", (2, 3, NH * HD, N), BF16).ap()
        shift_dram = nc.dram_tensor("shift_dram", (2, NH, N), BF16).ap()
        xe_dram = nc.dram_tensor("xe_dram", (E * CAP, ROW), FP32).ap()
        acc_dram = nc.dram_tensor("acc_dram", (T, D), FP32).ap()

        ident = sb(ctx, "ident", [P, P])
        ones = sb(ctx, "ones", [P, P])
        before = sb(ctx, "before", [P, P])
        upto = sb(ctx, "upto", [P, 4, P])
        after = sb(ctx, "after", [P, 4, P])
        one_head = sb(ctx, "one_head", [P, DC, H], BF16)
        flag = sb(ctx, "flag", [1, 4], I32)
        raw1 = sb(ctx, "raw1", [P, 2, DC, F])
        r1_loaded, r2_loaded = sem("r1_loaded"), sem("r2_loaded")
        more = sb(ctx, "more", [1, E], I32)
        more_before = sb(ctx, "more_before", [1, E], I32)
        consts_ready = sem("consts_ready")

        def load_up(sp, e):
            one = bass.ds(e, 1)
            for k, w in enumerate((wg_T, w1_T)):
                sp.dma_start(raw1[:, k], w[one].rearrange("o (c p) f -> p (o c) f", p=P)).then_inc(r1_loaded, 16)

        att = ctx.enter_context(ExitStack())
        v_all = sb(att, "v_all", [P, NH, NT, HD])
        blank = sb(att, "blank", [P, ROW])

        NB = T // BLK
        U = 2 * DC
        xT_loaded = [sem(f"xT_loaded{j}") for j in range(2)]
        w_loaded = sem("w_loaded")
        proj_ready, hi_ready, proj_read, mid_ready, proj_split = (sem("proj_ready"), sem("hi_ready"), sem("proj_read"), sem("mid_ready"),
                                                                 sem("proj_split"))
        sq_ready, norm_ready, norm_read = sem("sq_ready"), sem("norm_ready"), sem("norm_read")
        v_ready, v_read = sem("v_ready"), sem("v_read")
        w_hi, w_split, x_hi, x_split = sem("w_hi"), sem("w_split"), sem("x_hi"), sem("x_split")
        parts_stored = [sem(f"parts_stored{n}") for n in range(NB // B)]
        dve1, shift_ready, shift_stored = sem("dve1"), sem("shift_ready"), sem("shift_stored")
        top_ready, top_row, flag_ready = sem("top_ready"), sem("top_row"), sem("flag_ready")
        blank_ready, xe_cleared = sem("blank_ready"), sem("xe_cleared")

        with ExitStack() as st, nc.Block() as block:
            xT = sb(st, "xT", [P, 2, DC, BLK])
            w_in = sb(st, "w_in", [P, 3, DC, D])
            w = [sb(st, f"w_{s}", [P, 3, DC, D], FP32R) for s in ("hi", "lo")]
            x = [sb(st, f"x_{s}", [P, 2, DC, BLK], FP32R) for s in ("hi", "lo")]
            PAIRS = ((0, 0), (1, 0), (0, 1))
            parts = sb(st, "parts", [P, 3, U, N], BF16)
            rest = sb(st, "rest", [P, 2, BLK])
            sq = sb(st, "sq", [P, U, BLK], BF16)
            qn = sb(st, "qn", [H, N])
            kn = sb(st, "kn", [H, NB // B])
            qm = sb(st, "qm", [H, NB // B])
            kmax = sb(st, "kmax", [H, 1])
            qmax = sb(st, "qmax", [H, 1])
            shift = sb(st, "shift", [H, 2, T], BF16)
            bound = sb(st, "bound", [H, N])
            topb = sb(st, "topb", [H, B])
            top = sb(st, "top", [H, 1])
            topr = sb(st, "topr", [1, 1])
            proj = ps(st, "proj", [P, U, BLK])
            norm = ps(st, "norm", [P, 2, BLK])
            vps = ps(st, "vps", [P, 2, 2, D])

            @block.gpsimd
            def _(pool):
                pool.memset(ident[:], 0.0).then_inc(consts_ready, 1)
                pool.memset(ones[:], 1.0).then_inc(consts_ready, 1)
                pool.memset(one_head[:], 1.0).then_inc(consts_ready, 1)
                pool.memset(upto[:], 1.0).then_inc(consts_ready, 1)
                pool.memset(after[:], 1.0).then_inc(consts_ready, 1)
                pool.memset(blank[:], 0.0).then_inc(consts_ready, 1)
                pool.wait_ge(consts_ready, 6)
                pool.memset(blank[:, COL_ID:COL_ID + 1], float(T)).then_inc(blank_ready, 1)
                pool.affine_select(out=ident[:], in_=ident[:], compare_op=ALU.not_equal, fill=1.0, base=0,
                                   pattern=[[-1, P]], channel_multiplier=1).then_inc(consts_ready, 1)
                pool.affine_select(out=before[:], in_=ones[:], compare_op=ALU.is_gt, fill=0.0, base=0,
                                   pattern=[[1, P]], channel_multiplier=-1).then_inc(consts_ready, 1)
                pool.affine_select(out=upto[:], in_=upto[:], compare_op=ALU.is_ge, fill=0.0, base=0,
                                   pattern=[[0, 4], [1, P]], channel_multiplier=-1).then_inc(consts_ready, 1)
                pool.affine_select(out=after[:], in_=after[:], compare_op=ALU.is_gt, fill=0.0, base=0,
                                   pattern=[[0, 4], [-1, P]], channel_multiplier=1).then_inc(consts_ready, 1)
                pool.affine_select(out=one_head[:], in_=one_head[:], compare_op=ALU.is_ge, fill=0.0, base=0,
                                   pattern=[[P, DC], [-HD, H]], channel_multiplier=1).then_inc(consts_ready, 1)
                pool.wait_ge(consts_ready, 11)
                pool.affine_select(out=one_head[:], in_=one_head[:], compare_op=ALU.is_ge, fill=0.0, base=HD - 1,
                                   pattern=[[-P, DC], [HD, H]], channel_multiplier=-1).then_inc(consts_ready, 1)

            @block.sync
            def _(sp):
                for i, w_dram in enumerate((wq, wk, wv)):
                    sp.dma_start(w_in[:, i], w_dram.rearrange("(c p) n -> p c n", p=P)).then_inc(w_loaded, 16)
                xT_view = x_T.rearrange("(c p) t -> p c t", p=P)
                for j in range(2):
                    sp.dma_start(xT[:, j], xT_view[:, :, j * BLK:(j + 1) * BLK]).then_inc(xT_loaded[j], 16)
                for n in range(NB):
                    if n + 2 < NB:
                        sp.wait_ge(x_split, DC * (n + 1))
                        sp.dma_start(xT[:, n % 2], xT_view[:, :, (n + 2) * BLK:(n + 3) * BLK]).then_inc(xT_loaded[n % 2], 16)
                    sp.wait_ge(proj_split, U + U * (n + 1))
                    b, cols = n // NG, slice(n % NG * BLK, (n % NG + 1) * BLK)
                    for i in range(2):
                        for s in range(3):
                            sp.dma_start(split_dram[i, s, b * D:(b + 1) * D, cols].rearrange("(c p) t -> p c t", p=P),
                                         parts[:, s, DC * i:DC * (i + 1), cols]).then_inc(parts_stored[n % NG], 16)
                    if n % NG == NG - 1:
                        sp.wait_ge(shift_ready, b + 1)
                        sp.dma_start(shift_dram[:, b * H:(b + 1) * H, :].rearrange("s h t -> h s t"),
                                     shift[:, :, b * N:(b + 1) * N]).then_inc(shift_stored, 16)
                for n in range(NB // B):
                    sp.wait_ge(parts_stored[n], 16 * 6 * B)
                sp.wait_ge(shift_stored, 16 * B)

            @block.tensor
            def _(pe):
                pe.sem_inc(norm_ready, 1)
                pe.wait_ge(w_split, 3)
                pe.wait_ge(consts_ready, 12)
                with pe.Fori(0, NB // 2) as i:
                    for j in range(2):
                        pe.wait_ge(x_split, i * (2 * DC) + (j + 1) * DC)
                        for u in range(U):
                            pe.wait_ge(proj_read, i * (2 * U) + (j * U + u + 1))
                            for c in range(DC):
                                for a, b in PAIRS:
                                    last = nc.tensor.matmul(proj[:, u, :], w[a][:, u // DC, c, (u % DC) * P:(u % DC + 1) * P], x[b][:, j, c, :],
                                                            start=(c == 0 and (a, b) == PAIRS[0]), stop=(c == DC - 1 and (a, b) == PAIRS[-1]))
                            last.then_inc(proj_ready, 1)
                        for t in range(4):
                            pe.wait_ge(v_read, i * 8 + (4 * j + 2 * (t // 2) + 2))
                            for c in range(DC):
                                for a, b in PAIRS:
                                    last = nc.tensor.matmul(vps[:, t // 2, t % 2, :], x[a][:, j, c, t * P:(t + 1) * P], w[b][:, 2, c, :],
                                                            start=(c == 0 and (a, b) == PAIRS[0]), stop=(c == DC - 1 and (a, b) == PAIRS[-1]))
                            last.then_inc(v_ready, 1)
                        pe.wait_ge(sq_ready, i * (2 * U) + (j + 1) * U)
                        pe.wait_ge(norm_read, i * 6 + (3 * j + 3))
                        for u in range(U):
                            last = nc.tensor.matmul(norm[0:H, u // DC, :], one_head[:, u % DC, :], sq[:, u, :],
                                                    start=(u % DC == 0), stop=(u % DC == DC - 1))
                        last.then_inc(norm_ready, 1)
                pe.wait_ge(top_ready, 1)
                nc.tensor.matmul(proj[0:1, 0, 0:H], top[:], ident[0:H, 0:H], start=True, stop=True).then_inc(top_row, 1)

            @block.scalar
            def _(act):
                act.sem_inc(v_read, 4)
                v_by_tile = v_all[:].rearrange("p (b h) t d -> p b h t d", b=B)
                act.wait_ge(w_loaded, 48)
                for m in range(3):
                    nc.scalar.activation(w[0][:, m], w_in[:, m], ACT.Copy).then_inc(w_hi, 1)

                def split_x(pair, j):
                    act.wait_ge(xT_loaded[j], pair * 16 + 16)
                    for c in range(DC):
                        nc.scalar.activation(x[0][:, j, c, :], xT[:, j, c, :], ACT.Copy).then_inc(x_hi, 1)

                def one_block(b, i, j):
                    if not (b == B - 1 and isinstance(i, int) and i + 1 == NB // 2 // B and j == 1):
                        split_x(i + (b * (NB // 2 // B) + j), 1 - j)
                    if b > 0:
                        act.wait_ge(parts_stored[2 * i + j], 16 * 6)
                    act.wait_ge(norm_ready, i * 2 + (b * (NB // B) + j + 1))
                    cols = bass.ds(i * (2 * BLK) + j * BLK, BLK)
                    for u in range(U + 1):
                        at = i * (2 * U) + (b * (U * NB // B) + j * U + u)
                        if u < U:
                            act.wait_ge(proj_ready, at + 1)
                            nc.scalar.activation(sq[:, u, :], proj[:, u, :], ACT.Square).then_inc(sq_ready, 1)
                            nc.scalar.activation(parts[:, 0, u, cols], proj[:, u, :], ACT.Copy).then_inc(hi_ready, 1)
                        if u >= 1:
                            act.wait_ge(proj_read, at + U)
                            nc.scalar.activation(parts[:, 1, u - 1, cols], rest[:, (u - 1) % 2, :], ACT.Copy).then_inc(mid_ready, 1)
                    for t in range(4):
                        act.wait_ge(v_ready, i * 8 + (b * (4 * NB // B) + 4 * j + 2 * (t // 2) + 2))
                        nc.scalar.activation(v_by_tile[:, b:b + 1, :, bass.ds(i * 8 + (4 * j + t), 1), :],
                                             vps[:, t // 2, t % 2, :].rearrange("p (x h y d) -> p x h y d", x=1, y=1, h=H),
                                             ACT.Copy).then_inc(v_read, 1)

                split_x(0, 0)
                with act.Fori(0, NB // 2 // B) as i:
                    for j in range(2):
                        one_block(0, i, j)
                for n in range(NB // B):
                    one_block(1, n // 2, n % 2)

            @block.vector
            def _(dve):
                dve.sem_inc(proj_read, U)
                dve.sem_inc(proj_split, U)
                dve.sem_inc(norm_read, 3)
                links_b = 5
                for m in range(3):
                    dve.wait_ge(w_hi, m + 1)
                    nc.vector.tensor_tensor(w[1][:, m], w_in[:, m], w[0][:, m].bitcast(FP32), ALU.subtract).then_inc(w_split, 1)

                def split_x(pair, j):
                    for c in range(DC):
                        dve.wait_ge(x_hi, pair * (2 * DC) + (j * DC + c + 1))
                        nc.vector.tensor_tensor(x[1][:, j, c, :], xT[:, j, c, :], x[0][:, j, c, :].bitcast(FP32), ALU.subtract).then_inc(x_split, 1)

                def one_block(b, i, j):
                    if not (b == B - 1 and isinstance(i, int) and i + 1 == NB // 2 // B and j == 1):
                        split_x(i + (b * (NB // 2 // B) + j), 1 - j)
                    hi, mid, lo = ([parts[:, s, u, bass.ds(i * (2 * BLK) + j * BLK, BLK)] for u in range(U)] for s in range(3))
                    for u in range(U + 1):
                        at = i * (2 * U) + (b * (U * NB // B) + j * U + u)
                        if u < U:
                            dve.wait_ge(hi_ready, at + 1)
                            dve.wait_ge(proj_split, at + U - 1)
                            nc.vector.tensor_tensor(rest[:, u % 2, :], proj[:, u, :], hi[u], ALU.subtract).then_inc(proj_read, 1)
                        if u >= 1:
                            dve.wait_ge(mid_ready, at)
                            nc.vector.tensor_tensor(lo[u - 1], rest[:, (u - 1) % 2, :], mid[u - 1], ALU.subtract).then_inc(proj_split, 1)
                    dve.wait_ge(norm_ready, i * 2 + (b * (NB // B) + j + 2))
                    nc.vector.tensor_copy(qn[:, bass.ds(i * (2 * BLK) + j * BLK, BLK)], norm[0:H, 0, :]).then_inc(norm_read, 1)
                    nc.vector.tensor_reduce(qm[:, bass.ds(i * 2 + j, 1)], norm[0:H, 0, :], AX.X, ALU.max).then_inc(norm_read, 1)
                    nc.vector.tensor_reduce(kn[:, bass.ds(i * 2 + j, 1)], norm[0:H, 1, :], AX.X, ALU.max).then_inc(norm_read, 1)

                split_x(0, 0)
                for b in range(B):
                    if b < B - 1:
                        with dve.Fori(0, NB // 2 // B) as i:
                            for j in range(2):
                                one_block(b, i, j)
                    else:
                        for n in range(NB // B):
                            one_block(b, n // 2, n % 2)
                    step = b * links_b
                    dve.wait_ge(norm_read, (b + 1) * (3 * NB // B) + 3)
                    nc.vector.tensor_reduce(kmax[:], kn[:], AX.X, ALU.max).then_inc(dve1, 1)
                    nc.vector.tensor_reduce(qmax[:], qm[:], AX.X, ALU.max).then_inc(dve1, 1)
                    dve.wait_ge(dve1, step + 2)
                    nc.vector.tensor_scalar(topb[:, b:b + 1], qmax[:], kmax[:], 0.125, ALU.add, ALU.mult).then_inc(dve1, 1)
                    nc.vector.tensor_scalar(bound[:], qn[:], kmax[:], 0.125, ALU.add, ALU.mult).then_inc(dve1, 1)
                    dve.wait_ge(dve1, step + 4)
                    if b == B - 1:
                        nc.vector.tensor_reduce(top[:], topb[:], AX.X, ALU.max).then_inc(top_ready, 1)
                    nc.vector.tensor_copy(shift[:, 0, b * N:(b + 1) * N], bound[:]).then_inc(dve1, 1)
                    dve.wait_ge(dve1, step + 5)
                    nc.vector.tensor_tensor(shift[:, 1, b * N:(b + 1) * N], bound[:], shift[:, 0, b * N:(b + 1) * N],
                                            ALU.subtract).then_inc(shift_ready, 1)
                    dve.wait_ge(shift_ready, b + 1)
                dve.wait_ge(top_row, 1)
                nc.vector.tensor_reduce(topr[:], proj[0:1, 0, 0:H], AX.X, ALU.max).then_inc(dve1, 1)
                dve.wait_ge(dve1, B * links_b + 1)
                nc.vector.tensor_scalar(flag[0:1, 0:1], topr[:], BOUND_MAX, None, ALU.is_gt).then_inc(flag_ready, 1)

        attn = sb(att, "attn", [P, 2, NT, HD])
        aq = [sb(att, f"aq{j}", [P, N], BF16) for j in range(2)]
        ak = [sb(att, f"ak{j}", [P, N], BF16) for j in range(2)]
        KR = 6 * HD
        AQ = ((0, 3), (1, 2), (2, 1))
        AK = ((0, 3), (3, 2), (5, 1))
        KS = KR + 2
        A_DMAS = 6 + 3

        def load_operands(sp, j, n, done):
            for s, (part, times) in enumerate(AQ):
                for r in range(times):
                    at = (0, 3, 5)[s] + r
                    sp.dma_start(aq[j][at * HD:(at + 1) * HD, :], split_dram[0, part, bass.ds(n * HD, HD), :]).then_inc(done, 16)
            for at, k in AK:
                sp.dma_start(ak[j][at * HD:(at + k) * HD, :], split_dram[1, 0:k, bass.ds(n * HD, HD), :]).then_inc(done, 16)

        g_loaded, g_link, g_scores, g_read = sem("g_loaded"), sem("g_link"), sem("g_scores"), sem("g_read")
        g_max, g_row, g_row_sb, g_stored, g_over = sem("g_max"), sem("g_row"), sem("g_row_sb"), sem("g_stored"), sem("g_over")
        with ExitStack() as st, nc.Block() as block:
            s_all = ps(st, "s_all", [P, N])
            m_ps = ps(st, "m_ps", [P, BLK])
            m_sb = sb(st, "m_sb", [P, NT])
            m_32 = sb(st, "m_32", [NT, P])
            m_row = sb(st, "m_row", [NT, 2, P], BF16)

            @block.sync
            def _(sp):
                sp.wait_ge(flag_ready, 1)
                loose = sp.value_load(flag[0:1, 0:1], min_val=0, max_val=1)
                with sp.If(loose > 0):
                    with sp.Fori(0, NH) as n:
                        load_operands(sp, 0, n, g_loaded)
                        sp.wait_ge(g_row_sb, n * 1 + 1)
                        for s in range(2):
                            sp.dma_start(shift_dram[s, bass.ds(n, 1), :].rearrange("o (t q) -> (o t) q", q=P),
                                         m_row[:, s, :]).then_inc(g_stored, 16)
                        sp.wait_ge(g_stored, n * 32 + 32)
                        sp.sem_inc(g_over, 1)

            @block.tensor
            def _(pe):
                pe.wait_ge(flag_ready, 1)
                loose = pe.value_load(flag[0:1, 0:1], min_val=0, max_val=1)
                with pe.If(loose > 0):
                    with pe.Fori(0, NH) as n:
                        pe.wait_ge(g_loaded, n * (16 * A_DMAS) + 16 * A_DMAS)
                        for i in range(NT):
                            pe.wait_ge(g_read, n * NT + i + 1)
                            for k in range(NG):
                                last = nc.tensor.matmul(s_all[:, k * BLK:(k + 1) * BLK], aq[0][0:KR, i * P:(i + 1) * P],
                                                        ak[0][0:KR, k * BLK:(k + 1) * BLK], start=True, stop=True)
                            last.then_inc(g_scores, 1)
                        pe.wait_ge(g_read, n * NT + NT + 1)
                        nc.tensor.matmul(m_ps[0:NT, 0:P], m_sb[:], ident[:], start=True, stop=True).then_inc(g_row, 1)

            @block.vector
            def _(dve):
                dve.wait_ge(flag_ready, 1)
                loose = dve.value_load(flag[0:1, 0:1], min_val=0, max_val=1)
                with dve.If(loose > 0):
                    dve.sem_inc(g_read, 1)
                    with dve.Fori(0, NH) as n:
                        for i in range(NT):
                            dve.wait_ge(g_scores, n * NT + i + 1)
                            nc.vector.tensor_reduce(m_sb[:, i:i + 1], s_all[:], AX.X, ALU.max).then_inc(g_read, 1)
                        dve.wait_ge(g_row, n * 1 + 1)
                        nc.vector.tensor_scalar(m_32[:], m_ps[0:NT, 0:P], 0.25, None, ALU.mult).then_inc(g_link, 1)
                        dve.wait_ge(g_link, n * 2 + 1)
                        nc.vector.tensor_copy(m_row[:, 0, :], m_32[:]).then_inc(g_link, 1)
                        dve.wait_ge(g_link, n * 2 + 2)
                        nc.vector.tensor_tensor(m_row[:, 1, :], m_32[:], m_row[:, 0, :], ALU.subtract).then_inc(g_row_sb, 1)

        a_loaded = [sem(f"a_loaded{j}") for j in range(2)]
        vh_ready, minus_ready, fills_ready = sem("vh_ready"), sem("minus_ready"), sem("fills_ready")
        scores_ready, exp_done, pv_done = sem("scores_ready"), sem("exp_done"), sem("pv_done")
        mask_done, out_copied, out_turned, out_read = sem("mask_done"), sem("out_copied"), sem("out_turned"), sem("out_read")
        x_summed, head_done, hidden_ready, dve3 = sem("x_summed"), sem("head_done"), sem("hidden_ready"), sem("dve3")
        x_loaded = sem("x_loaded")
        adding_head = sem("adding_head")
        attn_added, st_ready = sem("attn_added"), sem("st_ready")
        x_sb = sb(att, "x_sb", [P, TT, D])
        stats = sb(att, "stats", [P, TT, 6])
        with ExitStack() as st, nc.Block() as block:
            probs = sb(st, "probs", [P, P_RING, KSPAN])
            expq = sb(st, "expq", [P, X_RING, KSPAN])
            vh = [sb(st, f"vh{j}", [P, NT, 32]) for j in range(2)]
            only_sum = sb(st, "only_sum", [P, 32])
            zeros = sb(st, "zeros", [P, 32])
            hidden = sb(st, "hidden", [P, 4, P])
            o_sb = sb(st, "o_sb", [P, O_RING, BLK])
            num = sb(st, "num", [P, NT, HD + 1])
            sums = sb(st, "sums", [P, 2, NT + 3])
            den = sb(st, "den", [P, NT])
            inv = sb(st, "inv", [P, NT])
            scores = [ps(st, f"scores{j}", [P, KSPAN]) for j in range(S_RING)]
            o_ps = [ps(st, f"o_ps{j}", [P, BLK]) for j in range(O_RING)]
            pairs = NH // 2

            @block.sync
            def _(sp):
                def load_head(j, n):
                    load_operands(sp, j, n, a_loaded[j])
                    sp.dma_start(aq[j][KR:KS, :], shift_dram[:, bass.ds(n, 1), :].rearrange("s o t -> (s o) t")).then_inc(a_loaded[j], 16)

                for j in range(2):
                    load_head(j, j)
                sp.dma_start(x_sb[:], x_tok.rearrange("(t p) d -> p t d", p=P)).then_inc(x_loaded, 16)
                sp.wait_ge(blank_ready, 1)
                sp.wait_ge(consts_ready, 12)
                sp.dma_start(xe_dram.rearrange("(p s) c -> p s c", p=P),
                             blank[:, None, :].to_broadcast([P, E * CAP // P, ROW])).then_inc(xe_cleared, 16)
                load_up(sp, 0)
                with sp.Fori(1, pairs) as i:
                    for j in range(2):
                        sp.wait_ge(scores_ready, i * (2 * NS) + (j - 1) * NS)
                        load_head(j, i * 2 + j)
                sp.wait_ge(x_loaded, 16)

            @block.gpsimd
            def _(pool):
                for j in range(2):
                    pool.memset(vh[j][:], 0.0).then_inc(fills_ready, 1)
                    pool.memset(sums[:, j, :], 0.0).then_inc(fills_ready, 1)
                pool.memset(only_sum[:], 0.0).then_inc(fills_ready, 1)
                pool.memset(zeros[:], 0.0).then_inc(fills_ready, 1)
                pool.wait_ge(fills_ready, 6)
                pool.memset(only_sum[:, HD:HD + 1], 1.0).then_inc(fills_ready, 1)
                for j in range(2):
                    pool.memset(vh[j][:, :, HD:HD + 1], 1.0).then_inc(fills_ready, 1)
                pool.wait_ge(fills_ready, 9)
                pool.sem_inc(attn_added, 2)

                def fill_v(i, j):
                    pool.wait_ge(pv_done, i * (2 * NK) + (j * NK + NK + P_RING))
                    nc.gpsimd.tensor_copy(vh[j][:, :, 0:HD], v_all[:, bass.ds(i * 2 + j, 1), :, :].rearrange("p o t d -> p (o t) d")).then_inc(vh_ready, 1)

                def add_before(i, j, b):
                    pool.wait_ge(head_done, i * 2 + (j - 2 + 1 + 2))
                    pool.sem_inc(adding_head, 1)
                    cols = x_sb[:, b * NT:(b + 1) * NT, bass.ds(i * (2 * HD) + ((j - 2) * HD - b * D), HD)]
                    nc.gpsimd.tensor_tensor(cols, cols, attn[:, j], ALU.add).then_inc(attn_added, 1)

                for j in range(2):
                    fill_v(0, j)
                pool.wait_ge(x_loaded, 16)
                for b in range(B):
                    with pool.Fori(b * H // 2 + 1, min((b + 1) * H // 2 + 1, pairs)) as i:
                        for j in range(2):
                            fill_v(i, j)
                            add_before(i, j, b)
                for j in range(2):
                    add_before(pairs, j, B - 1)

            @block.tensor
            def _(pe):
                pe.wait_ge(fills_ready, 9)
                pe.wait_ge(minus_ready, 2)
                pe.sem_inc(pv_done, P_RING + 2 * NK)

                def fill(i, j, t):
                    kind, m = SEQ[t]
                    pe.wait_ge(exp_done, i * (2 * NS) + (j * NS + t + 1))
                    dst = scores[t % S_RING]
                    pieces = []
                    if kind == "K":
                        for g, k, at, w in KT[m]:
                            pieces.append((at, ak[j][0:KS, k * P:(k + 1) * P], aq[j], (g + 1) * BLK - w, w))
                    else:
                        for q, at, lo, w, _ in QT[m]:
                            while w:
                                step = min(w, BLK - at % BLK)
                                pieces.append((at, aq[j][0:KS, q * P:(q + 1) * P], ak[j], lo, step))
                                at, lo, w = at + step, lo + step, w - step
                    for at, still, moving, lo, w in pieces:
                        last = nc.tensor.matmul(dst[:, at:at + w], still, moving[0:KS, lo:lo + w], start=True, stop=True, skip_group_check=True)
                    last.then_inc(scores_ready, 1)

                def products(i, j, name):
                    unit, done = UNITS[name]
                    if name[0] == "D":
                        pe.wait_ge(mask_done, i * (2 * NG) + (j * NG + name[1] + 1))
                    else:
                        pe.wait_ge(exp_done, i * (2 * NS) + (j * NS + K_POS[unit[-1][0]] + 1 + S_RING))
                    for m, g, k, at, w in unit:
                        dst, r = o_ps[g % O_RING], k % 4
                        first = k < 4
                        if first and k == 0:
                            pe.wait_ge(out_read, i * (2 * NG) + (j * NG + g + 1))
                        last = nc.tensor.matmul(dst[32 * r:32 * r + 32, BLK - w:BLK], vh[j % 2][:, k, :], probs[:, m % P_RING, at:at + w],
                                                start=first, stop=True, skip_group_check=True)
                    if name == ("D", 0):
                        for m, g, k, at, w in unit[1:]:
                            nc.tensor.matmul(o_ps[0][32 * k:32 * k + 32, 0:BLK - w], zeros[:], probs[:, m % P_RING, at:at + BLK - w],
                                             start=False, stop=True, skip_group_check=True)
                    if name[0] == "D":
                        for r, lo, n in ((3, 3, 1), (2, 1, 2), (1, 0, 1)):
                            last = nc.tensor.matmul(o_ps[name[1] % O_RING][32 * r:32 * r + 32, lo * P:(lo + n) * P], only_sum[:],
                                                    hidden[:, lo:lo + n, :].rearrange("p r c -> p (r c)"),
                                                    start=False, stop=True, skip_group_check=True)
                    last.then_inc(pv_done, done)

                def turn(i, j, g):
                    pe.wait_ge(out_copied, i * (2 * NG) + (j * NG + g + 1))
                    for q in range(4):
                        last = nc.tensor.transpose(o_ps[g % O_RING][:, q * P:(q + 1) * P], o_sb[:, g % O_RING, q * P:(q + 1) * P], ident[:])
                    last.then_inc(out_turned, 1)

                def head(i, j, older):
                    pe.wait_ge(a_loaded[j], i * (16 * (A_DMAS + 1)) + 16 * (A_DMAS + 1))
                    pe.wait_ge(vh_ready, i * 2 + (j + 1))
                    for t in range(NS):
                        fill(i, j, t)
                        for back, work, which in AFTER[t]:
                            if older or not back:
                                (products if work == "unit" else turn)(i, j - back, which)

                head(0, 0, False)
                head(0, 1, True)
                with pe.Fori(1, pairs) as i:
                    for j in range(2):
                        head(i, j, True)
                for t in range(NS):
                    for back, work, which in AFTER[t]:
                        if back:
                            (products if work == "unit" else turn)(pairs, -back, which)

            @block.scalar
            def _(act):
                act.sem_inc(exp_done, S_RING)
                act.wait_ge(fills_ready, 9)
                with act.Fori(0, pairs) as i:
                    for j in range(2):
                        act.wait_ge(head_done, i * 2 + (j + 1))
                        for t, (kind, m) in enumerate(SEQ):
                            src = scores[t % S_RING]
                            act.wait_ge(scores_ready, i * (2 * NS) + (j * NS + t + 1))
                            if kind == "K":
                                act.wait_ge(pv_done, i * (2 * NK) + (j * NK + m + 1 + 2 * NK))
                                w = sum(u[3] for u in KT[m])
                                last = nc.scalar.activation(probs[:, m % P_RING, 0:w], src[:, 0:w], ACT.Exp, scale=HD ** -0.5)
                            elif m in MANY:
                                n = MANY.index(m)
                                act.wait_ge(x_summed, i * (2 * NM) + (j * NM + n + 1))
                                w = sum(u[3] for u in QT[m])
                                last = nc.scalar.activation(expq[:, n % X_RING, 0:w], src[:, 0:w], ACT.Exp, scale=HD ** -0.5)
                            else:
                                (q, at, lo, w, col), = QT[m]
                                last = nc.scalar.activation(src[:, at:at + w], src[:, at:at + w], ACT.Exp, scale=HD ** -0.5,
                                                            accum_out=sums[:, j, col:col + 1])
                            last.then_inc(exp_done, 1)

            @block.vector
            def _(dve):
                for j in range(2):
                    nc.vector.memset(ak[j][KR:KS, :], -1.0 / HD ** -0.5).then_inc(minus_ready, 1)
                dve.sem_inc(out_read, O_RING)
                dve.sem_inc(x_summed, X_RING)
                dve.sem_inc(head_done, 2)
                LINKS = 3

                def mask(i, j, g):
                    m = DIAG[g]
                    dve.wait_ge(pv_done, i * (2 * NK) + (j * NK + (DIAG[g - 1] + 1 if g else DIAG[-1] + 1 - NK) + P_RING + 2 * NK))
                    dve.wait_ge(exp_done, i * (2 * NS) + (j * NS + K_POS[m] + 1 + S_RING))
                    three = probs[:, m % P_RING, :].rearrange("p (r c) -> p r c", c=BLK)[:, :, 0:P]
                    fourth = probs[:, m % P_RING, D_AT[3]:D_AT[3] + P]
                    nc.vector.tensor_tensor(hidden[:, 0:3, :], three, after[:, 0:3, :], ALU.mult).then_inc(hidden_ready, 1)
                    nc.vector.tensor_tensor(hidden[:, 3, :], fourth, after[:, 3, :], ALU.mult).then_inc(hidden_ready, 1)
                    dve.wait_ge(hidden_ready, i * (4 * NG) + (j * (2 * NG) + 2 * g + 2))
                    nc.vector.tensor_tensor(three, three, upto[:, 0:3, :], ALU.mult)
                    nc.vector.tensor_tensor(fourth, fourth, upto[:, 3, :], ALU.mult).then_inc(mask_done, 1)

                def sum_up(i, j, n):
                    m = MANY[n]
                    if n == 0:
                        dve.wait_ge(head_done, i * 2 + (j + 1))
                    dve.wait_ge(exp_done, i * (2 * NS) + (j * NS + Q_POS[m] + 1 + S_RING))
                    for q, at, lo, w, col in QT[m]:
                        last = nc.vector.tensor_reduce(sums[:, j % 2, col:col + 1], expq[:, n % X_RING, at:at + w], AX.X, ALU.add)
                    last.then_inc(x_summed, 1)

                def take(i, j, g):
                    dve.wait_ge(pv_done, i * (2 * NK) + (j * NK + LAST[g] + 1 + P_RING + 2 * NK))
                    nc.vector.tensor_copy(o_sb[:, g % O_RING, :], o_ps[g % O_RING][:]).then_inc(out_copied, 1)

                def gather(i, j, g):
                    if g == 0:
                        dve.wait_ge(head_done, i * 2 + (j + 2))
                    dve.wait_ge(out_turned, i * (2 * NG) + (j * NG + g + 1))
                    turned = o_ps[g % O_RING][:].rearrange("p (q r d) -> p q d r", q=4, r=4)[:, :, 0:HD + 1, :]
                    nc.vector.tensor_reduce(num[:, 4 * g:4 * g + 4, :], turned, AX.X, ALU.add).then_inc(out_read, 1)

                def finish(i, j, _):
                    step = i * (2 * LINKS) + j * LINKS
                    dve.wait_ge(attn_added, i * 2 + (j + 1))
                    dve.wait_ge(exp_done, i * (2 * NS) + (j * NS + NS + S_RING))
                    dve.wait_ge(x_summed, i * (2 * NM) + (j * NM + NM + X_RING))
                    dve.wait_ge(out_read, i * (2 * NG) + (j * NG + NG + O_RING))
                    nc.vector.tensor_tensor(den[:], num[:, :, HD], sums[:, j % 2, 0:NT], ALU.add).then_inc(dve3, 1)
                    dve.wait_ge(dve3, step + 1)
                    nc.vector.tensor_tensor(den[:, 0:3], den[:, 0:3], sums[:, j % 2, NT:NT + 3], ALU.add).then_inc(dve3, 1)
                    dve.wait_ge(dve3, step + 2)
                    nc.vector.reciprocal(inv[:], den[:]).then_inc(dve3, 1)
                    dve.wait_ge(dve3, step + 3)
                    nc.vector.tensor_tensor(attn[:, j % 2], num[:, :, 0:HD],
                                            inv[:, :, None].to_broadcast([P, NT, HD]), ALU.mult).then_inc(head_done, 1)

                WORK = {"mask": mask, "sum": sum_up, "take": take, "gather": gather, "final": finish}

                def head(i, j, older):
                    for back, work, which in DVE_ORDER:
                        if older or not back:
                            WORK[work](i, j - back, which)

                head(0, 0, False)
                head(0, 1, True)
                first = pairs - NT // 4
                with dve.Fori(1, first) as i:
                    for j in range(2):
                        head(i, j, True)
                dve.wait_ge(attn_added, H + 2)
                with dve.Fori(first, pairs) as i:
                    for j in range(2):
                        head(i, j, True)
                        for k in range(2):
                            tile = bass.ds(i * 4 + (2 * j + k - 4 * first), 1)
                            nc.vector.bn_stats(stats[:, tile, :].rearrange("p o s -> p (o s)"),
                                               x_sb[:, tile, :].rearrange("p o d -> p (o d)")).then_inc(st_ready, 1)
                for back, work, which in DVE_ORDER:
                    if back:
                        WORK[work](pairs, -back, which)

        dve4, dve5 = sem("dve4"), sem("dve5")
        var_ready, std_ready, scale_found, h_by_dve, h_by_act = sem("var_ready"), sem("std_ready"), sem("scale_found"), sem("h_by_dve"), sem("h_by_act")
        hT_ready, hT_by_act, hT_by_dve, lg_ready = sem("hT_ready"), sem("hT_by_act"), sem("hT_by_dve"), sem("lg_ready")
        wr_loaded, logit_off, p_exp = sem("wr_loaded"), sem("logit_off"), sem("p_exp")
        iota_ready, keep_ready, prefix_ready = sem("iota_ready"), sem("keep_ready"), sem("prefix_ready")
        over_ready, cand_ready, cand_count = sem("over_ready"), sem("cand_ready"), sem("cand_count")
        rows_ready, more_ready, rows_sent, acc_stored = sem("rows_ready"), sem("more_ready"), sem("rows_sent"), sem("acc_stored")
        GT = 4
        GB = NT // GT
        SENT = 16 * TOPK * TT
        with ExitStack() as st, nc.Block() as block:
            mean = sb(st, "mean", [P, TT])
            var = sb(st, "var", [P, TT])
            std = sb(st, "std", [P, TT])
            rstd = sb(st, "rstd", [P, TT])
            tmp = sb(st, "tmp", [P, TT])
            nbias = sb(st, "nbias", [P, TT])
            h = sb(st, "h", [P, TT, ROW])
            hT = [sb(st, f"hT{j}", [P, DC, GT * P]) for j in range(2)]
            wr = sb(st, "wr", [P, DC, E])
            probs = sb(st, "rprobs", [P, TT, E])
            work = sb(st, "work", [P, TT, E])
            pick = [sb(st, f"pick{k}", [P, TT, E]) for k in range(TOPK)]
            keep = sb(st, "keep", [P, TT, E])
            wgt = sb(st, "wgt", [P, TOPK, TT])
            kept_w = sb(st, "kept_w", [P, TOPK, TT])
            red = sb(st, "red", [P, TT])
            cs = [sb(st, f"cs{k}", [P, TT, E]) for k in range(2)]
            tot = sb(st, "tot", [P, TT, E])
            pos = sb(st, "pos", [P, TT, E])
            total = sb(st, "total", [P, E])
            over = sb(st, "over", [P, 1])
            big = [sb(st, f"big{j}", [1, E]) for j in range(3)]
            dest_f = sb(st, "dest_f", [P, TOPK, TT])
            dest = sb(st, "dest", [P, TOPK, TT], U32)
            ids = sb(st, "ids", [P, TT], I32)
            ebase_i = sb(st, "ebase_i", [P, E], I32)
            first_i = sb(st, "first_i", [P, E], I32)
            ebase = sb(st, "ebase", [P, E])
            first = sb(st, "first", [P, E])
            wm = sb(st, "wm", [P, TT, E])
            tau = sb(st, "tau", [P, E], I32)
            cand = sb(st, "cand", [P, E], I32)
            bit = sb(st, "bit", [P, E], I32)
            bit_f = sb(st, "bit_f", [P, E])
            cnt = sb(st, "cnt", [P, E])
            step_i = sb(st, "step_i", [P, E], I32)
            hT_ps = [ps(st, f"hT_ps{j}", [P, DC, GT * P]) for j in range(2)]
            lg_ps = [ps(st, f"lg_ps{b}", [P, BLK // E, E]) for b in range(B)]
            pf_ps = ps(st, "pf_ps", [P, 2, TT, E])
            cand_ps = ps(st, "cand_ps", [P, E])
            ALL = slice(0, TT)

            def of_batch(b):
                return slice(b * NT, (b + 1) * NT)

            def wide(x):
                return x[:, :, None].to_broadcast([P, x.shape[1], E])

            def each(x, tiles):
                return x[:, None, :].to_broadcast([P, tiles.stop - tiles.start, E])

            @block.sync
            def _(sp):
                sp.dma_start(wr[:], wr_T.rearrange("(c p) e -> p c e", p=P)).then_inc(wr_loaded, 16)
                for b in range(B):
                    sp.wait_ge(h_by_dve, NT // 2 * (b + 1))
                    sp.wait_ge(h_by_act, NT // 2 * (b + 1))
                    sp.dma_start(acc_dram.rearrange("(t p) d -> p t d", p=P)[:, of_batch(b), :], h[:, of_batch(b), 0:D]).then_inc(acc_stored, 16)
                sp.wait_ge(wr_loaded, 16)
                sp.wait_ge(acc_stored, 16 * B)

            @block.gpsimd
            def _(pool):
                pool.iota(ids[:], pattern=[[P, TT]], base=0, channel_multiplier=1).then_inc(iota_ready, 1)
                pool.iota(ebase_i[:], pattern=[[CAP, E]], base=0, channel_multiplier=0).then_inc(iota_ready, 1)
                pool.iota(first_i[:], pattern=[[-1, E]], base=E, channel_multiplier=0).then_inc(iota_ready, 1)
                pool.wait_ge(iota_ready, 3)
                nc.gpsimd.tensor_copy(ebase[:], ebase_i[:]).then_inc(iota_ready, 1)
                nc.gpsimd.tensor_copy(first[:], first_i[:]).then_inc(iota_ready, 1)
                nc.gpsimd.tensor_copy(h[:, :, COL_ID], ids[:]).then_inc(iota_ready, 1)
                pool.memset(h[:, :, COL_ID + 1:ROW], 0.0).then_inc(iota_ready, 1)

                def send(tiles):
                    for k in range(TOPK):
                        for t in range(tiles.start, tiles.stop):
                            pool.indirect_dma_start(out=xe_dram[:, :], out_offset=bass.IndirectOffsetOnAxis(ap=dest[:, k, t:t + 1], axis=0),
                                                    in_=h[:, t, :], in_offset=None, bounds_check=E * CAP - 1,
                                                    oob_is_err=False).then_inc(rows_sent, 16)

                pool.wait_ge(iota_ready, 7)
                pool.wait_ge(xe_cleared, 16)
                for b in range(B):
                    pool.wait_ge(rows_ready, b + 1)
                    send(of_batch(b))
                pool.wait_ge(rows_sent, SENT)
                pool.wait_ge(over_ready, 1)
                too_many = pool.value_load(flag[0:1, 1:2], min_val=0, max_val=1)
                with pool.If(too_many > 0):
                    pool.wait_ge(rows_ready, B + 1)
                    send(ALL)
                    pool.wait_ge(rows_sent, 2 * SENT)

            @block.scalar
            def _(act):
                for b in range(B):
                    act.wait_ge(var_ready, b + 1)
                    nc.scalar.activation(std[:, of_batch(b)], var[:, of_batch(b)], ACT.Sqrt).then_inc(std_ready, 1)
                    act.wait_ge(scale_found, b + 1)

                    def normalise(g):
                        for t in range(GT * g + GT // 2, GT * (g + 1)):
                            nc.scalar.activation(h[:, t, 0:D], x_sb[:, t, :], ACT.Identity, bias=nbias[:, t:t + 1], scale=rstd[:, t:t + 1]).then_inc(h_by_act, 1)

                    def copy_hT(g):
                        act.wait_ge(hT_ready, g + 1)
                        if g >= 2:
                            act.wait_ge(lg_ready, g - 1)
                        nc.scalar.activation(hT[g % 2][:, 0, :], hT_ps[g % 2][:, 0, :], ACT.Copy).then_inc(hT_by_act, 1)

                    for g in range(GB * b, GB * (b + 1) + 2):
                        if g < GB * (b + 1):
                            normalise(g)
                        if g >= GB * b + 2:
                            copy_hT(g - 2)
                    act.wait_ge(logit_off, b + 1)
                    nc.scalar.activation(probs[:, of_batch(b), :], work[:, of_batch(b), :], ACT.Exp).then_inc(p_exp, 1)

            def prefix_products(tiles):
                flat = keep[:, tiles, :].rearrange("p t e -> p (t e)")
                nc.tensor.matmul(pf_ps[:, 0, tiles, :].rearrange("p t e -> p (t e)"), before[:], flat, start=True, stop=True, skip_group_check=True)
                return nc.tensor.matmul(pf_ps[:, 1, tiles, :].rearrange("p t e -> p (t e)"), ones[:], flat, start=True, stop=True, skip_group_check=True)

            @block.tensor
            def _(pe):
                pe.wait_ge(wr_loaded, 16)

                def turn(g):
                    pe.wait_ge(h_by_dve, GT // 2 * (g + 1))
                    pe.wait_ge(h_by_act, GT // 2 * (g + 1))
                    if g >= 2:
                        pe.wait_ge(hT_by_act, g - 1)
                        pe.wait_ge(hT_by_dve, g - 1)
                    for c in range(DC):
                        for t in range(GT):
                            last = nc.tensor.transpose(hT_ps[g % 2][:, c, t * P:(t + 1) * P], h[:, GT * g + t, c * P:(c + 1) * P], ident[:])
                    last.then_inc(hT_ready, 1)

                def logits(g):
                    pe.wait_ge(hT_by_act, g + 1)
                    pe.wait_ge(hT_by_dve, g + 1)
                    b, at = g // GB, g % GB * GT
                    for t in range(GT):
                        for c in range(DC):
                            last = nc.tensor.matmul(lg_ps[b][:, at + t, :], hT[g % 2][:, c, t * P:(t + 1) * P], wr[:, c, :],
                                                    start=(at + t == 0 and c == 0), stop=(c == DC - 1), skip_group_check=True)
                    last.then_inc(lg_ready, 1)

                for b in range(B):
                    for g in range(GB * b, GB * (b + 1) + 1):
                        if g < GB * (b + 1):
                            turn(g)
                        if g > GB * b:
                            logits(g - 1)
                    pe.wait_ge(keep_ready, b + 1)
                    prefix_products(of_batch(b)).then_inc(prefix_ready, 1)
                pe.wait_ge(over_ready, 1)
                too_many = pe.value_load(flag[0:1, 1:2], min_val=0, max_val=1)
                with pe.If(too_many > 0):
                    with pe.Fori(0, TAU_BITS) as i:
                        pe.wait_ge(cand_ready, i * 1 + 1)
                        nc.tensor.matmul(cand_ps[:], ones[:], cnt[:], start=True, stop=True).then_inc(cand_count, 1)
                    pe.wait_ge(cand_ready, TAU_BITS + 1)
                    nc.tensor.matmul(cand_ps[:], ones[:], cnt[:], start=True, stop=True).then_inc(cand_count, 1)
                    for n in range(2):
                        pe.wait_ge(keep_ready, B + n + 1)
                        prefix_products(ALL).then_inc(prefix_ready, 1)

            @block.vector
            def _(dve):
                link = chain(dve, dve4)

                def measure(b):
                    tiles = of_batch(b)
                    if b == 1:
                        dve.wait_ge(attn_added, NH + 2)
                        for t in range(NT, TT):
                            nc.vector.bn_stats(stats[:, t, :], x_sb[:, t, :]).then_inc(st_ready, 1)
                    dve.wait_ge(st_ready, tiles.stop)
                    layer_stats(nc, link, stats[:, tiles, :], mean[:, tiles], var[:, tiles], tmp[:, tiles]).then_inc(var_ready, 1)
                    dve.wait_ge(std_ready, b + 1)
                    link(inverse_root(nc, link, var[:, tiles], std[:, tiles], rstd[:, tiles], tmp[:, tiles]))
                    nc.vector.scalar_tensor_tensor(nbias[:, tiles], mean[:, tiles], -1.0, rstd[:, tiles], ALU.mult, ALU.mult).then_inc(scale_found, 1)

                def normalise(g):
                    for t in range(GT * g, GT * g + GT // 2):
                        nc.vector.tensor_scalar(h[:, t, 0:D], x_sb[:, t, :], mean[:, t:t + 1], rstd[:, t:t + 1], ALU.subtract, ALU.mult).then_inc(h_by_dve, 1)

                def copy_hT(g):
                    dve.wait_ge(hT_ready, g + 1)
                    if g >= 2:
                        dve.wait_ge(lg_ready, g - 1)
                    nc.vector.tensor_copy(hT[g % 2][:, 1, :], hT_ps[g % 2][:, 1, :]).then_inc(hT_by_dve, 1)

                def weigh(link, w, of, tiles):
                    link(nc.vector.tensor_tensor(red[:, tiles], of[:, 0, tiles], of[:, 1, tiles], ALU.add))
                    link(nc.vector.tensor_scalar(red[:, tiles], red[:, tiles], MOE_EPS, None, ALU.max))
                    link(nc.vector.reciprocal(tmp[:, tiles], red[:, tiles]))
                    link(nc.vector.tensor_tensor(w[:, :, tiles], of[:, :, tiles],
                                                 tmp[:, None, tiles].to_broadcast([P, TOPK, tiles.stop - tiles.start]), ALU.mult))

                def prefixes(link, n, tiles):
                    many = tiles.stop - tiles.start
                    dve.wait_ge(prefix_ready, n)
                    link(nc.vector.tensor_copy(tot[:, 0:many, :], pf_ps[:, 1, tiles, :]))
                    a, s, src = 0, 1, tot
                    while s < many:
                        nc.vector.tensor_copy(cs[a][:, 0:s, :], src[:, 0:s, :])
                        link(nc.vector.tensor_tensor(cs[a][:, s:many, :], src[:, s:many, :], src[:, :many - s, :], ALU.add))
                        a, s, src = 1 - a, 2 * s, cs[a]
                    link(nc.vector.tensor_tensor(pos[:, tiles, :], src[:, 0:many, :], tot[:, 0:many, :], ALU.subtract))
                    link(nc.vector.tensor_tensor(pos[:, tiles, :], pos[:, tiles, :], pf_ps[:, 0, tiles, :], ALU.add))
                    return src

                def places(link, tiles):
                    nc.vector.tensor_copy(h[:, tiles, COL_W:COL_W + TOPK], kept_w[:, :, tiles].rearrange("p k t -> p t k"))
                    link(nc.vector.tensor_scalar(work[:, tiles, :], pos[:, tiles, :], float(CAP), float(E * CAP), ALU.is_ge, ALU.mult))
                    link(nc.vector.tensor_tensor(pos[:, tiles, :], pos[:, tiles, :], each(ebase, tiles), ALU.add))
                    link(nc.vector.tensor_tensor(pos[:, tiles, :], pos[:, tiles, :], work[:, tiles, :], ALU.add))
                    link(nc.vector.tensor_tensor(work[:, tiles, :], pick[0][:, tiles, :], pos[:, tiles, :], ALU.mult))
                    nc.vector.tensor_reduce(dest_f[:, 0, tiles], work[:, tiles, :], AX.X, ALU.add)
                    link(nc.vector.tensor_tensor(pos[:, tiles, :], pick[1][:, tiles, :], pos[:, tiles, :], ALU.mult))
                    link(nc.vector.tensor_reduce(dest_f[:, 1, tiles], pos[:, tiles, :], AX.X, ALU.add))
                    nc.vector.tensor_copy(dest[:, :, tiles], dest_f[:, :, tiles]).then_inc(rows_ready, 1)

                def route(b):
                    tiles = of_batch(b)
                    p, w, r = probs[:, tiles, :], work[:, tiles, :], red[:, tiles]
                    dve.wait_ge(lg_ready, GB * (b + 1))
                    link(nc.vector.tensor_reduce(r, lg_ps[b][:, 0:NT, :], AX.X, ALU.max))
                    nc.vector.tensor_tensor(w, lg_ps[b][:, 0:NT, :], wide(r), ALU.subtract).then_inc(logit_off, 1)
                    dve.wait_ge(iota_ready, 7)
                    dve.wait_ge(p_exp, b + 1)
                    link(nc.vector.tensor_reduce(r, p, AX.X, ALU.add))
                    link(nc.vector.reciprocal(tmp[:, tiles], r))
                    link(nc.vector.tensor_tensor(p, p, wide(tmp[:, tiles]), ALU.mult))
                    for k in range(TOPK):
                        link(nc.vector.tensor_reduce(wgt[:, k, tiles], p, AX.X, ALU.max))
                        link(nc.vector.tensor_tensor(w, p, wide(wgt[:, k, tiles]), ALU.is_equal))
                        link(nc.vector.tensor_tensor(w, w, each(first, tiles), ALU.mult))
                        link(nc.vector.tensor_reduce(r, w, AX.X, ALU.max))
                        nc.vector.tensor_scalar(h[:, tiles, COL_E + k], r, -1.0, float(E), ALU.mult, ALU.add)
                        link(nc.vector.tensor_tensor(pick[k][:, tiles, :], w, wide(r), ALU.is_equal))
                        if k == 0:
                            link(nc.vector.scalar_tensor_tensor(p, pick[0][:, tiles, :], -4.0, p, ALU.mult, ALU.add))
                    nc.vector.tensor_tensor(keep[:, tiles, :], pick[0][:, tiles, :], pick[1][:, tiles, :], ALU.add).then_inc(keep_ready, 1)
                    weigh(link, wgt, wgt, tiles)
                    weigh(link, kept_w, wgt, tiles)
                    upto_tile = prefixes(link, b + 1, tiles)
                    if b == 0:
                        link(nc.vector.tensor_copy(total[:], upto_tile[:, NT - 1, :]))
                    else:
                        link(nc.vector.tensor_tensor(pos[:, tiles, :], pos[:, tiles, :], each(total, tiles), ALU.add))
                        link(nc.vector.tensor_tensor(total[:], total[:], upto_tile[:, NT - 1, :], ALU.add))
                    places(link, tiles)

                for b in range(B):
                    measure(b)
                    for g in range(GB * b, GB * (b + 1) + 2):
                        if g < GB * (b + 1):
                            normalise(g)
                        if g >= GB * b + 2:
                            copy_hT(g - 2)
                    route(b)
                link(nc.vector.tensor_scalar(big[0][:], total[0:1, :], float(2 * GA), None, ALU.is_gt))
                link(nc.vector.tensor_copy(more[:], big[0][:]))
                a, s, src = 1, 1, big[0]
                while s < E:
                    nc.vector.tensor_copy(big[a][:, 0:s], src[:, 0:s])
                    link(nc.vector.tensor_tensor(big[a][:, s:], src[:, s:], src[:, :E - s], ALU.add))
                    a, s, src = 3 - a, 2 * s, big[a]
                nc.vector.tensor_tensor(more_before[:], src[:], big[0][:], ALU.subtract).then_inc(more_ready, 1)
                dve.wait_ge(more_ready, 1)
                link(nc.vector.tensor_reduce(over[:], total[:], AX.X, ALU.max))
                nc.vector.tensor_scalar(flag[0:1, 1:2], over[0:1, :], float(CAP), None, ALU.is_gt).then_inc(over_ready, 1)
                dve.wait_ge(over_ready, 1)
                dve.wait_ge(rows_ready, B)
                too_many = dve.value_load(flag[0:1, 1:2], min_val=0, max_val=1)
                with dve.If(too_many > 0):
                    link5 = chain(dve, dve5)
                    link5(nc.vector.tensor_tensor(wm[:], pick[0][:], wide(wgt[:, 0, :]), ALU.mult))
                    link5(nc.vector.tensor_tensor(work[:], pick[1][:], wide(wgt[:, 1, :]), ALU.mult))
                    link5(nc.vector.tensor_tensor(wm[:], wm[:], work[:], ALU.add))
                    link5(nc.vector.scalar_tensor_tensor(wm[:], keep[:], -1.0, wm[:], ALU.add, ALU.add))
                    link5(nc.vector.memset(tau[:], 0))
                    link5(nc.vector.memset(bit[:], 1 << (TAU_BITS - 1)))
                    pre = link5.count()
                    with dve.Fori(0, TAU_BITS) as i:
                        at = i * 6 + pre
                        nc.vector.tensor_tensor(cand[:], tau[:], bit[:], ALU.bitwise_or).then_inc(dve5, 1)
                        dve.wait_ge(dve5, at + 1)
                        nc.vector.tensor_tensor(work[:], wm[:], each(cand.bitcast(FP32), ALL), ALU.is_ge).then_inc(dve5, 1)
                        dve.wait_ge(dve5, at + 2)
                        nc.vector.tensor_reduce(cnt[:], work[:].rearrange("p t e -> p e t"), AX.X, ALU.add).then_inc(cand_ready, 1)
                        nc.vector.tensor_copy(bit_f[:], bit[:]).then_inc(dve5, 1)
                        dve.wait_ge(dve5, at + 3)
                        dve.wait_ge(cand_count, i * 1 + 1)
                        nc.vector.scalar_tensor_tensor(step_i[:], cand_ps[:], float(CAP), bit_f[:], ALU.is_ge, ALU.mult).then_inc(dve5, 1)
                        dve.wait_ge(dve5, at + 4)
                        nc.vector.tensor_tensor(tau[:], tau[:], step_i[:], ALU.bitwise_or).then_inc(dve5, 1)
                        nc.vector.tensor_scalar(bit[:], bit[:], 1, None, ALU.logical_shift_right).then_inc(dve5, 1)
                        dve.wait_ge(dve5, at + 6)
                    link5.skip(6 * TAU_BITS)
                    link5(nc.vector.tensor_tensor(work[:], wm[:], each(tau.bitcast(FP32), ALL), ALU.is_gt))
                    nc.vector.tensor_reduce(cnt[:], work[:].rearrange("p t e -> p e t"), AX.X, ALU.add).then_inc(cand_ready, 1)
                    nc.vector.tensor_tensor(keep[:], wm[:], each(tau.bitcast(FP32), ALL), ALU.is_equal).then_inc(keep_ready, 1)
                    dve.wait_ge(cand_count, TAU_BITS + 1)
                    link5(nc.vector.tensor_copy(cnt[:], cand_ps[:]))
                    prefixes(link5, B + 1, ALL)
                    link5(nc.vector.tensor_tensor(pos[:], pos[:], each(cnt, ALL), ALU.add))
                    link5(nc.vector.scalar_tensor_tensor(wm[:], pos[:], float(CAP), keep[:], ALU.is_lt, ALU.mult))
                    nc.vector.tensor_tensor(keep[:], work[:], wm[:], ALU.add).then_inc(keep_ready, 1)
                    prefixes(link5, B + 2, ALL)
                    link5(nc.vector.scalar_tensor_tensor(pos[:], pos[:], -float(E * CAP), keep[:], ALU.add, ALU.mult))
                    link5(nc.vector.tensor_scalar(pos[:], pos[:], float(E * CAP), None, ALU.add))
                    for k in range(TOPK):
                        link5(nc.vector.tensor_tensor(work[:], pick[k][:], keep[:], ALU.mult))
                        link5(nc.vector.tensor_reduce(red[:], work[:], AX.X, ALU.add))
                        link5(nc.vector.tensor_tensor(kept_w[:, k, :], wgt[:, k, :], red[:], ALU.mult))
                    weigh(link5, kept_w, kept_w, ALL)
                    dve.wait_ge(rows_sent, SENT)
                    places(link5, ALL)
        att.close()

        xin_loaded, xrest_loaded = ([sem(f"{s}_loaded{j}") for j in range(2)] for s in ("xin", "xrest"))
        w1_hi, w1_split, w2_hi, w2_split = sem("w1_hi"), sem("w1_split"), sem("w2_hi"), sem("w2_split")
        xt_ready, xt_hi, xt_split = sem("xt_ready"), sem("xt_hi"), sem("xt_split")
        y_cleared, splitting = sem("y_cleared"), sem("splitting")
        up_ready, silu_done, mul_done, mid_hi, mid_split = sem("up_ready"), sem("silu_done"), sem("mul_done"), sem("mid_hi"), sem("mid_split")
        c_up_ready, c_silu_done, c_mul_done, c_mid_hi, c_mid_split = (sem("c_up_ready"), sem("c_silu_done"), sem("c_mul_done"),
                                                                      sem("c_mid_hi"), sem("c_mid_split"))
        c_xt_ready, c_xt_hi, c_xt_split, c_y_ready, c_y_done = (sem("c_xt_ready"), sem("c_xt_hi"), sem("c_xt_split"), sem("c_y_ready"),
                                                                sem("c_y_done"))
        y_ready, y_done, added, expert_over = sem("y_ready"), sem("y_done"), sem("added"), sem("expert_over")
        adding, c_done, leaving, dve6 = sem("adding"), sem("c_done"), sem("leaving"), sem("dve6")
        with ExitStack() as st, nc.Block() as block:
            raw2 = sb(st, "raw2", [P, FC, D])
            wup = [sb(st, f"wup_{s}", [P, 2, DC, F], FP32R) for s in ("hi", "lo")]
            w2 = [sb(st, f"w2_{s}", [P, FC, D], FP32R) for s in ("hi", "lo")]
            xin = [sb(st, f"xin{j}", [P, CT, ROW]) for j in range(2)]
            xT = [sb(st, f"xeT_{s}", [P, DC, 2 * GA], FP32R) for s in ("hi", "lo")]
            xTC = [sb(st, f"xeTC_{s}", [P, DC, GC], FP32R) for s in ("hi", "lo")]
            gate = [sb(st, f"gate{j}", [P, GA]) for j in range(2)]
            mid = [sb(st, f"mid{j}", [P, GA]) for j in range(2)]
            mid2 = [sb(st, f"mid_{s}", [P, FC, GA], FP32R) for s in ("hi", "lo")]
            y = [sb(st, f"y{j}", [P, CT, D]) for j in range(2)]
            wt = sb(st, "wt", [P, 2, CT])
            wt2 = [sb(st, f"wt2_{j}", [P, CT]) for j in range(2)]
            row = [sb(st, f"row{j}", [P, CT], U32) for j in range(2)]
            e_now = sb(st, "e_now", [P, 1])
            xt_ps = [ps(st, f"xt_ps{j}", [P, GA]) for j in range(2)]
            up_ps = [ps(st, f"up_ps{j}", [P, 2, GA]) for j in range(2)]
            y_ps = ps(st, "y_ps", [P, 4, D])
            PAIRS = ((0, 0), (1, 0), (0, 1))

            def count(per, i, j, k):
                return i * (2 * per) + (j * per + k)

            def experts(eng, body):
                with eng.Fori(0, E // 2 - 1) as i:
                    for j in range(2):
                        body(i, j, True)
                body(E // 2 - 1, 0, True)
                body(E // 2 - 1, 1, False)

            def extra(eng, i, j):
                e = i * 2 + j
                return (eng.value_load(more[0:1, bass.ds(e, 1)], min_val=0, max_val=1),
                        eng.value_load(more_before[0:1, bass.ds(e, 1)], min_val=0, max_val=E))

            @block.sync
            def _(sp):
                def load_down(sp, e):
                    sp.dma_start(raw2[:], w2_T[bass.ds(e, 1)].rearrange("o (c p) d -> p (o c) d", p=P)).then_inc(r2_loaded, 16)

                def load_rows(e, j):
                    sp.dma_start(xin[j][:, 0:NA, :], xe_dram[bass.ds(e * CAP, GA), :].rearrange("(s p) c -> p s c", p=P)).then_inc(xin_loaded[j], 16)
                    sp.dma_start(xin[j][:, NA:CT, :], xe_dram[bass.ds(e * CAP + GA, CAP - GA), :].rearrange("(s p) c -> p s c", p=P)).then_inc(xrest_loaded[j], 16)

                load_rows(0, 0)
                load_down(sp, 0)
                load_rows(1, 1)

                def body(i, j, prep):
                    if not prep:
                        return
                    e = i * 2 + (j + 1)
                    sp.wait_ge(w1_split, count(4, i, j, 4))
                    load_up(sp, e)
                    sp.wait_ge(w2_split, count(1, i, j, 1))
                    load_down(sp, e)
                    if not (isinstance(i, int) and j == 0):
                        sp.wait_ge(y_done, count(2 * NA, i, j, 3 * NA))
                        load_rows(i * 2 + (j + 2), j)

                experts(sp, body)

            @block.gpsimd
            def _(pool):
                pool.sem_inc(expert_over, 2)
                for j in range(2):
                    pool.memset(y[j][:], 0.0).then_inc(y_cleared, 1)

                def split_down(i, j):
                    pool.wait_ge(r2_loaded, count(16, i, j, 16))
                    pool.sem_inc(splitting, 1)
                    nc.gpsimd.tensor_copy(w2[0][:], raw2[:]).then_inc(w2_hi, 1)

                split_down(0, 0)

                def body(i, j, prep):
                    def add(tiles):
                        for t in tiles:
                            pool.indirect_dma_start(out=acc_dram[:, :], out_offset=bass.IndirectOffsetOnAxis(ap=row[j][:, t:t + 1], axis=0),
                                                    in_=y[j][:, t, :], in_offset=None, bounds_check=T - 1, oob_is_err=False,
                                                    compute_op=ALU.add).then_inc(added, 16)

                    pool.wait_ge(y_done, count(2 * NA, i, j, 2 * NA))
                    pool.sem_inc(adding, 1)
                    add(range(NA))
                    pool.wait_ge(c_done, i * 2 + (j + 1))
                    pool.sem_inc(adding, 1)
                    add(range(2 * NA, CT))
                    if prep:
                        pool.wait_ge(y_ready, count(2, i, j, 2))
                        split_down(i, j + 1)
                    pool.wait_ge(y_done, count(2 * NA, i, j, 3 * NA))
                    pool.sem_inc(adding, 1)
                    add(range(NA, 2 * NA))
                    pool.wait_ge(added, count(16 * CT, i, j, 16 * CT))
                    pool.sem_inc(expert_over, 1)

                experts(pool, body)

            @block.tensor
            def _(pe):
                def turn(j, g):
                    for c in range(DC):
                        for t in range(NA):
                            last = nc.tensor.transpose(xt_ps[c][:, t * P:(t + 1) * P], xin[j][:, g * NA + t, c * P:(c + 1) * P], ident[:])
                        last.then_inc(xt_ready, 1)

                def up(n, f, x, cols):
                    for k in range(2):
                        for c in range(DC):
                            for a, b in PAIRS:
                                last = nc.tensor.matmul(up_ps[n % 2][:, k, 0:cols.stop - cols.start], wup[a][:, k, c, f * P:(f + 1) * P], x[b][:, c, cols],
                                                        start=(c == 0 and (a, b) == PAIRS[0]), stop=(c == DC - 1 and (a, b) == PAIRS[-1]))
                    return last

                def down(f, nt):
                    for t in range(nt):
                        for a, b in PAIRS:
                            last = nc.tensor.matmul(y_ps[:, t, :], mid2[a][:, f, t * P:(t + 1) * P], w2[b][:, f, :],
                                                    start=(f == 0 and t % 2 == 0 and (a, b) == PAIRS[0]),
                                                    stop=(f == FC - 1 and (a, b) == PAIRS[-1]), skip_group_check=True)
                    return last

                pe.wait_ge(xin_loaded[0], 16)
                for g in range(2):
                    if g == 1:
                        pe.wait_ge(xrest_loaded[0], 16)
                        pe.wait_ge(xt_split, DC)
                    turn(0, g)

                def body(i, j, prep):
                    has, before_it = extra(pe, i, j)
                    pe.wait_ge(xt_split, count(4, i, j, 4))
                    pe.wait_ge(w1_split, count(4, i, j, 4))
                    for g in range(2):
                        if g == 1:
                            with pe.If(has > 0):
                                pe.wait_ge(mul_done, count(2 * FC, i, j, FC + 2))
                                pe.wait_ge(c_xt_split, before_it * DC + DC)
                                for f in range(FC):
                                    if f >= 2:
                                        pe.wait_ge(c_mul_done, before_it * FC + (f - 1))
                                    up(f, f, xTC, slice(0, GC)).then_inc(c_up_ready, 1)
                                pe.wait_ge(y_done, count(2 * NA, i, j, 2 * NA))
                                for f in range(FC):
                                    pe.wait_ge(c_mid_split, before_it * FC + (f + 1))
                                    last = down(f, NC)
                                last.then_inc(c_y_ready, 1)
                        for f in range(FC):
                            pe.wait_ge(mul_done, count(2 * FC, i, j, g * FC + f + 1))
                            up(f, f, xT, slice(g * GA, (g + 1) * GA)).then_inc(up_ready, 1)
                        if g == 0:
                            with pe.If(has > 0):
                                for c in range(DC):
                                    for t in range(NC):
                                        last = nc.tensor.transpose(xt_ps[c][:, t * P:(t + 1) * P], xin[j][:, 2 * NA + t, c * P:(c + 1) * P], ident[:])
                                    last.then_inc(c_xt_ready, 1)
                            pe.wait_ge(w2_split, count(1, i, j, 1))
                        else:
                            pe.wait_ge(c_done, i * 2 + (j + 1))
                        pe.wait_ge(y_done, count(2 * NA, i, j, (g + 1) * NA))
                        for f in range(FC):
                            if g == 1 and prep and f == 0:
                                pe.wait_ge(xin_loaded[1 - j], i * 16 + 16 * (j + 1))
                                turn(1 - j, 0)
                            if g == 1 and prep and f == FC // 2:
                                pe.wait_ge(xrest_loaded[1 - j], i * 16 + 16 * (j + 1))
                                pe.wait_ge(xt_split, count(2 * DC, i, j, 3 * DC))
                                turn(1 - j, 1)
                            pe.wait_ge(mid_split, count(2 * FC, i, j, g * FC + f + 3))
                            last = down(f, NA)
                        last.then_inc(y_ready, 1)

                experts(pe, body)

            @block.scalar
            def _(act):
                def turn_hi(i, j, g):
                    for c in range(DC):
                        act.wait_ge(xt_ready, count(4, i, j, g * DC + c + 1))
                        nc.scalar.activation(xT[0][:, c, g * GA:(g + 1) * GA], xt_ps[c][:], ACT.Copy).then_inc(xt_hi, 1)

                def split_up(i, j):
                    act.wait_ge(r1_loaded, count(32, i, j, 32))
                    for k in range(2):
                        for c in range(DC):
                            nc.scalar.activation(wup[0][:, k, c, :], raw1[:, k, c, :], ACT.Copy).then_inc(w1_hi, 1)

                split_up(0, 0)
                turn_hi(0, 0, 0)
                turn_hi(0, 0, 1)

                def body(i, j, prep):
                    for g in range(2):
                        if g == 1:
                            has, before_it = extra(act, i, j)
                            with act.If(has > 0):
                                for c in range(DC):
                                    act.wait_ge(c_xt_ready, before_it * DC + (c + 1))
                                    nc.scalar.activation(xTC[0][:, c, :], xt_ps[c][:, 0:GC], ACT.Copy).then_inc(c_xt_hi, 1)
                                for f in range(FC + 1):
                                    if f < FC:
                                        act.wait_ge(c_up_ready, before_it * FC + (f + 1))
                                        if f >= 2:
                                            act.wait_ge(c_mul_done, before_it * FC + (f - 1))
                                        nc.scalar.activation(gate[f % 2][:, 0:GC], up_ps[f % 2][:, 0, 0:GC], ACT.Silu).then_inc(c_silu_done, 1)
                                    if f >= 1:
                                        act.wait_ge(c_mul_done, before_it * FC + f)
                                        nc.scalar.activation(mid2[0][:, f - 1, 0:GC], mid[(f - 1) % 2][:, 0:GC], ACT.Copy).then_inc(c_mid_hi, 1)
                        for f in range(FC + 1):
                            if f < FC:
                                act.wait_ge(up_ready, count(2 * FC, i, j, g * FC + f + 1))
                                act.wait_ge(mul_done, count(2 * FC, i, j, g * FC + f + 1))
                                nc.scalar.activation(gate[f % 2][:], up_ps[f % 2][:, 0, :], ACT.Silu).then_inc(silu_done, 1)
                            if f >= 1:
                                act.wait_ge(mul_done, count(2 * FC, i, j, g * FC + f + 2))
                                nc.scalar.activation(mid2[0][:, f - 1, :], mid[(f - 1) % 2][:], ACT.Copy).then_inc(mid_hi, 1)
                    if prep:
                        turn_hi(i, j + 1, 0)
                        split_up(i, j + 1)
                        turn_hi(i, j + 1, 1)

                experts(act, body)

            @block.vector
            def _(dve):
                dve.sem_inc(mul_done, 2)
                dve.sem_inc(mid_split, 2)
                dve.sem_inc(y_done, NA)
                nc.vector.memset(e_now[:], 0.0).then_inc(dve6, 1)
                LINKS = 4

                def split_up(i, j):
                    for n in range(2 * DC):
                        k, c = n // DC, n % DC
                        dve.wait_ge(w1_hi, count(4, i, j, n + 1))
                        nc.vector.tensor_tensor(wup[1][:, k, c, :], raw1[:, k, c, :], wup[0][:, k, c, :].bitcast(FP32), ALU.subtract).then_inc(w1_split, 1)

                def split_down(i, j):
                    dve.wait_ge(w2_hi, count(1, i, j, 1))
                    nc.vector.tensor_tensor(w2[1][:], raw2[:], w2[0][:].bitcast(FP32), ALU.subtract).then_inc(w2_split, 1)

                def turn_lo(i, j, g):
                    for c in range(DC):
                        dve.wait_ge(xt_hi, count(4, i, j, g * DC + c + 1))
                        cols = slice(g * GA, (g + 1) * GA)
                        nc.vector.tensor_tensor(xT[1][:, c, cols], xt_ps[c][:], xT[0][:, c, cols].bitcast(FP32), ALU.subtract).then_inc(xt_split, 1)

                def lo_of_mid(f, n):
                    return nc.vector.tensor_tensor(mid2[1][:, f, 0:n], mid[f % 2][:, 0:n], mid2[0][:, f, 0:n].bitcast(FP32), ALU.subtract)

                split_up(0, 0)
                turn_lo(0, 0, 0)
                turn_lo(0, 0, 1)
                dve.wait_ge(y_cleared, 2)

                def body(i, j, prep):
                    step = count(LINKS, i, j, 1)
                    dve.wait_ge(xin_loaded[j], i * 16 + 16)
                    dve.wait_ge(xrest_loaded[j], i * 16 + 16)
                    dve.wait_ge(dve6, step)
                    dve.wait_ge(expert_over, i * 2 + (j + 1))
                    for k in range(TOPK):
                        nc.vector.scalar_tensor_tensor(wt[:, k, :], xin[j][:, :, COL_E + k], e_now[:], xin[j][:, :, COL_W + k],
                                                       ALU.is_equal, ALU.mult).then_inc(dve6, 1)
                    nc.vector.tensor_copy(row[j][:], xin[j][:, :, COL_ID])
                    dve.wait_ge(dve6, step + 2)
                    nc.vector.tensor_tensor(wt2[j][:], wt[:, 0, :], wt[:, 1, :], ALU.add).then_inc(dve6, 1)
                    nc.vector.tensor_scalar(e_now[:], e_now[:], 1.0, None, ALU.add).then_inc(dve6, 1)
                    for g in range(2):
                        if g == 1:
                            with dve.If(has > 0):
                                for f in range(FC + 1):
                                    if f < FC:
                                        dve.wait_ge(c_silu_done, before_it * FC + (f + 1))
                                        if f >= 2:
                                            dve.wait_ge(c_mid_split, before_it * FC + (f - 1))
                                        nc.vector.tensor_tensor(mid[f % 2][:, 0:GC], up_ps[f % 2][:, 1, 0:GC], gate[f % 2][:, 0:GC],
                                                                ALU.mult).then_inc(c_mul_done, 1)
                                    if f >= 1:
                                        dve.wait_ge(c_mid_hi, before_it * FC + f)
                                        lo_of_mid(f - 1, GC).then_inc(c_mid_split, 1)
                                dve.wait_ge(c_y_ready, before_it * 1 + 1)
                                for t in range(NC):
                                    nc.vector.tensor_scalar(y[j][:, 2 * NA + t, :], y_ps[:, t, :], wt2[j][:, 2 * NA + t:2 * NA + t + 1], None,
                                                            ALU.mult).then_inc(c_y_done, 1)
                                dve.wait_ge(c_y_done, before_it * NC + NC)
                                dve.sem_inc(leaving, 1)
                            dve.sem_inc(c_done, 1)
                        for f in range(FC + 1):
                            if f < FC:
                                dve.wait_ge(silu_done, count(2 * FC, i, j, g * FC + f + 1))
                                dve.wait_ge(mid_split, count(2 * FC, i, j, g * FC + f + 1))
                                nc.vector.tensor_tensor(mid[f % 2][:], up_ps[f % 2][:, 1, :], gate[f % 2][:], ALU.mult).then_inc(mul_done, 1)
                            if f >= 1:
                                dve.wait_ge(mid_hi, count(2 * FC, i, j, g * FC + f))
                                lo_of_mid(f - 1, GA).then_inc(mid_split, 1)
                            if g == 0 and f == FC // 2:
                                split_down(i, j)
                        if g == 0:
                            has, before_it = extra(dve, i, j)
                            with dve.If(has > 0):
                                for c in range(DC):
                                    dve.wait_ge(c_xt_hi, before_it * DC + (c + 1))
                                    nc.vector.tensor_tensor(xTC[1][:, c, :], xt_ps[c][:, 0:GC], xTC[0][:, c, :].bitcast(FP32),
                                                            ALU.subtract).then_inc(c_xt_split, 1)
                        if g == 1 and prep:
                            turn_lo(i, j + 1, 0)
                            split_up(i, j + 1)
                            turn_lo(i, j + 1, 1)
                        dve.wait_ge(y_ready, count(2, i, j, g + 1))
                        for t in range(NA):
                            last = nc.vector.tensor_scalar(y[j][:, g * NA + t, :], y_ps[:, t, :], wt2[j][:, g * NA + t:g * NA + t + 1], None, ALU.mult)
                            last.then_inc(y_done, 1)

                experts(dve, body)

        LD = 8
        HALF = TT // 2
        BY_DVE = 9
        PIECES = ((0, LD, LD, 0), (LD, HALF, HALF, 0), (HALF, HALF + BY_DVE, 0, BY_DVE), (HALF + BY_DVE, TT, TT - BY_DVE, 0))
        acc_loaded = [sem(f"acc_loaded{c}") for c in range(TT // LD)]
        st2_ready, var2_ready, std2_ready, scale_ready = sem("st2_ready"), sem("var2_ready"), sem("std2_ready"), sem("scale_ready")
        dve7, act_normed, dve_normed, stored = sem("dve7"), sem("act_normed"), sem("dve_normed"), sem("stored")
        with ExitStack() as st, nc.Block() as block:
            a = sb(st, "a", [P, TT, D])
            stats = sb(st, "stats2", [P, TT, 6])
            mean = sb(st, "mean2", [P, TT])
            var = sb(st, "var2", [P, TT])
            std = sb(st, "std2", [P, TT])
            rstd = sb(st, "rstd2", [P, TT])
            nbias = sb(st, "nbias2", [P, TT])
            tmp = sb(st, "tmp2", [P, TT])
            acc_view = acc_dram.rearrange("(t p) d -> p t d", p=P)
            out_view = out.rearrange("(t p) d -> p t d", p=P)

            def part(c):
                return slice(c * HALF, (c + 1) * HALF)

            @block.sync
            def _(sp):
                for c in range(TT // LD):
                    tiles = slice(c * LD, (c + 1) * LD)
                    sp.dma_start(a[:, tiles, :], acc_view[:, tiles, :]).then_inc(acc_loaded[c], 16)
                for lo, hi, by_act, by_dve in PIECES:
                    if by_act:
                        sp.wait_ge(act_normed, by_act)
                    if by_dve:
                        sp.wait_ge(dve_normed, by_dve)
                    sp.dma_start(out_view[:, lo:hi, :], a[:, lo:hi, :]).then_inc(stored, 16)
                sp.wait_ge(stored, 16 * len(PIECES))

            @block.scalar
            def _(act):
                def root(c):
                    act.wait_ge(var2_ready, c + 1)
                    nc.scalar.activation(std[:, part(c)], var[:, part(c)], ACT.Sqrt).then_inc(std2_ready, 1)

                def normalise(c):
                    act.wait_ge(scale_ready, c + 1)
                    for t in range(c * (HALF + BY_DVE), (c + 1) * HALF):
                        nc.scalar.activation(a[:, t, :], a[:, t, :], ACT.Identity, bias=nbias[:, t:t + 1], scale=rstd[:, t:t + 1]).then_inc(act_normed, 1)

                for c in range(2):
                    root(c)
                    normalise(c)

            @block.vector
            def _(dve):
                link = chain(dve, dve7)

                def measure(c):
                    for t in range(c * HALF, (c + 1) * HALF):
                        if t % LD == 0:
                            dve.wait_ge(acc_loaded[t // LD], 16)
                        nc.vector.bn_stats(stats[:, t, :], a[:, t, :]).then_inc(st2_ready, 1)
                    dve.wait_ge(st2_ready, (c + 1) * HALF)
                    layer_stats(nc, link, stats[:, part(c), :], mean[:, part(c)], var[:, part(c)], tmp[:, part(c)]).then_inc(var2_ready, 1)

                def scale(c):
                    dve.wait_ge(std2_ready, c + 1)
                    link(inverse_root(nc, link, var[:, part(c)], std[:, part(c)], rstd[:, part(c)], tmp[:, part(c)]))
                    nc.vector.scalar_tensor_tensor(nbias[:, part(c)], mean[:, part(c)], -1.0, rstd[:, part(c)], ALU.mult, ALU.mult).then_inc(scale_ready, 1)

                measure(0)
                scale(0)
                measure(1)
                scale(1)
                for t in range(HALF, HALF + BY_DVE):
                    nc.vector.tensor_scalar(a[:, t, :], a[:, t, :], mean[:, t:t + 1], rstd[:, t:t + 1], ALU.subtract, ALU.mult).then_inc(dve_normed, 1)


def kernel(L0_attn_content, L0_attn_Wq, L0_attn_Wk, L0_attn_Wv, L0_ffn_router_weight, L0_ffn_ff_pre_act_weight,
           L0_ffn_gate_weight, L0_ffn_ff_post_act_weight):
    import numpy as np
    import concourse.bacc as bacc
    from concourse.bass_utils import run_bass_kernel_spmd

    x = np.asarray(L0_attn_content).reshape(T, D)
    arrays = {
        "x_tok": x,
        "x_T": x.T,
        "wq": np.asarray(L0_attn_Wq),
        "wk": np.asarray(L0_attn_Wk),
        "wv": np.asarray(L0_attn_Wv),
        "wr_T": np.asarray(L0_ffn_router_weight).T,
        "w1_T": np.asarray(L0_ffn_ff_pre_act_weight).transpose(0, 2, 1),
        "wg_T": np.asarray(L0_ffn_gate_weight).transpose(0, 2, 1),
        "w2_T": np.asarray(L0_ffn_ff_post_act_weight).transpose(0, 2, 1),
    }
    arrays = {name: np.ascontiguousarray(a) for name, a in arrays.items()}
    nc = bacc.Bacc("TRN2", target_bir_lowering=False, num_devices=1)
    args = [nc.dram_tensor(name, a.shape, mybir.dt.from_np(a.dtype), kind="ExternalInput").ap() for name, a in arrays.items()]
    out = nc.dram_tensor("out", (T, D), FP32, kind="ExternalOutput").ap()
    program(nc, *args, out)
    result = run_bass_kernel_spmd(nc, [arrays], core_ids=[0])
    return result.results[0]["out"].reshape(B, N, D)
```
